# Optimizing a Trainium2 kernel written in Bass

```python
import numpy as np
import jax
import jax.numpy as jnp

def _softmax(x, axis=-1):
    return jax.nn.softmax(x, axis=axis)

def _gelu(x):
    return jax.nn.gelu(x, approximate=True)

def _silu(x):
    return jax.nn.silu(x)

def _sigmoid(x):
    return jax.nn.sigmoid(x)

def _layernorm(x, axis=-1, eps=1e-05):
    m = jnp.mean(x, axis=axis, keepdims=True)
    v = jnp.var(x, axis=axis, keepdims=True)
    return (x - m) / jnp.sqrt(v + eps)

def _scatter_add(tgt, idx, src, axis=0):
    return tgt.at[idx].add(src)

def _segment_sum(src, seg, n):
    return jax.ops.segment_sum(src, seg, n)
kernel_name = 'mk_perceiver_d1_seqx_r2_39e7b2'

def setup_inputs(seed: int=0):
    np.random.seed(seed)
    _w = jnp.asarray

    def _rec_inputs():
        import jax
        import jax.numpy as jnp
        _rk = jax.random.key(seed)
        x = -0.0005207 + 1.001 * jax.random.normal(jax.random.fold_in(_rk, 1), (1, 256, 512), jnp.float32)
        _lenS = 256 - jax.random.randint(jax.random.fold_in(_rk, 7), (1,), 0, max(1, 256 // 4) + 1, jnp.int32)
        _lenS2 = 25088 - jax.random.randint(jax.random.fold_in(_rk, 8), (1,), 0, max(1, 25088 // 4) + 1, jnp.int32)
        _ctx_1024P = jax.random.normal(jax.random.fold_in(_rk, 11), (1, 16, 512), jnp.float32)
        _ctx_1024c = jax.random.dirichlet(jax.random.fold_in(_rk, 511), 0.3 * jnp.ones((16,), jnp.float32), (1, 25088))
        _ctx_1024t = jnp.einsum('bsk,bkd->bsd', _ctx_1024c, _ctx_1024P)
        _ctx_1024t = _ctx_1024t * jax.lax.rsqrt(jnp.mean(jnp.square(_ctx_1024t)) + 1e-12) * 0.953939
        ctx_1024 = -1.39393e-06 + 0.999914 * (_ctx_1024t + 0.3 * jax.random.normal(jax.random.fold_in(_rk, 611), (1, 25088, 512), jnp.float32))
        fside_Bx16xSxS2_0 = 1.50688e-05 + 0.100006 * jax.random.normal(jax.random.fold_in(_rk, 12), (1, 16, 256, 25088), jnp.float32)
        _validS = jnp.arange(256)[None, :] < _lenS[:, None]
        _validS2 = jnp.arange(25088)[None, :] < _lenS2[:, None]
        _causal = jnp.tril(jnp.ones((256, 256), dtype=bool))
        mask_BxS2_bk0 = jnp.logical_not(jnp.broadcast_to(_validS2[:, :], (1, 25088)))
        return (x, ctx_1024, fside_Bx16xSxS2_0, mask_BxS2_bk0)
    x, ctx_1024, fside_Bx16xSxS2_0, mask_BxS2_bk0 = _rec_inputs()

    def _L0_xattn_setup():
        import jax, jax.numpy as jnp
        import numpy as np
        B, NQ, NK, D, H = (2, 512, 1024, 512, 16)
        HD = D // H
        SCALE = HD ** (-0.5)
        key = jax.random.key(seed)
        ks = jax.random.split(key, 14)
        inp = {'query': jax.random.normal(ks[0], (B, NQ, D), jnp.float32), 'key': jax.random.normal(ks[1], (B, NK, D), jnp.float32), 'value': jax.random.normal(ks[2], (B, NK, D), jnp.float32), 'attn_bias': jax.random.normal(ks[3], (B, H, NQ, NK), jnp.float32) * 0.1, 'key_padding_mask': jax.random.bernoulli(ks[4], 0.1, (B, NK))}
        s = D ** (-0.5)
        inp['Wq'] = jax.random.normal(ks[5], (D, D), jnp.float32) * s
        inp['bq'] = jnp.zeros((D,), jnp.float32)
        inp['Wk'] = jax.random.normal(ks[6], (D, D), jnp.float32) * s
        inp['bk'] = jnp.zeros((D,), jnp.float32)
        inp['Wv'] = jax.random.normal(ks[7], (D, D), jnp.float32) * s
        inp['bv'] = jnp.zeros((D,), jnp.float32)
        inp['Wo'] = jax.random.normal(ks[8], (D, D), jnp.float32) * s
        inp['bo'] = jnp.zeros((D,), jnp.float32)
        return inp
    _L0_xattn_all = _L0_xattn_setup()
    _L0_xattn_in = {k: v for k, v in _L0_xattn_all.items() if k in ('Wq', 'bq', 'Wk', 'bk', 'Wv', 'bv', 'Wo', 'bo')}
    del _L0_xattn_all

    def _L0_attn_setup():
        import jax, jax.numpy as jnp
        import numpy as np
        HEADS = 16
        DIM_HEAD = 64
        EPS = 1e-08
        key = jax.random.key(seed)
        ks = jax.random.split(key, 5)
        B, N, D = (2, 1024, 512)
        inner = HEADS * DIM_HEAD
        return {'x': jax.random.normal(ks[0], (B, N, D), jnp.float32), 'Wq': jax.random.normal(ks[1], (D, inner), jnp.float32) * D ** (-0.5), 'Wkv': jax.random.normal(ks[2], (D, 2 * inner), jnp.float32) * D ** (-0.5), 'Wo': jax.random.normal(ks[3], (inner, D), jnp.float32) * inner ** (-0.5), 'bo': jax.random.normal(ks[4], (D,), jnp.float32) * 0.02}
    _L0_attn_all = _L0_attn_setup()
    _L0_attn_in = {k: v for k, v in _L0_attn_all.items() if k in ('Wq', 'Wkv', 'Wo', 'bo')}
    del _L0_attn_all

    def _L0_ffn_setup():
        import jax, jax.numpy as jnp
        import numpy as np
        H, I, E, NS, C = (512, 512, 6, 2, 2)
        TOPK = 2
        TEMP = 1.0
        EPS = 1e-06
        key = jax.random.key(seed)
        ks = jax.random.split(key, 20)
        sd = 0.02
        inp = {'x': jax.random.normal(ks[0], (4, 1024, H), jnp.float32), 'router_W': jax.random.normal(ks[1], (C, H, E), jnp.float32) * sd, 'router_b': jax.random.normal(ks[2], (C, E), jnp.float32) * sd, 'gate_bias': jax.random.normal(ks[3], (C, E), jnp.float32) * sd, 'exp_Wup': jax.random.normal(ks[4], (E, H, I), jnp.float32) * sd, 'exp_bup': jnp.zeros((E, I), jnp.float32), 'exp_Wg': jax.random.normal(ks[5], (E, I, I), jnp.float32) * sd, 'exp_bg': jnp.zeros((E, I), jnp.float32), 'exp_Wdown': jax.random.normal(ks[6], (E, I, H), jnp.float32) * sd, 'exp_bdown': jnp.zeros((E, H), jnp.float32), 'share_Wup': jax.random.normal(ks[7], (H, NS * I), jnp.float32) * sd, 'share_bup': jnp.zeros((NS * I,), jnp.float32), 'share_Wg': jax.random.normal(ks[8], (I, I), jnp.float32) * sd, 'share_bg': jnp.zeros((I,), jnp.float32), 'share_Wdown': jax.random.normal(ks[9], (I, H), jnp.float32) * sd, 'share_bdown': jnp.zeros((H,), jnp.float32), 'norm_w': jnp.ones((C, H), jnp.float32)}
        return inp
    _L0_ffn_all = _L0_ffn_setup()
    _L0_ffn_in = {k: v for k, v in _L0_ffn_all.items() if k in ('router_W', 'router_b', 'gate_bias', 'exp_Wup', 'exp_bup', 'exp_Wg', 'exp_bg', 'exp_Wdown', 'exp_bdown', 'share_Wup', 'share_bup', 'share_Wg', 'share_bg', 'share_Wdown', 'share_bdown', 'norm_w')}
    del _L0_ffn_all
    return {'x': x, 'ctx_1024': ctx_1024, 'fside_Bx16xSxS2_0': fside_Bx16xSxS2_0, 'mask_BxS2_bk0': mask_BxS2_bk0, 'L0_xattn_Wq': _L0_xattn_in['Wq'], 'L0_xattn_bq': _L0_xattn_in['bq'], 'L0_xattn_Wk': _L0_xattn_in['Wk'], 'L0_xattn_bk': _L0_xattn_in['bk'], 'L0_xattn_Wv': _L0_xattn_in['Wv'], 'L0_xattn_bv': _L0_xattn_in['bv'], 'L0_xattn_Wo': _L0_xattn_in['Wo'], 'L0_xattn_bo': _L0_xattn_in['bo'], 'L0_attn_Wq': _L0_attn_in['Wq'], 'L0_attn_Wkv': _L0_attn_in['Wkv'], 'L0_attn_Wo': _L0_attn_in['Wo'], 'L0_attn_bo': _L0_attn_in['bo'], 'L0_ffn_router_W': _L0_ffn_in['router_W'], 'L0_ffn_router_b': _L0_ffn_in['router_b'], 'L0_ffn_gate_bias': _L0_ffn_in['gate_bias'], 'L0_ffn_exp_Wup': _L0_ffn_in['exp_Wup'], 'L0_ffn_exp_bup': _L0_ffn_in['exp_bup'], 'L0_ffn_exp_Wg': _L0_ffn_in['exp_Wg'], 'L0_ffn_exp_bg': _L0_ffn_in['exp_bg'], 'L0_ffn_exp_Wdown': _L0_ffn_in['exp_Wdown'], 'L0_ffn_exp_bdown': _L0_ffn_in['exp_bdown'], 'L0_ffn_share_Wup': _L0_ffn_in['share_Wup'], 'L0_ffn_share_bup': _L0_ffn_in['share_bup'], 'L0_ffn_share_Wg': _L0_ffn_in['share_Wg'], 'L0_ffn_share_bg': _L0_ffn_in['share_bg'], 'L0_ffn_share_Wdown': _L0_ffn_in['share_Wdown'], 'L0_ffn_share_bdown': _L0_ffn_in['share_bdown'], 'L0_ffn_norm_w': _L0_ffn_in['norm_w']}

def reference(x, ctx_1024, fside_Bx16xSxS2_0, mask_BxS2_bk0, L0_xattn_Wq, L0_xattn_bq, L0_xattn_Wk, L0_xattn_bk, L0_xattn_Wv, L0_xattn_bv, L0_xattn_Wo, L0_xattn_bo, L0_attn_Wq, L0_attn_Wkv, L0_attn_Wo, L0_attn_bo, L0_ffn_router_W, L0_ffn_router_b, L0_ffn_gate_bias, L0_ffn_exp_Wup, L0_ffn_exp_bup, L0_ffn_exp_Wg, L0_ffn_exp_bg, L0_ffn_exp_Wdown, L0_ffn_exp_bdown, L0_ffn_share_Wup, L0_ffn_share_bup, L0_ffn_share_Wg, L0_ffn_share_bg, L0_ffn_share_Wdown, L0_ffn_share_bdown, L0_ffn_norm_w):
    import jax
    import jax.numpy as jnp

    def _L0_xattn_ref(query, key, value, attn_bias, key_padding_mask, Wq, bq, Wk, bk, Wv, bv, Wo, bo):
        import jax, jax.numpy as jnp
        import numpy as np
        B, NQ, NK, D, H = (2, 512, 1024, 512, 16)
        HD = D // H
        SCALE = HD ** (-0.5)
        b, nq, d = query.shape
        nk = key.shape[1]
        q = (query @ Wq + bq).reshape(b, nq, H, HD).transpose(0, 2, 1, 3)
        k = (key @ Wk + bk).reshape(b, nk, H, HD).transpose(0, 2, 1, 3)
        v = (value @ Wv + bv).reshape(b, nk, H, HD).transpose(0, 2, 1, 3)
        logits = jnp.einsum('bhqd,bhkd->bhqk', q, k) * SCALE + attn_bias
        all_masked = jnp.all(key_padding_mask, axis=1)
        safe_mask = key_padding_mask.at[:, 0].set(jnp.where(all_masked, False, key_padding_mask[:, 0]))
        logits = jnp.where(safe_mask[:, None, None, :], -jnp.inf, logits)
        attn = jax.nn.softmax(logits, axis=-1)
        out = jnp.einsum('bhqk,bhkd->bhqd', attn, v)
        out = out.transpose(0, 2, 1, 3).reshape(b, nq, d)
        return out @ Wo + bo

    def _L0_attn_ref(x, Wq, Wkv, Wo, bo):
        import jax, jax.numpy as jnp
        import numpy as np
        HEADS = 16
        DIM_HEAD = 64
        EPS = 1e-08
        B, N, D = x.shape
        H, Dh = (HEADS, DIM_HEAD)
        scale = Dh ** (-0.5)
        q = (x @ Wq).reshape(B, N, H, Dh).transpose(0, 2, 1, 3)
        kv = x @ Wkv
        k = kv[..., :H * Dh].reshape(B, N, H, Dh).transpose(0, 2, 1, 3)
        v = kv[..., H * Dh:].reshape(B, N, H, Dh).transpose(0, 2, 1, 3)
        s = jnp.einsum('bhid,bhjd->bhij', q * scale, k)
        gm = jax.lax.stop_gradient(jnp.max(s, axis=-1, keepdims=True))
        causal_mask = jnp.triu(jnp.ones((N, N), bool), 1)
        p = jnp.where(causal_mask, 0.0, jnp.exp(s - gm))
        num = jnp.einsum('bhij,bhjd->bhid', p, v)
        out = num / (jnp.sum(p, axis=-1, keepdims=True) + EPS)
        out = out.transpose(0, 2, 1, 3).reshape(B, N, H * Dh)
        return out @ Wo + bo

    def _L0_ffn_ref(x, router_W, router_b, gate_bias, exp_Wup, exp_bup, exp_Wg, exp_bg, exp_Wdown, exp_bdown, share_Wup, share_bup, share_Wg, share_bg, share_Wdown, share_bdown, norm_w):
        import jax, jax.numpy as jnp
        import numpy as np
        H, I, E, NS, C = (512, 512, 6, 2, 2)
        TOPK = 2
        TEMP = 1.0
        EPS = 1e-06
        B, S, Hd = x.shape
        xf = x.reshape(-1, Hd)
        for j in range(C):
            residual = xf
            gate = (xf @ router_W[j] + router_b[j]) / TEMP
            biased = gate + gate_bias[j]
            _, ids = jax.lax.top_k(biased, TOPK)
            sel = (ids[:, :, None] == jnp.arange(E)[None, None, :]).any(axis=1)
            weights = jax.nn.softmax(jnp.where(sel, gate, -jnp.inf), axis=-1)
            h = jnp.einsum('nh,ehi->eni', xf, exp_Wup) + exp_bup[:, None, :]
            h = jax.nn.silu(jnp.einsum('eni,eij->enj', h, exp_Wg) + exp_bg[:, None, :]) * h
            eo = jnp.einsum('eni,eih->enh', h, exp_Wdown) + exp_bdown[:, None, :]
            combined = jnp.einsum('ne,enh->nh', weights, eo)
            s = (xf @ share_Wup + share_bup).reshape(-1, NS, I)
            s = jax.nn.silu(s @ share_Wg + share_bg) * s
            share_out = (s @ share_Wdown + share_bdown).sum(axis=1)
            z = combined + share_out
            y = residual + z
            y = y * jax.lax.rsqrt(jnp.mean(y * y, axis=-1, keepdims=True) + EPS) * norm_w[j]
            xf = y
        return xf.reshape(B, S, Hd)
    x = x + _L0_xattn_ref(_layernorm(x, axis=-1), ctx_1024, ctx_1024, fside_Bx16xSxS2_0, mask_BxS2_bk0, L0_xattn_Wq, L0_xattn_bq, L0_xattn_Wk, L0_xattn_bk, L0_xattn_Wv, L0_xattn_bv, L0_xattn_Wo, L0_xattn_bo)
    x = x + _L0_attn_ref(_layernorm(x, axis=-1), L0_attn_Wq, L0_attn_Wkv, L0_attn_Wo, L0_attn_bo)
    x = x + _L0_ffn_ref(_layernorm(x, axis=-1), L0_ffn_router_W, L0_ffn_router_b, L0_ffn_gate_bias, L0_ffn_exp_Wup, L0_ffn_exp_bup, L0_ffn_exp_Wg, L0_ffn_exp_bg, L0_ffn_exp_Wdown, L0_ffn_exp_bdown, L0_ffn_share_Wup, L0_ffn_share_bup, L0_ffn_share_Wg, L0_ffn_share_bg, L0_ffn_share_Wdown, L0_ffn_share_bdown, L0_ffn_norm_w)
    return x

_drawn_inputs = setup_inputs


def setup_inputs(seed=0):
    import zlib

    import numpy as np

    out = dict(_drawn_inputs(seed))
    spreads = {'L0_xattn_bq': (0.0, 0.372),
     'L0_xattn_bk': (0.0, 0.8),
     'L0_xattn_bv': (0.0, 0.1),
     'L0_xattn_bo': (0.0, 0.1),
     'L0_ffn_exp_bup': (0.0, 0.8),
     'L0_ffn_exp_bg': (0.0, 0.8),
     'L0_ffn_exp_bdown': (0.0, 0.1),
     'L0_ffn_share_bup': (0.0, 0.8),
     'L0_ffn_share_bg': (0.0, 0.598),
     'L0_ffn_share_bdown': (0.0, 0.1),
     'L0_ffn_norm_w': (1.0, 0.2)}
    factors = {'fside_Bx16xSxS2_0': 8.0,
     'L0_attn_bo': 3.561,
     'L0_ffn_router_b': 8.0,
     'L0_ffn_gate_bias': 6.244,
     'L0_ffn_exp_Wup': 4.317,
     'L0_ffn_exp_Wg': 4.779,
     'L0_ffn_exp_Wdown': 4.276}
    for name, (base, spread) in spreads.items():
        noise = np.random.default_rng([zlib.crc32(name.encode()), seed]).standard_normal(out[name].shape)
        drawn = base * np.exp(spread * noise) if base else spread * noise
        out[name] = jnp.asarray(drawn.astype(out[name].dtype))
    for name, factor in factors.items():
        out[name] = (out[name] * factor).astype(out[name].dtype)
    return out
```

```python
from contextlib import ExitStack

import concourse.bass as bass
from concourse import mybir

F32 = mybir.dt.float32
F32R = mybir.dt.float32r
U8 = mybir.dt.uint8
ALU = mybir.AluOpType
ACT = mybir.ActivationFunctionType
AX_X = mybir.AxisListType.X

P = 128
D = 512
DB = D // P
NQ = 256
QT = NQ // P
H = 16
HD = D // H
KC = 512
KB = KC // P
HG = P // HD
NG = H // HG
SCALE = HD ** -0.5
MASKED = -(2.0 ** 100)
NO_MAX = -3.0e38
LN_EPS = 1e-5

RING = 8
AHEAD = RING - 1
TILES = 12
V1, CT, K01, V0, K23 = 0, 2, 6, 8, 10
K_TILE = {0: K01, 1: K01 + 1, 2: K23, 3: K23 + 1}


def load_and_project_queries(nc, A, S):
    nkt = A["mask"].shape[-1] // P
    with ExitStack() as ctx:
        def sb(name, shape, dt=F32):
            return ctx.enter_context(nc.sbuf_tensor(name, shape, dt))

        def sem(name):
            return ctx.enter_context(nc.semaphore(name))

        wq = sb("wq", [P, DB, D])
        wk = sb("wk", [P, DB, D])
        wv = sb("wv", [P, DB, D])
        stats = sb("ln_stats", [P, QT, 6])
        mv = sb("ln_mv", [P, QT, 2])
        veps = sb("ln_veps", [P, QT])
        std = sb("ln_std", [P, QT])
        rstd = sb("ln_rstd", [P, QT])
        xn = sb("xn", [P, QT, D])
        xnT = sb("xnT", [P, DB, NQ])
        bq = sb("bq", [P, NG])
        q_f = sb("q_f", [P, NG, NQ])
        q_hi = sb("q_hi", [P, NG, NQ], F32R)
        q_lo = sb("q_lo", [P, NG, NQ], F32R)
        mask_u8 = sb("mask_u8", [P, nkt], U8)
        mask_f = sb("mask_f", [P, nkt])
        mask_r = sb("mask_r", [P, nkt], F32R)
        mask_min = sb("mask_min", [P, 1])
        all_masked = sb("all_masked", [P, 1])
        ones = sb("ones", [P, P])
        tp = [ctx.enter_context(nc.psum_tensor(f"xnT_ps{i}", [P, 512], F32)) for i in range(2)]
        qp = [ctx.enter_context(nc.psum_tensor(f"q_ps{i}", [P, NQ], F32)) for i in range(2)]
        cp = ctx.enter_context(nc.psum_tensor("count_ps", [P, 512], F32))

        x_ld, wq_ld, wk_ld, wv_ld = sem("x_ld"), sem("wq_ld"), sem("wk_ld"), sem("wv_ld")
        mask_ld, const_ld = sem("mask_ld"), sem("const_ld")
        zeroed, consts = sem("zeroed"), sem("consts")
        chain = sem("prep_chain")
        var_ready, std_ready = sem("var_ready"), sem("std_ready")
        xn_ready, xnT_full, xnT_ready = sem("xn_ready"), sem("xnT_full"), sem("xnT_ready")
        q_full, q_free, q_split = sem("q_full"), sem("q_free"), sem("q_split")
        w_hi = sem("w_hi")
        min_ready, count_ready, mask_ready = sem("min_ready"), sem("count_ready"), sem("mask_ready")
        stored = sem("prep_stored")
        ones_row = sem("ones_row")
        block = ctx.enter_context(nc.Block())

        @block.sync
        def _(sp):
            sp.dma_start(S["x"][:], A["x"].rearrange("(t p) d -> p t d", p=P)).then_inc(x_ld, 16)
            sp.dma_start(wq[:], A["xWq"].rearrange("(j p) n -> p j n", p=P)).then_inc(wq_ld, 16)
            sp.dma_start(bq[:], A["xbq"].rearrange("(g p) -> p g", p=P),
                         allow_slow_non_contiguous=True).then_inc(const_ld, 16)
            sp.dma_start(S["bk"][:], A["xbk"].rearrange("(g p) -> p g", p=P),
                         allow_slow_non_contiguous=True).then_inc(const_ld, 16)
            sp.dma_start(mask_u8[:], A["mask"].rearrange("(p t) -> p t", p=P)).then_inc(mask_ld, 16)
            sp.dma_start(wk[:], A["xWk"].rearrange("(j p) n -> p j n", p=P)).then_inc(wk_ld, 16)
            sp.dma_start(wv[:], A["xWv"].rearrange("(j p) n -> p j n", p=P)).then_inc(wv_ld, 16)
            sp.wait_ge(mask_ready, 1)
            sp.dma_start(S["mask_row"].rearrange("(p t) -> p t", p=P), mask_r[:].bitcast(F32)).then_inc(stored, 16)
            for g in range(NG):
                sp.wait_ge(q_split, g + 1)
                for i in range(HG):
                    rows = slice(HD * i, HD * (i + 1))
                    for r, part in enumerate((q_hi, q_hi, q_lo)):
                        sp.dma_start(S["q_stack"][HD * r:HD * (r + 1), HG * g + i, :].bitcast(F32),
                                     part[rows, g, :].bitcast(F32)).then_inc(stored, 16)
            sp.wait_ge(stored, 16 + 16 * NG * HG * 3)

        @block.gpsimd
        def _(pool):
            pool.memset(S["ident"][:], 0.0).then_inc(zeroed, 1)
            pool.wait_ge(zeroed, 1)
            pool.affine_select(out=S["ident"][:], in_=S["ident"][:], compare_op=ALU.not_equal, fill=1.0,
                               base=0, pattern=[[-1, P]], channel_multiplier=1).then_inc(consts, 1)
            pool.memset(ones[:], 1.0).then_inc(consts, 1)

        @block.scalar
        def _(act):
            act.wait_ge(var_ready, 1)
            nc.scalar.activation(std[:], veps[:], ACT.Sqrt).then_inc(std_ready, 1)
            act.wait_ge(wk_ld, 16)
            nc.scalar.activation(S["wk_hi"][:], wk[:], ACT.Copy).then_inc(w_hi, 1)
            act.wait_ge(wv_ld, 16)
            nc.scalar.activation(S["wv_hi"][:], wv[:], ACT.Copy).then_inc(w_hi, 1)

        @block.vector
        def _(dve):
            n = [0]

            def link(ins):
                n[0] += 1
                ins.then_inc(chain, 1)
                dve.wait_ge(chain, n[0])

            dve.wait_ge(x_ld, 16)
            for t in range(QT):
                link(dve.bn_stats(stats[:, t, :], S["x"][:, t, :]))
                link(dve.bn_aggr(mv[:, t, :], stats[:, t, :]))
            dve.tensor_scalar(veps[:], mv[:, :, 1], LN_EPS, None, ALU.add).then_inc(var_ready, 1)
            dve.wait_ge(std_ready, 1)
            link(dve.reciprocal(rstd[:], std[:]))
            for t in range(QT):
                dve.tensor_scalar(xn[:, t, :], S["x"][:, t, :], mv[:, t, 0:1], rstd[:, t:t + 1],
                                  ALU.subtract, ALU.mult).then_inc(xn_ready, 1)
            dve.wait_ge(mask_ld, 16)
            link(dve.tensor_copy(mask_f[:], mask_u8[:]))
            dve.tensor_reduce(mask_min[:], mask_f[:], AX_X, ALU.min).then_inc(min_ready, 1)
            for h in range(2):
                dve.wait_ge(xnT_full, h + 1)
                dve.tensor_copy(xnT[:, 2 * h:2 * h + 2, :], tp[h][:].rearrange("p (j q) -> p j q", j=2)
                                ).then_inc(xnT_ready, 1)
            dve.wait_ge(consts, 1)
            link(dve.tensor_tensor(S["fold"][:], S["ident"][0:2 * HD, 0:HD],
                                   S["ident"][0:2 * HD, HD:2 * HD], ALU.add))
            link(dve.memset(S["q_stack"][3 * HD:3 * HD + 1, :, :].bitcast(F32), 1.0))
            link(dve.memset(S["m_old"][:], NO_MAX))
            link(dve.memset(S["l"][:], 0.0))
            link(dve.memset(S["o"][:], 0.0))
            dve.wait_ge(count_ready, 1)
            link(dve.tensor_scalar(all_masked[:], cp[:, 0:1], P - 0.5, None, ALU.is_ge))
            link(dve.tensor_tensor(mask_f[0:1, 0:1], mask_f[0:1, 0:1], all_masked[0:1, :], ALU.subtract))
            dve.tensor_scalar(mask_r[:], mask_f[:], MASKED, None, ALU.mult).then_inc(mask_ready, 1)
            dve.wait_ge(const_ld, 32)
            for g in range(NG):
                dve.wait_ge(q_full, g + 1)
                ins = dve.tensor_scalar(q_f[:, g, :], qp[g % 2][:], bq[:, g:g + 1], SCALE, ALU.add, ALU.mult)
                ins.then_inc(q_free, 1)
                dve.wait_ge(q_free, g + 1)
                link(dve.tensor_copy(q_hi[:, g, :], q_f[:, g, :]))
                dve.tensor_tensor(q_lo[:, g, :], q_f[:, g, :], q_hi[:, g, :].bitcast(F32),
                                  ALU.subtract).then_inc(q_split, 1)
            for i, (w, hi, lo) in enumerate(((wk, "wk_hi", "wk_lo"), (wv, "wv_hi", "wv_lo"))):
                dve.wait_ge(w_hi, i + 1)
                link(dve.tensor_tensor(S[lo][:], w[:], S[hi][:].bitcast(F32), ALU.subtract))

        @block.tensor
        def _(pe):
            pe.wait_ge(consts, 2)
            pe.wait_ge(xn_ready, QT)
            for h in range(2):
                for j in (2 * h, 2 * h + 1):
                    for t in range(QT):
                        at = (j % 2) * NQ + t * P
                        last = pe.transpose(tp[h][:, at:at + P], xn[:, t, j * P:(j + 1) * P], S["ident"][:])
                last.then_inc(xnT_full, 1)
            pe.wait_ge(min_ready, 1)
            pe.matmul(cp[:, 0:1], ones[:], mask_min[:], start=True, stop=True).then_inc(count_ready, 1)
            pe.wait_ge(xnT_ready, 2)
            pe.wait_ge(wq_ld, 16)
            for g in range(NG):
                if g >= 2:
                    pe.wait_ge(q_free, g - 1)
                for j in range(DB):
                    last = pe.matmul(qp[g % 2][:], wq[:, j, g * P:(g + 1) * P], xnT[:, j, :],
                                     start=(j == 0), stop=(j == DB - 1))
                last.then_inc(q_full, 1)


def cross_attention(nc, A, S):
    n_keys = A["ctx"].shape[0]
    NC = n_keys // KC
    assert n_keys % KC == 0 and NC >= 4
    with ExitStack() as ctx:
        def sb(name, shape, dt=F32):
            return ctx.enter_context(nc.sbuf_tensor(name, shape, dt))

        def bank(name):
            return ctx.enter_context(nc.psum_tensor(name, [P, 512], F32))

        def sem(name):
            return ctx.enter_context(nc.semaphore(name))

        k_stack = sb("k_stack", [P, H, KC], F32R)
        v = sb("v", [P, KB, H, 2, HD], F32R)
        ctx_sb = sb("ctx_sb", [P, KB, D])
        ctxT_hi = sb("ctxT_hi", [P, DB, KC], F32R)
        ctxT_lo = sb("ctxT_lo", [P, DB, KC], F32R)
        k_hi = sb("k_hi", [P, 2, KC], F32R)
        k_lo = sb("k_lo", [P, 2, KC], F32R)
        logits = sb("logits", [P, RING, QT, KC])
        pT_hi = sb("pT_hi", [P, 2, 2, 2 * NQ], F32R)
        pT_lo = sb("pT_lo", [P, 2, 2, 2 * NQ], F32R)
        oT = sb("oT", [2 * HD, 2, NQ])
        m_new = sb("m_new", [P, H, QT])
        m_neg = sb("m_neg", [P, H, QT])
        m_diff = sb("m_diff", [P, H, QT])
        alpha = sb("alpha", [P, H, QT])
        row_sum = sb("row_sum", [P, H, QT])
        one = sb("one", [P, QT])
        m_old, l, o = S["m_old"], S["l"], S["o"]

        s_ps = [bank(f"s_ps{t}") for t in range(QT)]
        pT_ps = [bank(f"pT_ps{b}") for b in range(2)]
        proj_ps = [bank(f"proj_ps{b}") for b in range(2)]
        oT_ps = bank("oT_ps")
        o_ps = bank("o_ps")

        bias_ld = [sem(f"bias_ld{r}") for r in range(RING)]
        ctx_ld = sem("ctx_ld")
        k_ld = [sem(f"k_ld{g}") for g in range(NG)]
        s_full = sem("s_full")
        t_done = sem("t_done")
        m_ready = sem("m_ready")
        one_set = sem("one_set")
        m_saved = sem("m_saved")
        p_done = sem("p_done")
        a_done = sem("a_done")
        l_scaled = sem("l_scaled")
        o_scaled = sem("o_scaled")
        l_done = sem("l_done")
        tr_done = sem("tr_done")
        hi_done = sem("hi_done")
        lo_done = sem("lo_done")
        pv_done = sem("pv_done")
        oT_done = sem("oT_done")
        ox_done = sem("ox_done")
        o_done = sem("o_done")
        proj_full = sem("proj_full")
        proj_hi = sem("proj_hi")
        proj_lo = sem("proj_lo")

        block = ctx.enter_context(nc.Block())

        def tiles(c, i):
            return TILES * (c + 1) + i - 1

        def wait(eng, s, value):
            if not isinstance(value, int) or value > 0:
                eng.wait_ge(s, value)

        def over_chunks(eng, steps):
            steps(0, False)
            with eng.Fori(1, NC - 1) as c:
                steps(c, False)
            steps(NC - 1, True)

        @block.sync
        def _(sp):
            def load_bias(c, h):
                n = H * c + h
                wait(sp, tr_done, 2 * (n - RING + 1))
                src = A["bias"][h, :, bass.ds(c * KC, KC)].rearrange("(t p) k -> p t k", p=P)
                sp.dma_start(logits[:, h % RING, :, :], src).then_inc(bias_ld[h % RING], 16)

            def load_ctx(c):
                sp.dma_start(ctx_sb[:], A["ctx"][bass.ds(c * KC, KC), :].rearrange("(b p) d -> p b d", p=P)
                             ).then_inc(ctx_ld, 16)

            def stack_keys(c, g):
                sp.wait_ge(proj_lo, tiles(c, K_TILE[g]))
                wait(sp, s_full, QT * (H * c + HG * (g + 1)))
                heads = slice(HG * g, HG * (g + 1))
                for i in range(HG):
                    rows = slice(HD * i, HD * (i + 1))
                    for r, part in enumerate((k_hi, k_lo, k_hi)):
                        sp.dma_start(k_stack[HD * r:HD * (r + 1), HG * g + i, :].bitcast(F32),
                                     part[rows, g % 2, :].bitcast(F32)).then_inc(k_ld[g], 16)
                row = S["mask_row"][bass.ds((c + 1) * KC, KC)].rearrange("(a b k) -> a b k", a=1, b=1)
                sp.dma_start(k_stack[3 * HD:3 * HD + 1, heads, :].bitcast(F32),
                             row.to_broadcast([1, HG, KC])).then_inc(k_ld[g], 16)

            load_ctx(0)
            for n in range(AHEAD):
                load_bias(0, n)
            sp.wait_ge(proj_full, tiles(-1, CT + DB - 1))
            load_ctx(1)
            for g in range(NG):
                stack_keys(-1, g)

            def steps(c, last):
                for h in range(H):
                    if h + AHEAD < H:
                        load_bias(c, h + AHEAD)
                    elif not last:
                        load_bias(c + 1, h + AHEAD - H)
                    if last:
                        continue
                    if h == 6 and not (isinstance(c, int) and c == NC - 2):
                        sp.wait_ge(proj_full, tiles(c, CT + DB - 1))
                        load_ctx(c + 2)
                    if h == 8:
                        stack_keys(c, 0)
                    if h == 10:
                        stack_keys(c, 1)
                    if h == 15:
                        stack_keys(c, 2)
                        stack_keys(c, 3)

            steps(0, False)
            with sp.Fori(1, NC - 2) as c:
                steps(c, False)
            steps(NC - 2, False)
            steps(NC - 1, True)

        @block.tensor
        def _(pe):
            def transpose(c, h, b):
                n = H * c + h
                if b == 0:
                    pe.wait_ge(p_done, QT * (n + 1))
                wait(pe, lo_done, 2 * (n - 1) + b + 1)
                for k in range(2):
                    for t in range(QT):
                        at = k * NQ + t * P
                        last = pe.transpose(pT_ps[b][:, at:at + P],
                                            logits[:, h % RING, t, bass.ts(2 * b + k, P)], S["ident"][:])
                last.then_inc(tr_done, 1)

            def scores(c, h):
                n = H * c + h
                if h % HG == 0:
                    pe.wait_ge(k_ld[h // HG], 16 * (3 * HG + 1) * (c + 1))
                for t in range(QT):
                    wait(pe, t_done, QT * (n - 1) + t + 1)
                    pe.matmul(s_ps[t][:], S["q_stack"][0:3 * HD + 1, h, bass.ts(t, P)],
                              k_stack[0:3 * HD + 1, h, :], start=True, stop=True).then_inc(s_full, 1)

            def weighted_values(c, h):
                n = H * c + h
                pe.wait_ge(lo_done, 2 * (n + 1))
                wait(pe, oT_done, n)
                if h == 0:
                    pe.wait_ge(proj_lo, tiles(c - 1, V0 + 1))
                if h == H // 2:
                    pe.wait_ge(proj_lo, tiles(c, V1 + 1))
                for kb in range(KB):
                    for i, part in enumerate((pT_hi, pT_lo)):
                        last = pe.matmul(oT_ps[0:2 * HD, 0:NQ],
                                         v[:, kb, h, :, :].rearrange("p a d -> p (a d)"),
                                         part[:, h % 2, kb // 2, (kb % 2) * NQ:(kb % 2 + 1) * NQ],
                                         start=(kb == 0 and i == 0), stop=(kb == KB - 1 and i == 1))
                last.then_inc(pv_done, 1)

            def turn_output(c, h):
                n = H * c + h
                pe.wait_ge(oT_done, n + 1)
                wait(pe, o_done, n)
                for t in range(QT):
                    last = pe.matmul(o_ps[:, t * HD:(t + 1) * HD], oT[:, h % 2, t * P:(t + 1) * P],
                                     S["fold"][:], start=True, stop=True)
                last.then_inc(ox_done, 1)

            def free_bank(c, i):
                wait(pe, proj_lo, tiles(c, i) - 2)

            def context_tile(c, j):
                i = CT + j
                free_bank(c, i)
                if j == 0:
                    pe.wait_ge(ctx_ld, 16 * (c + 2))
                for b in range(KB):
                    last = pe.transpose(proj_ps[i % 2][:, bass.ts(b, P)], ctx_sb[:, b, bass.ts(j, P)],
                                        S["ident"][:])
                last.then_inc(proj_full, 1)

            def key_tile(c, g, part):
                i = K_TILE[g]
                if part == 0:
                    free_bank(c, i)
                    if g == 0:
                        pe.wait_ge(proj_lo, tiles(c, CT + DB - 1))
                for j in (0, 1) if part == 0 else (2, 3):
                    for s, (w, x) in enumerate((("wk_hi", ctxT_hi), ("wk_hi", ctxT_lo), ("wk_lo", ctxT_hi))):
                        last = pe.matmul(proj_ps[i % 2][:], S[w][:, j, bass.ts(g, P)], x[:, j, :],
                                         start=(j == 0 and s == 0), stop=(j == DB - 1 and s == 2))
                if part == 1:
                    last.then_inc(proj_full, 1)

            def value_tile(c, i, half, part):
                if part == 0:
                    free_bank(c, i)
                b = 2 * (i % 2) + part
                cols = slice(half * D // 2, (half + 1) * D // 2)
                for j in range(DB):
                    for s, (x, w) in enumerate(((ctxT_hi, "wv_hi"), (ctxT_hi, "wv_lo"), (ctxT_lo, "wv_hi"))):
                        last = pe.matmul(proj_ps[i % 2][:, part * 256:(part + 1) * 256], x[:, j, bass.ts(b, P)],
                                         S[w][:, j, cols], start=(j == 0 and s == 0),
                                         stop=(j == DB - 1 and s == 2))
                if part == 1:
                    last.then_inc(proj_full, 1)

            for j in range(DB):
                context_tile(-1, j)
            for g in (0, 1):
                key_tile(-1, g, 0), key_tile(-1, g, 1)
            for i in (0, 1):
                value_tile(-1, V0 + i, 0, 0), value_tile(-1, V0 + i, 0, 1)
            for g in (2, 3):
                key_tile(-1, g, 0), key_tile(-1, g, 1)
            scores(0, 0)
            scores(0, 1)

            def project(c, h):
                if h < 4:
                    value_tile(c, V1 + h // 2, 1, h % 2)
                elif h < 6:
                    context_tile(c, 2 * (h - 4))
                    context_tile(c, 2 * (h - 4) + 1)
                elif h < 10:
                    key_tile(c, (h - 6) // 2, h % 2)
                elif h < 14:
                    value_tile(c, V0 + (h - 10) // 2, 0, h % 2)
                else:
                    key_tile(c, h - 12, 0)
                    key_tile(c, h - 12, 1)

            def steps(c, last):
                for h in range(H):
                    transpose(c, h, 0)
                    if h + 2 < H:
                        scores(c, h + 2)
                    elif not last:
                        scores(c + 1, h + 2 - H)
                    transpose(c, h, 1)
                    if not last or h < 4:
                        project(c, h)
                    if h >= 1:
                        weighted_values(c, h - 1)
                    elif not (isinstance(c, int) and c == 0):
                        weighted_values(c - 1, H - 1)
                    if h >= 2:
                        turn_output(c, h - 2)
                    elif not (isinstance(c, int) and c == 0):
                        turn_output(c - 1, H + h - 2)

            over_chunks(pe, steps)
            weighted_values(NC - 1, H - 1)
            turn_output(NC - 1, H - 2)
            turn_output(NC - 1, H - 1)

        def finished_tiles(h):
            return {1: [0], 3: [1], 4: [2, 3], 5: [4, 5], 7: [6], 9: [7], 11: [8], 13: [9],
                    14: [10], 15: [11]}.get(h, [])

        def value_out(i, half, part):
            b = 2 * (i % 2)
            return v[:, b:b + 2, half * H // 2:(half + 1) * H // 2, part, :]

        @block.scalar
        def _(act):
            def split_hi(c, h, b):
                n = H * c + h
                act.wait_ge(tr_done, 2 * n + b + 1)
                wait(act, pv_done, n - 1)
                nc.scalar.activation(pT_hi[:, h % 2, b, :], pT_ps[b][:], ACT.Copy).then_inc(hi_done, 1)

            def exponentials(c, h, t):
                n = H * c + h
                if t == 0:
                    act.wait_ge(m_ready, 2 * (n + 1))
                    wait(act, l_done, n - H + 1)
                at = logits[:, h % RING, t, :]
                nc.scalar.activation(at, at, ACT.Exp, bias=m_neg[:, h, t:t + 1],
                                     accum_out=row_sum[:, h, t:t + 1]).then_inc(p_done, 1)

            def rescaling(c, h):
                nc.scalar.activation(alpha[:, h, :], m_diff[:, h, :], ACT.Exp).then_inc(a_done, 1)

            def copy_output(c, h):
                n = H * c + h
                act.wait_ge(pv_done, n + 1)
                wait(act, ox_done, n - 1)
                nc.scalar.activation(oT[:, h % 2, :], oT_ps[0:2 * HD, 0:NQ], ACT.Copy).then_inc(oT_done, 1)

            def tile_hi(c, i):
                act.wait_ge(proj_full, tiles(c, i))
                src = proj_ps[i % 2]
                if CT <= i < CT + DB:
                    ins = nc.scalar.activation(ctxT_hi[:, i - CT, :], src[:], ACT.Copy)
                elif i in (V1, V1 + 1, V0, V0 + 1):
                    half = 1 if i < CT else 0
                    wait(act, pv_done, H * c if half else H * c + H // 2)
                    ins = nc.scalar.activation(value_out(i, half, 0),
                                               src[:].rearrange("p (b h d) -> p b h d", b=2, d=HD), ACT.Copy)
                else:
                    g = {j: g for g, j in K_TILE.items()}[i]
                    if g >= 2:
                        act.wait_ge(k_ld[g - 2], 16 * (3 * HG + 1) * (c + 2))
                    else:
                        wait(act, k_ld[g + 2], 16 * (3 * HG + 1) * (c + 1))
                    ins = nc.scalar.activation(k_hi[:, g % 2, :], src[:], ACT.Identity, bias=S["bk"][:, g:g + 1])
                ins.then_inc(proj_hi, 1)

            for i in range(CT, TILES):
                tile_hi(-1, i)
            for t in range(QT):
                exponentials(0, 0, t)
            rescaling(0, 0)

            def steps(c, last):
                for h in range(H):
                    ahead = (c, h + 1) if h + 1 < H else (c + 1, 0)
                    more = h + 1 < H or not last
                    split_hi(c, h, 0)
                    if more:
                        exponentials(*ahead, 0)
                    split_hi(c, h, 1)
                    if more:
                        exponentials(*ahead, 1)
                        rescaling(*ahead)
                    for i in finished_tiles(h):
                        if not last or i < CT:
                            tile_hi(c, i)
                    if h >= 1:
                        copy_output(c, h - 1)
                    elif not (isinstance(c, int) and c == 0):
                        copy_output(c - 1, H - 1)

            over_chunks(act, steps)
            copy_output(NC - 1, H - 1)

        @block.vector
        def _(dve):
            def split_lo(c, h, b):
                dve.wait_ge(hi_done, 2 * (H * c + h) + b + 1)
                dve.tensor_tensor(pT_lo[:, h % 2, b, :], pT_ps[b][:],
                                  pT_hi[:, h % 2, b, :].bitcast(F32), ALU.subtract).then_inc(lo_done, 1)

            def await_logits(c, h, t):
                n = H * c + h
                if t == 0:
                    use = (H // RING) * c + h // RING + 1
                    dve.wait_ge(bias_ld[h % RING], 16 * use)
                    wait(dve, m_saved, n - H + 1)
                dve.wait_ge(s_full, QT * n + t + 1)

            def logits_and_max(c, h, t):
                at = logits[:, h % RING, t, :]
                dve.tensor_tensor_reduce(at, s_ps[t][:], at, 1.0, m_old[:, h, t:t + 1], ALU.add, ALU.max,
                                         m_new[:, h, t:t + 1]).then_inc(t_done, 1)

            def add_output(c, h):
                n = H * c + h
                dve.wait_ge(ox_done, n + 1)
                dve.wait_ge(o_scaled, n + 1)
                dve.tensor_tensor(o[:, :, h, :], o[:, :, h, :],
                                  o_ps[:, 0:QT * HD].rearrange("p (t d) -> p t d", t=QT),
                                  ALU.add).then_inc(o_done, 1)

            def tile_lo(c, i):
                dve.wait_ge(proj_hi, tiles(c, i))
                src = proj_ps[i % 2]
                if CT <= i < CT + DB:
                    ins = dve.tensor_tensor(ctxT_lo[:, i - CT, :], src[:],
                                            ctxT_hi[:, i - CT, :].bitcast(F32), ALU.subtract)
                elif i in (V1, V1 + 1, V0, V0 + 1):
                    half = 1 if i < CT else 0
                    ins = dve.tensor_tensor(value_out(i, half, 1),
                                            src[:].rearrange("p (b h d) -> p b h d", b=2, d=HD),
                                            value_out(i, half, 0).bitcast(F32), ALU.subtract)
                else:
                    g = {j: g for g, j in K_TILE.items()}[i]
                    ins = dve.scalar_tensor_tensor(out=k_lo[:, g % 2, :], in0=src[:], scalar=S["bk"][:, g:g + 1],
                                                   in1=k_hi[:, g % 2, :].bitcast(F32), op0=ALU.add,
                                                   op1=ALU.subtract)
                ins.then_inc(proj_lo, 1)

            for i in range(CT, TILES):
                tile_lo(-1, i)
            for h in range(2):
                for t in range(QT):
                    await_logits(0, h, t)
                    logits_and_max(0, h, t)

            def steps(c, last):
                for h in range(H):
                    ahead = (c, h + 2) if h + 2 < H else (c + 1, h + 2 - H)
                    more = h + 2 < H or not last
                    for t in range(QT):
                        if more:
                            await_logits(*ahead, t)
                        split_lo(c, h, t)
                        if more:
                            logits_and_max(*ahead, t)
                    for i in finished_tiles(h):
                        if not last or i < CT:
                            tile_lo(c, i)
                    if h >= 2:
                        add_output(c, h - 2)
                    elif not (isinstance(c, int) and c == 0):
                        add_output(c - 1, H + h - 2)

            over_chunks(dve, steps)
            add_output(NC - 1, H - 2)
            add_output(NC - 1, H - 1)

        @block.gpsimd
        def _(pool):
            def maxima(c, h):
                n = H * c + h
                pool.wait_ge(t_done, QT * (n + 1))
                wait(pool, p_done, QT * (n - H + 1))
                wait(pool, a_done, n - H + 1)
                pool.tensor_tensor(m_diff[:, h, :], m_old[:, h, :], m_new[:, h, :],
                                   ALU.subtract).then_inc(m_ready, 1)
                pool.tensor_scalar(m_neg[:, h, :], m_new[:, h, :], -1.0, None, ALU.mult).then_inc(m_ready, 1)
                pool.wait_ge(m_ready, 2 * (n + 1))
                pool.tensor_tensor(m_old[:, h, :], m_new[:, h, :], one[:], ALU.mult).then_inc(m_saved, 1)

            def rescale(c, h):
                n = H * c + h
                pool.wait_ge(a_done, n + 1)
                wait(pool, l_done, n - H + 1)
                wait(pool, o_done, n - H + 1)
                pool.tensor_tensor(l[:, h, :], l[:, h, :], alpha[:, h, :], ALU.mult).then_inc(l_scaled, 1)
                pool.tensor_tensor(o[:, :, h, :], o[:, :, h, :],
                                   alpha[:, h, :].rearrange("p (t a) -> p t a", a=1).to_broadcast([P, QT, HD]),
                                   ALU.mult).then_inc(o_scaled, 1)
                pool.wait_ge(p_done, QT * (n + 1))
                pool.wait_ge(l_scaled, n + 1)
                pool.tensor_tensor(l[:, h, :], l[:, h, :], row_sum[:, h, :], ALU.add).then_inc(l_done, 1)

            pool.memset(one[:], 1.0).then_inc(one_set, 1)
            pool.wait_ge(one_set, 1)
            maxima(0, 0)
            rescale(0, 0)
            maxima(0, 1)

            def steps(c, last):
                for h in range(H):
                    if h + 1 < H:
                        rescale(c, h + 1)
                    elif not last:
                        rescale(c + 1, 0)
                    if h + 2 < H:
                        maxima(c, h + 2)
                    elif not last:
                        maxima(c + 1, h + 2 - H)

            over_chunks(pool, steps)


def attention_output(nc, A, S):
    with ExitStack() as ctx:
        def sb(name, shape, dt=F32):
            return ctx.enter_context(nc.sbuf_tensor(name, shape, dt))

        def sem(name):
            return ctx.enter_context(nc.semaphore(name))

        wo = sb("wo", [P, DB, D])
        bv = sb("bv", [P, D])
        bo = sb("bo", [P, D])
        l_inv = sb("l_inv", [P, H, QT])
        a = sb("a", [P, QT, D])
        aT = sb("aT", [P, DB, NQ])
        aT_ps = [ctx.enter_context(nc.psum_tensor(f"aT_ps{i}", [P, 512], F32)) for i in range(2)]
        y_ps = [ctx.enter_context(nc.psum_tensor(f"y_ps{i}", [P, 512], F32)) for i in range(QT)]
        w_ld, b_ld = sem("wo_ld"), sem("bo_ld")
        chain = sem("out_chain")
        a_ready, aT_full, aT_ready, y_full = sem("a_ready"), sem("aT_full"), sem("aT_ready"), sem("y_full")
        block = ctx.enter_context(nc.Block())

        @block.sync
        def _(sp):
            sp.dma_start(wo[:], A["xWo"].rearrange("(j p) n -> p j n", p=P)).then_inc(w_ld, 16)
            for dst, src in ((bv, "xbv"), (bo, "xbo")):
                sp.dma_start(dst[:], A[src].rearrange("(a d) -> a d", a=1).to_broadcast([P, D])).then_inc(b_ld, 16)

        @block.vector
        def _(dve):
            n = [0]

            def link(ins):
                n[0] += 1
                ins.then_inc(chain, 1)
                dve.wait_ge(chain, n[0])

            link(dve.reciprocal(l_inv[:], S["l"][:]))
            dve.wait_ge(b_ld, 32)
            for t in range(QT):
                link(dve.tensor_tensor(a[:, t, :].rearrange("p (h d) -> p h d", h=H), S["o"][:, t, :, :],
                                       l_inv[:, :, t:t + 1].to_broadcast([P, H, HD]), ALU.mult))
                dve.tensor_tensor(a[:, t, :], a[:, t, :], bv[:], ALU.add).then_inc(a_ready, 1)
                link(dve.tensor_tensor(S["x"][:, t, :], S["x"][:, t, :], bo[:], ALU.add))
            for i in range(2):
                dve.wait_ge(aT_full, i + 1)
                dve.tensor_copy(aT[:, 2 * i:2 * i + 2, :], aT_ps[i][:].rearrange("p (j q) -> p j q", j=2)
                                ).then_inc(aT_ready, 1)
            for t in range(QT):
                dve.wait_ge(y_full, t + 1)
                link(dve.tensor_tensor(S["x"][:, t, :], S["x"][:, t, :], y_ps[t][:], ALU.add))

        @block.tensor
        def _(pe):
            pe.wait_ge(a_ready, QT)
            for i in range(2):
                for j in (2 * i, 2 * i + 1):
                    for t in range(QT):
                        at = (j % 2) * NQ + t * P
                        last = pe.transpose(aT_ps[i][:, at:at + P], a[:, t, bass.ts(j, P)], S["ident"][:])
                last.then_inc(aT_full, 1)
            pe.wait_ge(w_ld, 16)
            pe.wait_ge(aT_ready, 2)
            for t in range(QT):
                for j in range(DB):
                    last = pe.matmul(y_ps[t][:], aT[:, j, bass.ts(t, P)], wo[:, j, :],
                                     start=(j == 0), stop=(j == DB - 1))
                last.then_inc(y_full, 1)


class Banks:

    def __init__(self, nc, ctx, name, count, order):
        self.bank = [ctx.enter_context(nc.psum_tensor(f"{name}{b}", [P, 512], F32)) for b in range(count)]
        self.full = [ctx.enter_context(nc.semaphore(f"{name}_full{b}")) for b in range(count)]
        self.free = [ctx.enter_context(nc.semaphore(f"{name}_free{b}")) for b in range(count)]
        self.at = {key: (i % count, i // count) for i, key in enumerate(order)}
        assert len(self.at) == len(order)
        self.rounds = len(order) // count

    def __getitem__(self, key):
        return self.bank[self.at[key][0]]

    def wait_free(self, pe, key, j=0):
        b, use = self.at[key]
        value = use + self.rounds * j
        if not isinstance(value, int) or value > 0:
            pe.wait_ge(self.free[b], value)

    def wait_full(self, eng, key, j=0):
        b, use = self.at[key]
        eng.wait_ge(self.full[b], use + 1 + self.rounds * j)

    def wait_read(self, eng, key, j=0):
        b, use = self.at[key]
        eng.wait_ge(self.free[b], use + 1 + self.rounds * j)

    def is_full(self, ins, key):
        ins.then_inc(self.full[self.at[key][0]], 1)

    def is_free(self, ins, key):
        ins.then_inc(self.free[self.at[key][0]], 1)


def self_attention(nc, A, S):
    DH = 64
    W = H * DH
    WB = W // P
    EPS = 1e-8
    with ExitStack() as ctx:
        def sb(name, shape, dt=F32):
            return ctx.enter_context(nc.sbuf_tensor(name, shape, dt))

        def sem(name):
            return ctx.enter_context(nc.semaphore(name))

        wq = sb("awq", [P, DB, W])
        wkv = sb("awkv", [P, DB, 2 * W])
        wo = sb("awo", [P, WB, D])
        bo = sb("abo", [P, D])
        stats = sb("a_stats", [P, QT, 6])
        mv = sb("a_mv", [P, QT, 2])
        veps = sb("a_veps", [P, QT])
        std = sb("a_std", [P, QT])
        rstd = sb("a_rstd", [P, QT])
        xn = sb("a_xn", [P, QT, D])
        xnT = sb("a_xnT", [P, DB, NQ])
        q_pad = sb("a_q", [P, H, NQ])
        kT = sb("a_kT", [P, WB, NQ])
        v = sb("a_v", [P, QT, W])
        causal = sb("causal", [P, QT, NQ])
        mx = sb("a_max", [P, H, QT])
        mneg = sb("a_mneg", [P, H, QT])
        e = sb("a_e", [P, 2, QT, NQ])
        p = sb("a_p", [P, 2, QT, NQ])
        den = sb("a_den", [P, H, QT])
        den_eps = sb("a_den_eps", [P, H, QT])
        rden = sb("a_rden", [P, H, QT])
        pT = sb("a_pT", [P, 2, 3 * P])
        a = sb("a_a", [P, QT, W])
        aT = sb("a_aT", [P, WB, NQ])

        order = [("xnT", i) for i in range(2)]
        order += [(k, i) for i in range(4) for k in ("q", "k")] + [("v", i) for i in range(4)]
        order += [("s", 0), ("s", 1)]
        for h in range(H):
            order += [("pT", h)] + ([("s", h + 2)] if h + 2 < H else []) + ([("o", h - 1)] if h else [])
        order += [("o", H - 1)] + [("aT", i) for i in range(4)] + [("y", t) for t in range(QT)]
        ps = Banks(nc, ctx, "a_ps", 8, order)

        w_ld, b_ld = [sem(f"aw_ld{i}") for i in range(3)], sem("abo_ld")
        chain = sem("a_chain")
        causal_set, q_zero = sem("causal_set"), sem("q_zero")
        var_ready, std_ready, xn_ready = sem("a_var_ready"), sem("a_std_ready"), sem("a_xn_ready")
        m_ready, p_ready = sem("a_m_ready"), sem("a_p_ready")
        block = ctx.enter_context(nc.Block())

        @block.sync
        def _(sp):
            sp.dma_start(wq[:], A["aWq"].rearrange("(j p) n -> p j n", p=P)).then_inc(w_ld[0], 16)
            sp.dma_start(wkv[:], A["aWkv"].rearrange("(j p) n -> p j n", p=P)).then_inc(w_ld[1], 16)
            sp.dma_start(wo[:], A["aWo"].rearrange("(j p) n -> p j n", p=P)).then_inc(w_ld[2], 16)
            sp.dma_start(bo[:], A["abo"].rearrange("(a d) -> a d", a=1).to_broadcast([P, D])).then_inc(b_ld, 16)

        @block.gpsimd
        def _(pool):
            pool.memset(q_pad[:], 0.0).then_inc(q_zero, 1)
            pool.memset(causal[:], 1.0).then_inc(causal_set, 1)
            pool.wait_ge(causal_set, 1)
            for t in range(QT):
                pool.affine_select(out=causal[:, t, :], in_=causal[:, t, :], compare_op=ALU.is_ge, fill=0.0,
                                   base=t * P, pattern=[[-1, NQ]], channel_multiplier=1).then_inc(causal_set, 1)

        def copy_pT(act, h):
            ps.wait_full(act, ("pT", h))
            if h >= 2:
                ps.wait_full(act, ("o", h - 2))
            ins = nc.scalar.activation(pT[:, h % 2, :], ps["pT", h][:, 0:3 * P], ACT.Copy)
            ps.is_free(ins, ("pT", h))

        @block.scalar
        def _(act):
            act.wait_ge(var_ready, 1)
            nc.scalar.activation(std[:], veps[:], ACT.Sqrt).then_inc(std_ready, 1)
            act.wait_ge(q_zero, 1)
            for i in range(4):
                ps.wait_full(act, ("q", i))
                src = ps["q", i][:].rearrange("p (b q) -> p b q", b=2)
                for r in range(2):
                    rows = slice(DH * r, DH * (r + 1))
                    ins = nc.scalar.activation(q_pad[rows, 4 * i + r:4 * i + r + 3:2, :], src[rows], ACT.Copy,
                                               scale=DH ** -0.5)
                ps.is_free(ins, ("q", i))
            for h in range(H):
                act.wait_ge(m_ready, h + 1)
                if h >= 2:
                    act.wait_ge(p_ready, QT * (h - 1))
                for t in range(QT):
                    ins = nc.scalar.activation(e[:, h % 2, t, :], ps["s", h][:, t * NQ:(t + 1) * NQ], ACT.Exp,
                                               bias=mneg[:, h, t:t + 1])
                ps.is_free(ins, ("s", h))
                if h:
                    copy_pT(act, h - 1)
            copy_pT(act, H - 1)

        @block.vector
        def _(dve):
            n = [0]

            def link(ins):
                n[0] += 1
                ins.then_inc(chain, 1)
                dve.wait_ge(chain, n[0])

            for t in range(QT):
                link(dve.bn_stats(stats[:, t, :], S["x"][:, t, :]))
                link(dve.bn_aggr(mv[:, t, :], stats[:, t, :]))
            dve.tensor_scalar(veps[:], mv[:, :, 1], LN_EPS, None, ALU.add).then_inc(var_ready, 1)
            dve.wait_ge(std_ready, 1)
            link(dve.reciprocal(rstd[:], std[:]))
            for t in range(QT):
                dve.tensor_scalar(xn[:, t, :], S["x"][:, t, :], mv[:, t, 0:1], rstd[:, t:t + 1],
                                  ALU.subtract, ALU.mult).then_inc(xn_ready, 1)
            dve.wait_ge(b_ld, 16)
            for t in range(QT):
                link(dve.tensor_tensor(S["x"][:, t, :], S["x"][:, t, :], bo[:], ALU.add))

            def take(key, dst, src):
                ps.wait_full(dve, key)
                ps.is_free(dve.tensor_copy(dst, src), key)

            for i in range(2):
                take(("xnT", i), xnT[:, 2 * i:2 * i + 2, :],
                     ps["xnT", i][:].rearrange("p (j q) -> p j q", j=2))
            for i in range(4):
                take(("k", i), kT[:, 2 * i:2 * i + 2, :], ps["k", i][:].rearrange("p (j q) -> p j q", j=2))
            for i in range(4):
                take(("v", i), v[:, i // 2, bass.ts(i % 2, D)], ps["v", i][:])

            def maximum(h):
                ps.wait_full(dve, ("s", h))
                link(dve.tensor_reduce(mx[:, h, :], ps["s", h][:].rearrange("p (t k) -> p t k", t=QT), AX_X, ALU.max))
                dve.tensor_scalar(mneg[:, h, :], mx[:, h, :], -1.0, None, ALU.mult).then_inc(m_ready, 1)

            def mask(h):
                ps.wait_read(dve, ("s", h))
                if h >= 2:
                    ps.wait_full(dve, ("pT", h - 2))
                for t in range(QT):
                    dve.tensor_tensor_reduce(p[:, h % 2, t, :], e[:, h % 2, t, :], causal[:, t, :], 1.0, 0.0,
                                             ALU.mult, ALU.add, den[:, h, t:t + 1]).then_inc(p_ready, 1)
                dve.wait_ge(p_ready, QT * (h + 1))
                link(dve.tensor_scalar(den_eps[:, h, :], den[:, h, :], EPS, None, ALU.add))
                link(dve.reciprocal(rden[:, h, :], den_eps[:, h, :]))

            def normalise(h):
                ps.wait_full(dve, ("o", h))
                for t in range(QT):
                    ins = dve.tensor_scalar(a[:, t, bass.ts(h, DH)], ps["o", h][:, bass.ts(t, DH)],
                                            rden[:, h, t:t + 1], None, ALU.mult)
                ps.is_free(ins, ("o", h))

            dve.wait_ge(causal_set, 1 + QT)
            maximum(0)
            for h in range(H):
                if h + 1 < H:
                    maximum(h + 1)
                mask(h)
                if h:
                    normalise(h - 1)
            normalise(H - 1)
            for i in range(4):
                take(("aT", i), aT[:, 2 * i:2 * i + 2, :], ps["aT", i][:].rearrange("p (j q) -> p j q", j=2))
            for t in range(QT):
                ps.wait_full(dve, ("y", t))
                link(dve.tensor_tensor(S["x"][:, t, :], S["x"][:, t, :], ps["y", t][:], ALU.add))

        @block.tensor
        def _(pe):
            def turn(key, src):
                ps.wait_free(pe, key)
                for j in range(2):
                    for t in range(QT):
                        at = j * NQ + t * P
                        last = pe.transpose(ps[key][:, at:at + P], src[:, t, bass.ts(2 * key[1] + j, P)],
                                            S["ident"][:])
                ps.is_full(last, key)

            pe.wait_ge(xn_ready, QT)
            for i in range(2):
                turn(("xnT", i), xn)
            ps.wait_read(pe, ("xnT", 0))
            ps.wait_read(pe, ("xnT", 1))
            pe.wait_ge(w_ld[0], 16)
            pe.wait_ge(w_ld[1], 16)
            for i in range(4):
                for k, w in (("q", wq), ("k", wkv)):
                    ps.wait_free(pe, (k, i))
                    for b in range(2):
                        for j in range(DB):
                            last = pe.matmul(ps[k, i][:, bass.ts(b, NQ)], w[:, j, bass.ts(2 * i + b, P)],
                                             xnT[:, j, :], start=(j == 0), stop=(j == DB - 1))
                    ps.is_full(last, (k, i))
            for i in range(4):
                ps.wait_free(pe, ("v", i))
                for j in range(DB):
                    last = pe.matmul(ps["v", i][:], xnT[:, j, bass.ts(i // 2, P)],
                                     wkv[:, j, W + (i % 2) * D:W + (i % 2 + 1) * D],
                                     start=(j == 0), stop=(j == DB - 1))
                ps.is_full(last, ("v", i))

            def scores(h):
                ps.wait_free(pe, ("s", h))
                if h % 4 == 0:
                    ps.wait_read(pe, ("q", h // 4))
                    ps.wait_read(pe, ("k", h // 4))
                for t in range(QT):
                    last = pe.matmul(ps["s", h][:, bass.ts(t, NQ)], q_pad[:, h, bass.ts(t, P)], kT[:, h // 2, :],
                                     start=True, stop=True)
                ps.is_full(last, ("s", h))

            def turn_probabilities(h):
                ps.wait_free(pe, ("pT", h))
                pe.wait_ge(p_ready, QT * (h + 1))
                for i, (t, b) in enumerate(((0, 0), (1, 0), (1, 1))):
                    last = pe.transpose(ps["pT", h][:, bass.ts(i, P)], p[:, h % 2, t, bass.ts(b, P)], S["ident"][:])
                ps.is_full(last, ("pT", h))

            def values(h):
                ps.wait_free(pe, ("o", h))
                ps.wait_read(pe, ("pT", h))
                if h == 0:
                    ps.wait_read(pe, ("v", 3))
                for t in range(QT):
                    for b in range(t + 1):
                        last = pe.matmul(ps["o", h][:, bass.ts(t, DH)], pT[:, h % 2, bass.ts(t + b, P)],
                                         v[:, b, bass.ts(h, DH)], start=(b == 0), stop=(b == t))
                ps.is_full(last, ("o", h))

            scores(0)
            scores(1)
            for h in range(H):
                turn_probabilities(h)
                if h + 2 < H:
                    scores(h + 2)
                if h:
                    values(h - 1)
            values(H - 1)
            ps.wait_read(pe, ("o", H - 1))
            for i in range(4):
                turn(("aT", i), a)
            pe.wait_ge(w_ld[2], 16)
            ps.wait_read(pe, ("aT", 3))
            for t in range(QT):
                ps.wait_free(pe, ("y", t))
                for j in range(WB):
                    last = pe.matmul(ps["y", t][:], aT[:, j, bass.ts(t, P)], wo[:, j, :],
                                     start=(j == 0), stop=(j == WB - 1))
                ps.is_full(last, ("y", t))


def moe(nc, A, S):
    LAYERS, E, _ = A["rb"].shape[0], A["rb"].shape[1], None
    RMS_EPS = 1e-6
    FAR = 1e30
    U = E + 2
    WR = 11
    NB = 6
    BUP, BG, SBUP, SBG = 0, E * DB, 2 * E * DB, 2 * E * DB + 2 * DB
    NBIAS = SBG + DB
    assert D // P == DB and NBIAS <= P

    ops = []
    for i in range(U + 2):
        ops += [("up", i)] if i < U else []
        ops += [("down", i - 2)] if 0 <= i - 2 and i - 2 != U - 2 else []
        ops += [("g", i - 1)] if 0 <= i - 1 < U else []
    MIX_AT = 3
    order = [("xT", i) for i in range(2)] + [("gate", t) for t in range(QT)]
    for i, (kind, u) in enumerate(ops):
        if i == MIX_AT:
            order += [("wT", t) for t in range(QT)] + [("bd", t) for t in range(QT)]
        order += [(kind, u, t) for t in range(2)]
    def matrix(kind, u):
        if kind == "up":
            return ("up", u)
        return (kind, min(u, E))
    matrices, last_use = [], {}
    for kind, u in ops:
        m = matrix(kind, u)
        if m not in matrices:
            matrices.append(m)
        last_use[m] = (kind, u, 1)
    NM = len(matrices)
    assert NM % WR == 0 and len(order) % NB == 0

    def source(m):
        kind, u = m
        if kind == "up":
            w = A["eWup"][u] if u < E else A["sWup"][:, (u - E) * D:(u - E + 1) * D]
        elif kind == "g":
            w = A["eWg"][u] if u < E else A["sWg"]
        else:
            w = A["eWdown"][u] if u < E else A["sWdown"]
        return w.rearrange("(j p) n -> p j n", p=P)

    with ExitStack() as ctx:
        def sb(name, shape, dt=F32):
            return ctx.enter_context(nc.sbuf_tensor(name, shape, dt))

        def sem(name):
            return ctx.enter_context(nc.semaphore(name))

        w_sb = sb("m_w", [P, WR, DB, D])
        bias_rows = sb("bias_rows", [NBIAS, P])
        bias = sb("bias_cols", [P, NBIAS])
        bdown = sb("bdown", [E + 1, D])
        rw = sb("router_w", [P, LAYERS, DB, E])
        rb = sb("router_b", [P, LAYERS, E])
        gb = sb("gate_bias", [P, LAYERS, E])
        nw = sb("norm_w", [P, LAYERS, D])
        earlier = sb("earlier", [P, E, E])
        stats = sb("m_stats", [P, QT, 6])
        mv = sb("m_mv", [P, QT, 2])
        veps = sb("m_veps", [P, QT])
        std = sb("m_std", [P, QT])
        rstd = sb("m_rstd", [P, QT])
        xf = sb("xf", [P, QT, D])
        xfT = sb("xfT", [P, DB, NQ])
        acc = sb("acc", [P, QT, D])
        square = sb("square", [P, QT, D])
        sq_sum = sb("sq_sum", [P, QT])
        hT = sb("hT", [P, 2, DB, NQ])
        sT = sb("sT", [P, 2, DB, NQ])
        aT = sb("m_aT", [P, 2, DB, NQ])
        gate = sb("gate", [P, QT, E])
        biased = sb("biased", [P, QT, E])
        above = sb("above", [P, QT, E, E])
        ties = sb("ties", [P, QT, E, E])
        rank = sb("rank", [P, QT, E])
        sel = sb("sel", [P, QT, E])
        far = sb("far", [P, QT, E])
        gate_max = sb("gate_max", [P, QT])
        e_sum = sb("e_sum", [P, QT])
        e_gate = sb("e_gate", [P, QT, E])
        wt = sb("wt", [P, QT, E + 1])
        wT = sb("wT", [E + 1, QT, P])

        ps = Banks(nc, ctx, "m_ps", NB, order)
        bias_ps = ctx.enter_context(nc.psum_tensor("bias_ps", [P, 512], F32))
        w_ld = [sem(f"m_w_ld{i}") for i in range(WR)]
        bias_ld, small_ld = sem("bias_ld_m"), sem("small_ld")
        consts, bias_full, bias_ready = sem("m_consts"), sem("bias_full"), sem("bias_ready")
        chain = sem("m_chain")
        var_ready, std_ready = sem("m_var_ready"), sem("m_std_ready")
        xf_ready = sem("xf_ready")
        far_ready, gate_e = sem("far_ready"), sem("gate_e")
        wt_ready, a_done = sem("wt_ready"), sem("m_a_done")
        A_OPS = 2 * U + 2
        block = ctx.enter_context(nc.Block())

        @block.sync
        def _(sp):
            def load(layer, i):
                seq = layer * NM + i
                if seq >= WR:
                    before = seq - WR
                    ps.wait_full(sp, last_use[matrices[before % NM]], before // NM)
                sp.dma_start(w_sb[:, i % WR, :, :], source(matrices[i])).then_inc(w_ld[i % WR], 16)

            load(0, 0)
            row = 0
            for name, pat, count in (("ebup", "e (i p) -> (e i) p", E * DB), ("ebg", "e (i p) -> (e i) p", E * DB),
                                     ("sbup", "(i p) -> i p", 2 * DB), ("sbg", "(i p) -> i p", DB)):
                sp.dma_start(bias_rows[row:row + count, :], A[name].rearrange(pat, p=P)).then_inc(bias_ld, 16)
                row += count
            for layer in range(LAYERS):
                sp.dma_start(rw[:, layer, :, :], A["rW"][layer].rearrange("(j p) e -> p j e", p=P)
                             ).then_inc(small_ld, 16)
            for dst, src, width in ((rb, "rb", E), (gb, "gb", E), (nw, "nw", D)):
                flat = A[src].rearrange("(a l) e -> a l e", a=1)
                sp.dma_start(dst[:], flat.to_broadcast([P, LAYERS, width])).then_inc(small_ld, 16)
            sp.dma_start(bdown[0:E, :], A["ebdown"]).then_inc(small_ld, 16)
            sp.dma_start(bdown[E:E + 1, :], A["sbdown"].rearrange("(a d) -> a d", a=1)).then_inc(small_ld, 16)
            for layer in range(LAYERS):
                for i in range(NM):
                    if layer or i:
                        load(layer, i)

        SMALL = 16 * (LAYERS + 5)

        @block.gpsimd
        def _(pool):
            pool.memset(wt[:], 2.0).then_inc(consts, 1)
            pool.memset(earlier[:], 1.0).then_inc(consts, 1)
            pool.wait_ge(consts, 2)
            pool.affine_select(out=earlier[:], in_=earlier[:], compare_op=ALU.is_gt, fill=0.0, base=0,
                               pattern=[[1, E], [-1, E]], channel_multiplier=0).then_inc(consts, 1)

        def bias_column(kind, u, b):
            if kind == "up":
                at = BUP + u * DB + b if u < E else SBUP + (u - E) * DB + b
            else:
                at = BG + u * DB + b if u < E else SBG + b
            return bias[:, at:at + 1]

        @block.scalar
        def _(act):
            act.wait_ge(var_ready, 1)
            nc.scalar.activation(std[:], veps[:], ACT.Sqrt).then_inc(std_ready, 1)
            act.wait_ge(bias_ready, 1)
            with act.Fori(0, LAYERS) as j:
                for i, (kind, u) in enumerate(ops):
                    if i == 2:
                        act.wait_ge(far_ready, j + 1)
                        for t in range(QT):
                            nc.scalar.activation(e_gate[:, t, :], far[:, t, :], ACT.Exp, bias=gate_max[:, t:t + 1],
                                                 accum_out=e_sum[:, t:t + 1]).then_inc(gate_e, 1)
                    if kind == "down":
                        continue
                    dst, func = (hT, ACT.Identity) if kind == "up" else (sT, ACT.Silu)
                    act.wait_ge(a_done, A_OPS * j + max(0, 2 * (u - 1)))
                    for tile in range(2):
                        ps.wait_full(act, (kind, u, tile), j)
                        for r in range(2):
                            b = 2 * tile + r
                            ins = nc.scalar.activation(dst[:, u % 2, b, :], ps[kind, u, tile][:, bass.ts(r, NQ)],
                                                       func, bias=bias_column(kind, u, b))
                        ps.is_free(ins, (kind, u, tile))
                act.wait_ge(var_ready, j + 2)
                nc.scalar.activation(std[:], veps[:], ACT.Sqrt).then_inc(std_ready, 1)

        @block.vector
        def _(dve):
            n = [0]
            base = [0]

            def link(ins):
                n[0] += 1
                ins.then_inc(chain, 1)
                dve.wait_ge(chain, base[0] + n[0])

            for t in range(QT):
                link(dve.bn_stats(stats[:, t, :], S["x"][:, t, :]))
                link(dve.bn_aggr(mv[:, t, :], stats[:, t, :]))
            dve.tensor_scalar(veps[:], mv[:, :, 1], LN_EPS, None, ALU.add).then_inc(var_ready, 1)
            dve.wait_ge(std_ready, 1)
            link(dve.reciprocal(rstd[:], std[:]))
            for t in range(QT):
                dve.tensor_scalar(xf[:, t, :], S["x"][:, t, :], mv[:, t, 0:1], rstd[:, t:t + 1],
                                  ALU.subtract, ALU.mult).then_inc(xf_ready, 1)
            dve.wait_ge(bias_full, 1)
            dve.tensor_copy(bias[:], bias_ps[:, 0:NBIAS]).then_inc(bias_ready, 1)
            dve.wait_ge(small_ld, SMALL)
            dve.wait_ge(consts, 3)
            before = n[0]
            n[0] = 0

            def router(j):
                one = bass.ds(j, 1)
                for t in range(QT):
                    ps.wait_full(dve, ("gate", t), j)
                    ps.is_free(dve.tensor_tensor(gate[:, t:t + 1, :], ps["gate", t][:, 0:E].rearrange(
                        "p (a e) -> p a e", a=1), rb[:, one, :], ALU.add), ("gate", t))
                ps.wait_read(dve, ("gate", QT - 1), j)
                for t in range(QT):
                    link(dve.tensor_tensor(biased[:, t:t + 1, :], gate[:, t:t + 1, :], gb[:, one, :], ALU.add))
                for t in range(QT):
                    other = biased[:, t:t + 1, :].to_broadcast([P, E, E])
                    own = biased[:, t, :].rearrange("p (e a) -> p e a", a=1).to_broadcast([P, E, E])
                    link(dve.tensor_tensor(above[:, t, :, :], other, own, ALU.is_gt))
                    link(dve.tensor_tensor(ties[:, t, :, :], other, own, ALU.is_equal))
                    link(dve.tensor_tensor(ties[:, t, :, :], ties[:, t, :, :], earlier[:], ALU.mult))
                link(dve.tensor_tensor(above[:], above[:], ties[:], ALU.add))
                link(dve.tensor_reduce(rank[:], above[:], AX_X, ALU.add))
                link(dve.tensor_scalar(sel[:], rank[:], 1.5, None, ALU.is_lt))
                link(dve.tensor_scalar(far[:], sel[:], 1.0, FAR, ALU.subtract, ALU.mult))
                link(dve.tensor_tensor(sel[:], sel[:], gate[:], ALU.mult))
                link(dve.tensor_tensor(far[:], far[:], sel[:], ALU.add))
                link(dve.tensor_reduce(gate_max[:], far[:], AX_X, ALU.max))
                dve.tensor_scalar(gate_max[:], gate_max[:], -1.0, None, ALU.mult).then_inc(far_ready, 1)

            def weights(j):
                dve.wait_ge(gate_e, QT * j + QT)
                link(dve.reciprocal(e_sum[:], e_sum[:]))
                for t in range(QT):
                    dve.tensor_scalar(wt[:, t, 0:E], e_gate[:, t, :], e_sum[:, t:t + 1], None, ALU.mult
                                      ).then_inc(wt_ready, 1)
                for t in range(QT):
                    ps.wait_full(dve, ("wT", t), j)
                    ps.is_free(dve.tensor_copy(wT[:, t, :], ps["wT", t][0:E + 1, 0:P]), ("wT", t))
                for t in range(QT):
                    ps.wait_full(dve, ("bd", t), j)
                    ps.is_free(dve.tensor_tensor(acc[:, t, :], xf[:, t, :], ps["bd", t][:], ALU.add), ("bd", t))

            def gated(j, u):
                for tile in range(2):
                    ps.wait_read(dve, ("g", u, tile), j)
                    if tile == 0 and u >= 2:
                        ps.wait_full(dve, ("down", u - 2, 1), j)
                    two = slice(2 * tile, 2 * tile + 2)
                    dve.tensor_tensor(aT[:, u % 2, two, :], sT[:, u % 2, two, :], hT[:, u % 2, two, :],
                                      ALU.mult).then_inc(a_done, 1)
                if u == U - 1:
                    dve.wait_ge(a_done, A_OPS * j + 2 * U)
                    for tile in range(2):
                        two = slice(2 * tile, 2 * tile + 2)
                        dve.tensor_tensor(aT[:, 1, two, :], aT[:, 1, two, :], aT[:, 0, two, :],
                                          ALU.add).then_inc(a_done, 1)

            def accumulate(j, u):
                for t in range(QT):
                    key = ("down", u, t)
                    ps.wait_full(dve, key, j)
                    if u == 0:
                        ps.wait_read(dve, ("bd", t), j)
                    else:
                        ps.wait_read(dve, ("down", u - 1 if u < E else E - 1, t), j)
                    if u < E:
                        ins = dve.scalar_tensor_tensor(out=acc[:, t, :], in0=ps[key][:], scalar=wt[:, t, u:u + 1],
                                                       in1=acc[:, t, :], op0=ALU.mult, op1=ALU.add)
                    else:
                        ins = dve.tensor_tensor(acc[:, t, :], acc[:, t, :], ps[key][:], ALU.add)
                    ps.is_free(ins, key)

            LINKS = 19
            with dve.Fori(0, LAYERS) as j:
                base[0] = LINKS * j + before
                for i in range(2):
                    ps.wait_full(dve, ("xT", i), j)
                    ps.is_free(dve.tensor_copy(xfT[:, 2 * i:2 * i + 2, :],
                                               ps["xT", i][:].rearrange("p (j q) -> p j q", j=2)), ("xT", i))
                router(j)
                for i, (kind, u) in enumerate(ops):
                    if i == MIX_AT:
                        weights(j)
                    if kind == "g":
                        gated(j, u)
                    elif kind == "down":
                        accumulate(j, u)
                ps.wait_read(dve, ("down", U - 1, QT - 1), j)
                for t in range(QT):
                    link(dve.tensor_tensor_reduce(square[:, t, :], acc[:, t, :], acc[:, t, :], 1.0, 0.0, ALU.mult,
                                                  ALU.add, sq_sum[:, t:t + 1]))
                dve.tensor_scalar(veps[:], sq_sum[:], 1.0 / D, RMS_EPS, ALU.mult, ALU.add).then_inc(var_ready, 1)
                dve.wait_ge(std_ready, j + 2)
                link(dve.reciprocal(rstd[:], std[:]))
                for t in range(QT):
                    dve.scalar_tensor_tensor(out=xf[:, t:t + 1, :], in0=acc[:, t:t + 1, :], scalar=rstd[:, t:t + 1],
                                             in1=nw[:, bass.ds(j, 1), :], op0=ALU.mult, op1=ALU.mult
                                             ).then_inc(xf_ready, 1)
                assert n[0] == LINKS, n[0]
            dve.wait_ge(xf_ready, QT * (LAYERS + 1))
            for t in range(QT):
                n[0] += 1
                dve.tensor_tensor(S["x"][:, t, :], S["x"][:, t, :], xf[:, t, :], ALU.add)

        @block.tensor
        def _(pe):
            pe.wait_ge(bias_ld, 64)
            pe.transpose(bias_ps[:, 0:NBIAS], bias_rows[:], S["ident"][0:NBIAS, 0:NBIAS]).then_inc(bias_full, 1)
            pe.wait_ge(small_ld, SMALL)
            with pe.Fori(0, LAYERS) as j:
                pe.wait_ge(xf_ready, QT * j + QT)
                for i in range(2):
                    ps.wait_free(pe, ("xT", i), j)
                    for b in range(2):
                        for t in range(QT):
                            at = b * NQ + t * P
                            last = pe.transpose(ps["xT", i][:, at:at + P], xf[:, t, bass.ts(2 * i + b, P)],
                                                S["ident"][:])
                    ps.is_full(last, ("xT", i))
                ps.wait_read(pe, ("xT", 0), j)
                ps.wait_read(pe, ("xT", 1), j)
                for t in range(QT):
                    ps.wait_free(pe, ("gate", t), j)
                    for b in range(DB):
                        last = pe.matmul(ps["gate", t][:, 0:E], xfT[:, b, bass.ts(t, P)],
                                         rw[:, bass.ds(j, 1), b, :].rearrange("p a e -> p (a e)"),
                                         start=(b == 0), stop=(b == DB - 1))
                    ps.is_full(last, ("gate", t))

                def mix():
                    pe.wait_ge(wt_ready, QT * j + QT)
                    for t in range(QT):
                        ps.wait_free(pe, ("wT", t), j)
                        ps.is_full(pe.transpose(ps["wT", t][0:E + 1, 0:P], wt[:, t, :], S["ident"][:]), ("wT", t))
                    for t in range(QT):
                        ps.wait_free(pe, ("bd", t), j)
                        ps.wait_read(pe, ("wT", t), j)
                        ps.is_full(pe.matmul(ps["bd", t][:], wT[:, t, :], bdown[:], start=True, stop=True), ("bd", t))

                for i, (kind, u) in enumerate(ops):
                    if i == MIX_AT:
                        mix()
                    m = matrices.index(matrix(kind, u))
                    pe.wait_ge(w_ld[m % WR], 16 * ((NM // WR) * j + m // WR + 1))
                    w = w_sb[:, m % WR, :, :]
                    if kind == "g":
                        ps.wait_read(pe, ("up", u, 0), j)
                        ps.wait_read(pe, ("up", u, 1), j)
                    if kind == "down":
                        pe.wait_ge(a_done, A_OPS * j + (2 * (u + 1) if u < E else A_OPS))
                    for tile in range(2):
                        ps.wait_free(pe, (kind, u, tile), j)
                        out = ps[kind, u, tile]
                        if kind == "down":
                            for b in range(DB):
                                last = pe.matmul(out[:], aT[:, u % 2, b, bass.ts(tile, P)], w[:, b, :],
                                                 start=(b == 0), stop=(b == DB - 1))
                        else:
                            for r in range(2):
                                for b in range(DB):
                                    x = xfT[:, b, :] if kind == "up" else hT[:, u % 2, b, :]
                                    last = pe.matmul(out[:, bass.ts(r, NQ)], w[:, b, bass.ts(2 * tile + r, P)], x,
                                                     start=(b == 0), stop=(b == DB - 1))
                        ps.is_full(last, (kind, u, tile))


def store(nc, A, S):
    with ExitStack() as ctx:
        stored = ctx.enter_context(nc.semaphore("stored"))
        block = ctx.enter_context(nc.Block())

        @block.sync
        def _(sp):
            sp.dma_start(A["out"].rearrange("(t p) d -> p t d", p=P), S["x"][:]).then_inc(stored, 16)
            sp.wait_ge(stored, 16)


def program(nc, A, stages):
    with ExitStack() as ctx:
        def sb(name, shape, dt=F32):
            return ctx.enter_context(nc.sbuf_tensor(name, shape, dt))

        S = {
            "x": sb("x_sb", [P, QT, D]),
            "ident": sb("ident", [P, P]),
            "fold": sb("fold", [2 * HD, HD]),
            "bk": sb("bk_sb", [P, NG]),
            "q_stack": sb("q_stack", [P, H, NQ], F32R),
            "m_old": sb("m_old", [P, H, QT]),
            "l": sb("l_run", [P, H, QT]),
            "o": sb("o_run", [P, QT, H, HD]),
            "mask_row": nc.dram_tensor("mask_row", [A["ctx"].shape[0]], F32, kind="Internal").ap(),
        }
        for w in ("wk_hi", "wk_lo", "wv_hi", "wv_lo"):
            S[w] = sb(w, [P, DB, D], F32R)
        for stage in stages:
            stage(nc, A, S)


_NAMES = {
    "x": "x", "ctx_1024": "ctx", "fside_Bx16xSxS2_0": "bias", "mask_BxS2_bk0": "mask",
    "L0_xattn_Wq": "xWq", "L0_xattn_bq": "xbq", "L0_xattn_Wk": "xWk", "L0_xattn_bk": "xbk",
    "L0_xattn_Wv": "xWv", "L0_xattn_bv": "xbv", "L0_xattn_Wo": "xWo", "L0_xattn_bo": "xbo",
    "L0_attn_Wq": "aWq", "L0_attn_Wkv": "aWkv", "L0_attn_Wo": "aWo", "L0_attn_bo": "abo",
    "L0_ffn_router_W": "rW", "L0_ffn_router_b": "rb", "L0_ffn_gate_bias": "gb",
    "L0_ffn_exp_Wup": "eWup", "L0_ffn_exp_bup": "ebup", "L0_ffn_exp_Wg": "eWg", "L0_ffn_exp_bg": "ebg",
    "L0_ffn_exp_Wdown": "eWdown", "L0_ffn_exp_bdown": "ebdown",
    "L0_ffn_share_Wup": "sWup", "L0_ffn_share_bup": "sbup", "L0_ffn_share_Wg": "sWg",
    "L0_ffn_share_bg": "sbg", "L0_ffn_share_Wdown": "sWdown", "L0_ffn_share_bdown": "sbdown",
    "L0_ffn_norm_w": "nw",
}
_BATCHED = ("x", "ctx", "bias", "mask")


def kernel(**inputs):
    import numpy as _np
    import concourse.bacc as _bacc
    from concourse import mybir as _mybir
    from concourse.bass_utils import run_bass_kernel_spmd as _run

    nc = _bacc.Bacc("TRN2", target_bir_lowering=False, num_devices=1)
    arrays, A = {}, {}
    for name, short in _NAMES.items():
        a = _np.ascontiguousarray(inputs[name])
        if short in _BATCHED:
            a = a.reshape(a.shape[1:])
        arrays[f"in_{short}_dram"] = a
        A[short] = nc.dram_tensor(f"in_{short}_dram", a.shape, _mybir.dt.from_np(a.dtype),
                                  kind="ExternalInput").ap()
    A["out"] = nc.dram_tensor("out_0_dram", A["x"].shape, _mybir.dt.float32, kind="ExternalOutput").ap()
    program(nc, A, (load_and_project_queries, cross_attention, attention_output, self_attention, moe, store))
    r = _run(nc, [arrays], core_ids=[0])
    got = r.results[0]["out_0_dram"]
    return got.reshape((1,) + got.shape)
```

```python
from contextlib import ExitStack

import concourse.bass as bass
from concourse import mybir

F32 = mybir.dt.float32
F32R = mybir.dt.float32r
U8 = mybir.dt.uint8
ALU = mybir.AluOpType
ACT = mybir.ActivationFunctionType
AX_X = mybir.AxisListType.X

P = 128
D = 512
DB = D // P
NQ = 256
QT = NQ // P
H = 16
HD = D // H
KC = 512
KB = KC // P
HG = P // HD
NG = H // HG
SCALE = HD ** -0.5
MASKED = -(2.0 ** 100)
NO_MAX = -3.0e38
LN_EPS = 1e-5

RING = 8
AHEAD = RING - 1
KDMA = 3 * HG + 1
TILES = 12
V1, CT, K01, V0, K23 = 0, 2, 6, 8, 10
K_TILE = {0: K01, 1: K01 + 1, 2: K23, 3: K23 + 1}
SHARE = [[(V1, 0)], [(V1, 1)], [(V1 + 1, 0)], [(V1 + 1, 1)],
         [(CT, 1), (CT + 1, 1)], [(CT + 2, 1), (CT + 3, 1)],
         [(K01, 0)], [(K01, 1)], [(K01 + 1, 0)], [(K01 + 1, 1)],
         [(V0, 0)], [(V0, 1)], [(V0 + 1, 0)], [(V0 + 1, 1)],
         [(K23, 0), (K23, 1)], [(K23 + 1, 0), (K23 + 1, 1)]]


def load_and_project_queries(nc, A, S):
    nkt = A["mask"].shape[-1] // P
    with ExitStack() as ctx:
        def sb(name, shape, dt=F32):
            return ctx.enter_context(nc.sbuf_tensor(name, shape, dt))

        def sem(name):
            return ctx.enter_context(nc.semaphore(name))

        wq = sb("wq", [P, DB, D])
        wk = sb("wk", [P, DB, D])
        wv = sb("wv", [P, DB, D])
        stats = sb("ln_stats", [P, QT, 6])
        mv = sb("ln_mv", [P, QT, 2])
        veps = sb("ln_veps", [P, QT])
        std = sb("ln_std", [P, QT])
        rstd = sb("ln_rstd", [P, QT])
        xn = sb("xn", [P, QT, D])
        xnT = sb("xnT", [P, DB, NQ])
        bq = sb("bq", [P, NG])
        q_f = sb("q_f", [P, NG, NQ])
        q_hi = sb("q_hi", [P, NG, NQ], F32R)
        q_lo = sb("q_lo", [P, NG, NQ], F32R)
        mask_u8 = sb("mask_u8", [P, nkt], U8)
        mask_f = sb("mask_f", [P, nkt])
        mask_r = sb("mask_r", [P, nkt], F32R)
        mask_min = sb("mask_min", [P, 1])
        all_masked = sb("all_masked", [P, 1])
        ones = sb("ones", [P, P])
        tp = [ctx.enter_context(nc.psum_tensor(f"xnT_ps{i}", [P, 512], F32)) for i in range(2)]
        qp = [ctx.enter_context(nc.psum_tensor(f"q_ps{i}", [P, NQ], F32)) for i in range(2)]
        cp = ctx.enter_context(nc.psum_tensor("count_ps", [P, 512], F32))

        x_ld, wq_ld, wk_ld, wv_ld = sem("x_ld"), sem("wq_ld"), sem("wk_ld"), sem("wv_ld")
        mask_ld, const_ld = sem("mask_ld"), sem("const_ld")
        zeroed, consts = sem("zeroed"), sem("consts")
        chain = sem("prep_chain")
        var_ready, std_ready = sem("var_ready"), sem("std_ready")
        xn_ready, xnT_full, xnT_ready = sem("xn_ready"), sem("xnT_full"), sem("xnT_ready")
        q_full, q_free, q_split = sem("q_full"), sem("q_free"), sem("q_split")
        w_hi = sem("w_hi")
        min_ready, count_ready, mask_ready = sem("min_ready"), sem("count_ready"), sem("mask_ready")
        stored = sem("prep_stored")
        ones_row = sem("ones_row")
        block = ctx.enter_context(nc.Block())

        @block.sync
        def _(sp):
            sp.dma_start(S["x"][:], A["x"].rearrange("(t p) d -> p t d", p=P)).then_inc(x_ld, 16)
            sp.dma_start(wq[:], A["xWq"].rearrange("(j p) n -> p j n", p=P)).then_inc(wq_ld, 16)
            sp.dma_start(bq[:], A["xbq"].rearrange("(g p) -> p g", p=P),
                         allow_slow_non_contiguous=True).then_inc(const_ld, 16)
            sp.dma_start(S["bk"][:], A["xbk"].rearrange("(g p) -> p g", p=P),
                         allow_slow_non_contiguous=True).then_inc(const_ld, 16)
            sp.dma_start(mask_u8[:], A["mask"].rearrange("(p t) -> p t", p=P)).then_inc(mask_ld, 16)
            sp.dma_start(wk[:], A["xWk"].rearrange("(j p) n -> p j n", p=P)).then_inc(wk_ld, 16)
            sp.dma_start(wv[:], A["xWv"].rearrange("(j p) n -> p j n", p=P)).then_inc(wv_ld, 16)
            sp.wait_ge(mask_ready, 1)
            sp.dma_start(S["mask_row"].rearrange("(p t) -> p t", p=P), mask_r[:].bitcast(F32)).then_inc(stored, 16)
            for g in range(NG):
                sp.wait_ge(q_split, g + 1)
                for i in range(HG):
                    rows = slice(HD * i, HD * (i + 1))
                    for r, part in enumerate((q_hi, q_hi, q_lo)):
                        sp.dma_start(S["q_stack"][HD * r:HD * (r + 1), HG * g + i, :].bitcast(F32),
                                     part[rows, g, :].bitcast(F32)).then_inc(stored, 16)
            sp.wait_ge(stored, 16 + 16 * NG * HG * 3)

        @block.gpsimd
        def _(pool):
            pool.memset(S["ident"][:], 0.0).then_inc(zeroed, 1)
            pool.wait_ge(zeroed, 1)
            pool.affine_select(out=S["ident"][:], in_=S["ident"][:], compare_op=ALU.not_equal, fill=1.0,
                               base=0, pattern=[[-1, P]], channel_multiplier=1).then_inc(consts, 1)
            pool.memset(ones[:], 1.0).then_inc(consts, 1)

        @block.scalar
        def _(act):
            act.wait_ge(var_ready, 1)
            nc.scalar.activation(std[:], veps[:], ACT.Sqrt).then_inc(std_ready, 1)
            act.wait_ge(wk_ld, 16)
            nc.scalar.activation(S["wk_hi"][:], wk[:], ACT.Copy).then_inc(w_hi, 1)
            act.wait_ge(wv_ld, 16)
            nc.scalar.activation(S["wv_hi"][:], wv[:], ACT.Copy).then_inc(w_hi, 1)

        @block.vector
        def _(dve):
            n = [0]

            def link(ins):
                n[0] += 1
                ins.then_inc(chain, 1)
                dve.wait_ge(chain, n[0])

            dve.wait_ge(x_ld, 16)
            for t in range(QT):
                link(dve.bn_stats(stats[:, t, :], S["x"][:, t, :]))
                link(dve.bn_aggr(mv[:, t, :], stats[:, t, :]))
            dve.tensor_scalar(veps[:], mv[:, :, 1], LN_EPS, None, ALU.add).then_inc(var_ready, 1)
            dve.wait_ge(std_ready, 1)
            link(dve.reciprocal(rstd[:], std[:]))
            for t in range(QT):
                dve.tensor_scalar(xn[:, t, :], S["x"][:, t, :], mv[:, t, 0:1], rstd[:, t:t + 1],
                                  ALU.subtract, ALU.mult).then_inc(xn_ready, 1)
            dve.wait_ge(mask_ld, 16)
            link(dve.tensor_copy(mask_f[:], mask_u8[:]))
            dve.tensor_reduce(mask_min[:], mask_f[:], AX_X, ALU.min).then_inc(min_ready, 1)
            for h in range(2):
                dve.wait_ge(xnT_full, h + 1)
                dve.tensor_copy(xnT[:, 2 * h:2 * h + 2, :], tp[h][:].rearrange("p (j q) -> p j q", j=2)
                                ).then_inc(xnT_ready, 1)
            link(dve.memset(S["q_stack"][3 * HD:3 * HD + 1, :, :].bitcast(F32), 1.0))
            link(dve.memset(S["m_old"][:], NO_MAX))
            link(dve.memset(S["l"][:], 0.0))
            link(dve.memset(S["o"][:], 0.0))
            dve.wait_ge(count_ready, 1)
            link(dve.tensor_scalar(all_masked[:], cp[:, 0:1], P - 0.5, None, ALU.is_ge))
            link(dve.tensor_tensor(mask_f[0:1, 0:1], mask_f[0:1, 0:1], all_masked[0:1, :], ALU.subtract))
            dve.tensor_scalar(mask_r[:], mask_f[:], MASKED, None, ALU.mult).then_inc(mask_ready, 1)
            dve.wait_ge(const_ld, 32)
            for g in range(NG):
                dve.wait_ge(q_full, g + 1)
                ins = dve.tensor_scalar(q_f[:, g, :], qp[g % 2][:], bq[:, g:g + 1], SCALE, ALU.add, ALU.mult)
                ins.then_inc(q_free, 1)
                dve.wait_ge(q_free, g + 1)
                link(dve.tensor_copy(q_hi[:, g, :], q_f[:, g, :]))
                dve.tensor_tensor(q_lo[:, g, :], q_f[:, g, :], q_hi[:, g, :].bitcast(F32),
                                  ALU.subtract).then_inc(q_split, 1)
            for i, (w, hi, lo) in enumerate(((wk, "wk_hi", "wk_lo"), (wv, "wv_hi", "wv_lo"))):
                dve.wait_ge(w_hi, i + 1)
                link(dve.tensor_tensor(S[lo][:], w[:], S[hi][:].bitcast(F32), ALU.subtract))

        @block.tensor
        def _(pe):
            pe.wait_ge(consts, 2)
            pe.wait_ge(xn_ready, QT)
            for h in range(2):
                for j in (2 * h, 2 * h + 1):
                    for t in range(QT):
                        at = (j % 2) * NQ + t * P
                        last = pe.transpose(tp[h][:, at:at + P], xn[:, t, j * P:(j + 1) * P], S["ident"][:])
                last.then_inc(xnT_full, 1)
            pe.wait_ge(min_ready, 1)
            pe.matmul(cp[:, 0:1], ones[:], mask_min[:], start=True, stop=True).then_inc(count_ready, 1)
            pe.wait_ge(xnT_ready, 2)
            pe.wait_ge(wq_ld, 16)
            for g in range(NG):
                if g >= 2:
                    pe.wait_ge(q_free, g - 1)
                for j in range(DB):
                    last = pe.matmul(qp[g % 2][:], wq[:, j, g * P:(g + 1) * P], xnT[:, j, :],
                                     start=(j == 0), stop=(j == DB - 1))
                last.then_inc(q_full, 1)


def cross_attention(nc, A, S):
    n_keys = A["ctx"].shape[0]
    NC = n_keys // KC
    assert n_keys % KC == 0 and NC >= 4
    with ExitStack() as ctx:
        def sb(name, shape, dt=F32):
            return ctx.enter_context(nc.sbuf_tensor(name, shape, dt))

        def bank(name):
            return ctx.enter_context(nc.psum_tensor(name, [P, 512], F32))

        def sem(name):
            return ctx.enter_context(nc.semaphore(name))

        k_stack = sb("k_stack", [P, H, KC], F32R)
        v = sb("v", [P, KB, H, 2, HD], F32R)
        ctx_sb = sb("ctx_sb", [P, KB, D])
        ctxT_hi = sb("ctxT_hi", [P, DB, KC], F32R)
        ctxT_lo = sb("ctxT_lo", [P, DB, KC], F32R)
        k_hi = sb("k_hi", [P, 2, KC], F32R)
        k_lo = sb("k_lo", [P, 2, KC], F32R)
        logits = sb("logits", [P, RING, QT, KC])
        pT_hi = sb("pT_hi", [P, 2, 2, 2 * NQ], F32R)
        pT_lo = sb("pT_lo", [P, 2, 2, 2 * NQ], F32R)
        oT = sb("oT", [P, 2, NQ])
        o_new = sb("o_new", [P, 2, QT * 2, HD])
        m_new = sb("m_new", [P, H, QT])
        m_neg = sb("m_neg", [P, H, QT])
        m_diff = sb("m_diff", [P, H, QT])
        alpha = sb("alpha", [P, H, QT])
        row_sum = sb("row_sum", [P, H, QT])
        one = sb("one", [P, QT])
        m_old, l, o = S["m_old"], S["l"], S["o"]

        s_ps = [bank(f"s_ps{t}") for t in range(QT)]
        pT_ps = [bank(f"pT_ps{b}") for b in range(2)]
        proj_ps = [bank(f"proj_ps{b}") for b in range(2)]
        oT_ps = bank("oT_ps")
        o_ps = bank("o_ps")

        bias_ld = [sem(f"bias_ld{r}") for r in range(RING)]
        ctx_ld = sem("ctx_ld")
        k_ld = [sem(f"k_ld{g}") for g in range(NG)]
        s_full = sem("s_full")
        t_done = sem("t_done")
        m_ready = sem("m_ready")
        one_set = sem("one_set")
        m_saved = sem("m_saved")
        p_done = sem("p_done")
        a_done = sem("a_done")
        l_scaled = sem("l_scaled")
        o_scaled = sem("o_scaled")
        l_done = sem("l_done")
        tr_done = sem("tr_done")
        hi_done = sem("hi_done")
        lo_done = sem("lo_done")
        pv_done = sem("pv_done")
        oT_done = sem("oT_done")
        ox_done = sem("ox_done")
        fold_done = sem("fold_done")
        o_done = sem("o_done")
        proj_full = sem("proj_full")
        proj_hi = sem("proj_hi")
        proj_lo = sem("proj_lo")

        block = ctx.enter_context(nc.Block())

        def group_of(i):
            return {tile: g for g, tile in K_TILE.items()}[i]

        def tiles(c, i):
            return TILES * (c + 1) + i - 1

        def wait(eng, s, value):
            if not isinstance(value, int) or value > 0:
                eng.wait_ge(s, value)

        def over_chunks(eng, steps):
            steps(0, False)
            with eng.Fori(1, NC - 1) as c:
                steps(c, False)
            steps(NC - 1, True)

        @block.sync
        def _(sp):
            def load_bias(c, h):
                n = H * c + h
                wait(sp, tr_done, 2 * (n - RING + 1))
                src = A["bias"][h, :, bass.ds(c * KC, KC)].rearrange("(t p) k -> p t k", p=P)
                sp.dma_start(logits[:, h % RING, :, :], src).then_inc(bias_ld[h % RING], 16)

            def load_ctx(c):
                sp.dma_start(ctx_sb[:], A["ctx"][bass.ds(c * KC, KC), :].rearrange("(b p) d -> p b d", p=P)
                             ).then_inc(ctx_ld, 16)

            def stack_keys(c, g):
                sp.wait_ge(proj_lo, tiles(c, K_TILE[g]))
                wait(sp, s_full, QT * (H * c + HG * (g + 1)))
                heads = slice(HG * g, HG * (g + 1))
                for i in range(HG):
                    rows = slice(HD * i, HD * (i + 1))
                    for r, part in enumerate((k_hi, k_lo, k_hi)):
                        sp.dma_start(k_stack[HD * r:HD * (r + 1), HG * g + i, :].bitcast(F32),
                                     part[rows, g % 2, :].bitcast(F32)).then_inc(k_ld[g], 16)
                row = S["mask_row"][bass.ds((c + 1) * KC, KC)].rearrange("(a b k) -> a b k", a=1, b=1)
                sp.dma_start(k_stack[3 * HD:3 * HD + 1, heads, :].bitcast(F32),
                             row.to_broadcast([1, HG, KC])).then_inc(k_ld[g], 16)

            load_ctx(0)
            for n in range(AHEAD):
                load_bias(0, n)
            sp.wait_ge(proj_full, tiles(-1, CT + DB - 1))
            load_ctx(1)
            for g in range(NG):
                stack_keys(-1, g)

            def steps(c, last):
                for h in range(H):
                    if h + AHEAD < H:
                        load_bias(c, h + AHEAD)
                    elif not last:
                        load_bias(c + 1, h + AHEAD - H)
                    if last:
                        continue
                    if h == 6 and not (isinstance(c, int) and c == NC - 2):
                        sp.wait_ge(proj_full, tiles(c, CT + DB - 1))
                        load_ctx(c + 2)
                    if h == 8:
                        stack_keys(c, 0)
                    if h == 10:
                        stack_keys(c, 1)
                    if h == 15:
                        stack_keys(c, 2)
                        stack_keys(c, 3)

            steps(0, False)
            with sp.Fori(1, NC - 2) as c:
                steps(c, False)
            steps(NC - 2, False)
            steps(NC - 1, True)

        @block.tensor
        def _(pe):
            def transpose(c, h, b):
                n = H * c + h
                if b == 0:
                    pe.wait_ge(p_done, QT * (n + 1))
                wait(pe, lo_done, 2 * (n - 1) + b + 1)
                for k in range(2):
                    for t in range(QT):
                        at = k * NQ + t * P
                        last = pe.transpose(pT_ps[b][:, at:at + P],
                                            logits[:, h % RING, t, bass.ts(2 * b + k, P)], S["ident"][:])
                last.then_inc(tr_done, 1)

            def scores(c, h):
                n = H * c + h
                if h % HG == 0:
                    pe.wait_ge(k_ld[h // HG], 16 * KDMA * (c + 1))
                for t in range(QT):
                    wait(pe, t_done, QT * (n - 1) + t + 1)
                    pe.matmul(s_ps[t][:], S["q_stack"][0:3 * HD + 1, h, bass.ts(t, P)],
                              k_stack[0:3 * HD + 1, h, :], start=True, stop=True).then_inc(s_full, 1)

            def weighted_values(c, h):
                n = H * c + h
                pe.wait_ge(lo_done, 2 * (n + 1))
                wait(pe, oT_done, n)
                if h == 0:
                    pe.wait_ge(proj_lo, tiles(c - 1, V0 + 1))
                if h == H // 2:
                    pe.wait_ge(proj_lo, tiles(c, V1 + 1))
                for kb in range(KB):
                    for i, part in enumerate((pT_hi, pT_lo)):
                        last = pe.matmul(oT_ps[0:2 * HD, 0:NQ],
                                         v[:, kb, h, :, :].rearrange("p a d -> p (a d)"),
                                         part[:, h % 2, kb // 2, (kb % 2) * NQ:(kb % 2 + 1) * NQ],
                                         start=(kb == 0 and i == 0), stop=(kb == KB - 1 and i == 1))
                last.then_inc(pv_done, 1)

            def turn_output(c, h):
                pair = H // 2 * c + h // 2
                pe.wait_ge(oT_done, H * c + h + 1)
                wait(pe, fold_done, pair)
                for t in range(QT):
                    last = pe.transpose(o_ps[:, bass.ts(t, P)], oT[:, h // 2 % 2, bass.ts(t, P)], S["ident"][:])
                last.then_inc(ox_done, 1)

            def free_bank(c, i):
                wait(pe, proj_lo, tiles(c, i) - 2)

            def context_tile(c, j):
                i = CT + j
                free_bank(c, i)
                if j == 0:
                    pe.wait_ge(ctx_ld, 16 * (c + 2))
                for b in range(KB):
                    last = pe.transpose(proj_ps[i % 2][:, bass.ts(b, P)], ctx_sb[:, b, bass.ts(j, P)],
                                        S["ident"][:])
                last.then_inc(proj_full, 1)

            def key_tile(c, g, part):
                i = K_TILE[g]
                if part == 0:
                    free_bank(c, i)
                    if g == 0:
                        pe.wait_ge(proj_lo, tiles(c, CT + DB - 1))
                for j in (0, 1) if part == 0 else (2, 3):
                    for s, (w, x) in enumerate((("wk_hi", ctxT_hi), ("wk_hi", ctxT_lo), ("wk_lo", ctxT_hi))):
                        last = pe.matmul(proj_ps[i % 2][:], S[w][:, j, bass.ts(g, P)], x[:, j, :],
                                         start=(j == 0 and s == 0), stop=(j == DB - 1 and s == 2))
                if part == 1:
                    last.then_inc(proj_full, 1)

            def value_tile(c, i, half, part):
                if part == 0:
                    free_bank(c, i)
                b = 2 * (i % 2) + part
                cols = slice(half * D // 2, (half + 1) * D // 2)
                for j in range(DB):
                    for s, (x, w) in enumerate(((ctxT_hi, "wv_hi"), (ctxT_hi, "wv_lo"), (ctxT_lo, "wv_hi"))):
                        last = pe.matmul(proj_ps[i % 2][:, part * 256:(part + 1) * 256], x[:, j, bass.ts(b, P)],
                                         S[w][:, j, cols], start=(j == 0 and s == 0),
                                         stop=(j == DB - 1 and s == 2))
                if part == 1:
                    last.then_inc(proj_full, 1)

            for j in range(DB):
                context_tile(-1, j)
            for g in (0, 1):
                key_tile(-1, g, 0), key_tile(-1, g, 1)
            for i in (0, 1):
                value_tile(-1, V0 + i, 0, 0), value_tile(-1, V0 + i, 0, 1)
            for g in (2, 3):
                key_tile(-1, g, 0), key_tile(-1, g, 1)
            scores(0, 0)
            scores(0, 1)

            def project(c, h):
                for i, half in SHARE[h]:
                    if CT <= i < CT + DB:
                        context_tile(c, i - CT)
                    elif i in K_TILE.values():
                        key_tile(c, group_of(i), half)
                    else:
                        value_tile(c, i, 1 if i < CT else 0, half)

            def steps(c, last):
                for h in range(H):
                    transpose(c, h, 0)
                    if h + 2 < H:
                        scores(c, h + 2)
                    elif not last:
                        scores(c + 1, h + 2 - H)
                    transpose(c, h, 1)
                    if not last or SHARE[h][0][0] < CT:
                        project(c, h)
                    if h >= 1:
                        weighted_values(c, h - 1)
                    elif not (isinstance(c, int) and c == 0):
                        weighted_values(c - 1, H - 1)
                    if h >= 3 and h % 2:
                        turn_output(c, h - 2)
                    elif h == 1 and not (isinstance(c, int) and c == 0):
                        turn_output(c - 1, H - 1)

            over_chunks(pe, steps)
            weighted_values(NC - 1, H - 1)
            turn_output(NC - 1, H - 1)

        def finished_tiles(h):
            return [i for i, half in SHARE[h] if half == 1]

        def value_out(i, half, part):
            b = 2 * (i % 2)
            return v[:, b:b + 2, half * H // 2:(half + 1) * H // 2, part, :]

        @block.scalar
        def _(act):
            def split_hi(c, h, b):
                n = H * c + h
                act.wait_ge(tr_done, 2 * n + b + 1)
                wait(act, pv_done, n - 1)
                nc.scalar.activation(pT_hi[:, h % 2, b, :], pT_ps[b][:], ACT.Copy).then_inc(hi_done, 1)

            def exponentials(c, h, t):
                n = H * c + h
                if t == 0:
                    act.wait_ge(m_ready, 2 * (n + 1))
                    wait(act, l_done, n - H + 1)
                at = logits[:, h % RING, t, :]
                nc.scalar.activation(at, at, ACT.Exp, bias=m_neg[:, h, t:t + 1],
                                     accum_out=row_sum[:, h, t:t + 1]).then_inc(p_done, 1)

            def rescaling(c, h):
                wait(act, o_done, H // 2 * (c - 1) + h // 2 + 1)
                nc.scalar.activation(alpha[:, h, :], m_diff[:, h, :], ACT.Exp).then_inc(a_done, 1)

            def copy_output(c, h):
                n = H * c + h
                act.wait_ge(pv_done, n + 1)
                wait(act, ox_done, H // 2 * c + h // 2 - 1)
                rows = slice(2 * HD * (h % 2), 2 * HD * (h % 2 + 1))
                nc.scalar.activation(oT[rows, h // 2 % 2, :], oT_ps[0:2 * HD, 0:NQ], ACT.Copy).then_inc(oT_done, 1)

            def tile_hi(c, i):
                act.wait_ge(proj_full, tiles(c, i))
                src = proj_ps[i % 2]
                if CT <= i < CT + DB:
                    ins = nc.scalar.activation(ctxT_hi[:, i - CT, :], src[:], ACT.Copy)
                elif i in (V1, V1 + 1, V0, V0 + 1):
                    half = 1 if i < CT else 0
                    wait(act, pv_done, H * c if half else H * c + H // 2)
                    ins = nc.scalar.activation(value_out(i, half, 0),
                                               src[:].rearrange("p (b h d) -> p b h d", b=2, d=HD), ACT.Copy)
                else:
                    g = group_of(i)
                    if g >= 2:
                        act.wait_ge(k_ld[g - 2], 16 * KDMA * (c + 2))
                    else:
                        wait(act, k_ld[g + 2], 16 * KDMA * (c + 1))
                    ins = nc.scalar.activation(k_hi[:, g % 2, :], src[:], ACT.Identity, bias=S["bk"][:, g:g + 1])
                ins.then_inc(proj_hi, 1)

            for i in range(CT, TILES):
                tile_hi(-1, i)
            for t in range(QT):
                exponentials(0, 0, t)
            rescaling(0, 0)

            def steps(c, last):
                for h in range(H):
                    ahead = (c, h + 1) if h + 1 < H else (c + 1, 0)
                    more = h + 1 < H or not last
                    split_hi(c, h, 0)
                    if more:
                        exponentials(*ahead, 0)
                    split_hi(c, h, 1)
                    if more:
                        exponentials(*ahead, 1)
                        rescaling(*ahead)
                    for i in finished_tiles(h):
                        if not last or i < CT:
                            tile_hi(c, i)
                    if h >= 1:
                        copy_output(c, h - 1)
                    elif not (isinstance(c, int) and c == 0):
                        copy_output(c - 1, H - 1)

            over_chunks(act, steps)
            copy_output(NC - 1, H - 1)

        @block.vector
        def _(dve):
            def split_lo(c, h, b):
                dve.wait_ge(hi_done, 2 * (H * c + h) + b + 1)
                dve.tensor_tensor(pT_lo[:, h % 2, b, :], pT_ps[b][:],
                                  pT_hi[:, h % 2, b, :].bitcast(F32), ALU.subtract).then_inc(lo_done, 1)

            def await_logits(c, h, t):
                n = H * c + h
                if t == 0:
                    use = (H // RING) * c + h // RING + 1
                    dve.wait_ge(bias_ld[h % RING], 16 * use)
                    wait(dve, m_saved, n - H + 1)
                dve.wait_ge(s_full, QT * n + t + 1)

            def logits_and_max(c, h, t):
                at = logits[:, h % RING, t, :]
                dve.tensor_tensor_reduce(at, s_ps[t][:], at, 1.0, m_old[:, h, t:t + 1], ALU.add, ALU.max,
                                         m_new[:, h, t:t + 1]).then_inc(t_done, 1)

            def fold_output(c, h):
                pair = H // 2 * c + h // 2
                dve.wait_ge(ox_done, pair + 1)
                wait(dve, o_done, pair - 1)
                dve.tensor_reduce(o_new[:, h // 2 % 2, :, :],
                                  o_ps[:, 0:QT * P].rearrange("p (b a d) -> p b d a", a=2, d=HD),
                                  AX_X, ALU.add).then_inc(fold_done, 1)

            def tile_lo(c, i):
                dve.wait_ge(proj_hi, tiles(c, i))
                src = proj_ps[i % 2]
                if CT <= i < CT + DB:
                    ins = dve.tensor_tensor(ctxT_lo[:, i - CT, :], src[:],
                                            ctxT_hi[:, i - CT, :].bitcast(F32), ALU.subtract)
                elif i in (V1, V1 + 1, V0, V0 + 1):
                    half = 1 if i < CT else 0
                    ins = dve.tensor_tensor(value_out(i, half, 1),
                                            src[:].rearrange("p (b h d) -> p b h d", b=2, d=HD),
                                            value_out(i, half, 0).bitcast(F32), ALU.subtract)
                else:
                    g = group_of(i)
                    ins = dve.scalar_tensor_tensor(out=k_lo[:, g % 2, :], in0=src[:], scalar=S["bk"][:, g:g + 1],
                                                   in1=k_hi[:, g % 2, :].bitcast(F32), op0=ALU.add,
                                                   op1=ALU.subtract)
                ins.then_inc(proj_lo, 1)

            for i in range(CT, TILES):
                tile_lo(-1, i)
            for h in range(2):
                for t in range(QT):
                    await_logits(0, h, t)
                    logits_and_max(0, h, t)

            def steps(c, last):
                for h in range(H):
                    ahead = (c, h + 2) if h + 2 < H else (c + 1, h + 2 - H)
                    more = h + 2 < H or not last
                    for t in range(QT):
                        if more:
                            await_logits(*ahead, t)
                        split_lo(c, h, t)
                        if more:
                            logits_and_max(*ahead, t)
                    for i in finished_tiles(h):
                        if not last or i < CT:
                            tile_lo(c, i)
                    if h >= 3 and h % 2:
                        fold_output(c, h - 2)
                    elif h == 1 and not (isinstance(c, int) and c == 0):
                        fold_output(c - 1, H - 1)

            over_chunks(dve, steps)
            fold_output(NC - 1, H - 1)

        @block.gpsimd
        def _(pool):
            def maxima(c, h):
                n = H * c + h
                pool.wait_ge(t_done, QT * (n + 1))
                wait(pool, p_done, QT * (n - H + 1))
                wait(pool, a_done, n - H + 1)
                pool.tensor_tensor(m_diff[:, h, :], m_old[:, h, :], m_new[:, h, :],
                                   ALU.subtract).then_inc(m_ready, 1)
                pool.tensor_scalar(m_neg[:, h, :], m_new[:, h, :], -1.0, None, ALU.mult).then_inc(m_ready, 1)
                pool.wait_ge(m_ready, 2 * (n + 1))
                pool.tensor_tensor(m_old[:, h, :], m_new[:, h, :], one[:], ALU.mult).then_inc(m_saved, 1)

            def rescale(c, h):
                n = H * c + h
                pool.wait_ge(a_done, n + 1)
                wait(pool, l_done, n - H + 1)
                pool.tensor_tensor(l[:, h, :], l[:, h, :], alpha[:, h, :], ALU.mult).then_inc(l_scaled, 1)
                pool.wait_ge(p_done, QT * (n + 1))
                pool.wait_ge(l_scaled, n + 1)
                pool.tensor_tensor(l[:, h, :], l[:, h, :], row_sum[:, h, :], ALU.add).then_inc(l_done, 1)

            def update_output(c, h):
                pair = H // 2 * c + h // 2
                heads = slice(h - 1, h + 1)
                factors = alpha[:, heads, :].rearrange("p h (t a) -> p t h a", a=1).to_broadcast([P, QT, 2, HD])
                wait(pool, o_done, H // 2 * (c - 1) + h // 2 + 1)
                pool.tensor_tensor(o[:, :, heads, :], o[:, :, heads, :], factors, ALU.mult).then_inc(o_scaled, 1)
                pool.wait_ge(fold_done, pair + 1)
                pool.wait_ge(o_scaled, pair + 1)
                pool.tensor_tensor(o[:, :, heads, :], o[:, :, heads, :],
                                   o_new[:, h // 2 % 2, :, :].rearrange("p (t h) d -> p t h d", t=QT),
                                   ALU.add).then_inc(o_done, 1)

            pool.memset(one[:], 1.0).then_inc(one_set, 1)
            pool.wait_ge(one_set, 1)
            maxima(0, 0)
            rescale(0, 0)
            maxima(0, 1)

            def steps(c, last):
                for h in range(H):
                    if h + 1 < H:
                        rescale(c, h + 1)
                    elif not last:
                        rescale(c + 1, 0)
                    if h + 2 < H:
                        maxima(c, h + 2)
                    elif not last:
                        maxima(c + 1, h + 2 - H)
                    if h >= 3 and h % 2:
                        update_output(c, h - 2)
                    elif h == 1 and not (isinstance(c, int) and c == 0):
                        update_output(c - 1, H - 1)

            over_chunks(pool, steps)
            update_output(NC - 1, H - 1)


def attention_output(nc, A, S):
    with ExitStack() as ctx:
        def sb(name, shape, dt=F32):
            return ctx.enter_context(nc.sbuf_tensor(name, shape, dt))

        def sem(name):
            return ctx.enter_context(nc.semaphore(name))

        wo = sb("wo", [P, DB, D])
        bv = sb("bv", [P, D])
        bo = sb("bo", [P, D])
        l_inv = sb("l_inv", [P, H, QT])
        a = sb("a", [P, QT, D])
        aT = sb("aT", [P, DB, NQ])
        aT_ps = [ctx.enter_context(nc.psum_tensor(f"aT_ps{i}", [P, 512], F32)) for i in range(2)]
        y_ps = [ctx.enter_context(nc.psum_tensor(f"y_ps{i}", [P, 512], F32)) for i in range(QT)]
        w_ld, b_ld = sem("wo_ld"), sem("bo_ld")
        chain = sem("out_chain")
        a_ready, aT_full, aT_ready, y_full = sem("a_ready"), sem("aT_full"), sem("aT_ready"), sem("y_full")
        block = ctx.enter_context(nc.Block())

        @block.sync
        def _(sp):
            sp.dma_start(wo[:], A["xWo"].rearrange("(j p) n -> p j n", p=P)).then_inc(w_ld, 16)
            for dst, src in ((bv, "xbv"), (bo, "xbo")):
                sp.dma_start(dst[:], A[src].rearrange("(a d) -> a d", a=1).to_broadcast([P, D])).then_inc(b_ld, 16)

        @block.vector
        def _(dve):
            n = [0]

            def link(ins):
                n[0] += 1
                ins.then_inc(chain, 1)
                dve.wait_ge(chain, n[0])

            link(dve.reciprocal(l_inv[:], S["l"][:]))
            dve.wait_ge(b_ld, 32)
            for t in range(QT):
                link(dve.tensor_tensor(a[:, t, :].rearrange("p (h d) -> p h d", h=H), S["o"][:, t, :, :],
                                       l_inv[:, :, t:t + 1].to_broadcast([P, H, HD]), ALU.mult))
                dve.tensor_tensor(a[:, t, :], a[:, t, :], bv[:], ALU.add).then_inc(a_ready, 1)
                link(dve.tensor_tensor(S["x"][:, t, :], S["x"][:, t, :], bo[:], ALU.add))
            for i in range(2):
                dve.wait_ge(aT_full, i + 1)
                dve.tensor_copy(aT[:, 2 * i:2 * i + 2, :], aT_ps[i][:].rearrange("p (j q) -> p j q", j=2)
                                ).then_inc(aT_ready, 1)
            for t in range(QT):
                dve.wait_ge(y_full, t + 1)
                link(dve.tensor_tensor(S["x"][:, t, :], S["x"][:, t, :], y_ps[t][:], ALU.add))

        @block.tensor
        def _(pe):
            pe.wait_ge(a_ready, QT)
            for i in range(2):
                for j in (2 * i, 2 * i + 1):
                    for t in range(QT):
                        at = (j % 2) * NQ + t * P
                        last = pe.transpose(aT_ps[i][:, at:at + P], a[:, t, bass.ts(j, P)], S["ident"][:])
                last.then_inc(aT_full, 1)
            pe.wait_ge(w_ld, 16)
            pe.wait_ge(aT_ready, 2)
            for t in range(QT):
                for j in range(DB):
                    last = pe.matmul(y_ps[t][:], aT[:, j, bass.ts(t, P)], wo[:, j, :],
                                     start=(j == 0), stop=(j == DB - 1))
                last.then_inc(y_full, 1)


class Banks:

    def __init__(self, nc, ctx, name, count, order, looped=False):
        self.bank = [ctx.enter_context(nc.psum_tensor(f"{name}{b}", [P, 512], F32)) for b in range(count)]
        self.full = [ctx.enter_context(nc.semaphore(f"{name}_full{b}")) for b in range(count)]
        self.free = [ctx.enter_context(nc.semaphore(f"{name}_free{b}")) for b in range(count)]
        self.at = {key: (i % count, i // count) for i, key in enumerate(order)}
        assert len(self.at) == len(order)
        self.rounds = len(order) // count
        self.credit = self.rounds if looped else 0

    def __getitem__(self, key):
        return self.bank[self.at[key][0]]

    def give_credit(self, eng):
        for s in self.full + self.free:
            eng.sem_inc(s, self.credit)

    def wait_free(self, pe, key, j=0):
        b, use = self.at[key]
        value = use + self.rounds * j + self.credit
        if not isinstance(value, int) or value > 0:
            pe.wait_ge(self.free[b], value)

    def wait_full(self, eng, key, j=0):
        b, use = self.at[key]
        eng.wait_ge(self.full[b], use + 1 + self.rounds * j + self.credit)

    def wait_full_before(self, eng, key, j):
        b, use = self.at[key]
        eng.wait_ge(self.full[b], use + 1 + self.rounds * j)

    def wait_read(self, eng, key, j=0):
        b, use = self.at[key]
        eng.wait_ge(self.free[b], use + 1 + self.rounds * j + self.credit)

    def is_full(self, ins, key):
        ins.then_inc(self.full[self.at[key][0]], 1)

    def is_free(self, ins, key):
        ins.then_inc(self.free[self.at[key][0]], 1)


def self_attention(nc, A, S):
    DH = 64
    W = H * DH
    WB = W // P
    EPS = 1e-8
    with ExitStack() as ctx:
        def sb(name, shape, dt=F32):
            return ctx.enter_context(nc.sbuf_tensor(name, shape, dt))

        def sem(name):
            return ctx.enter_context(nc.semaphore(name))

        wq = sb("awq", [P, DB, W])
        wkv = sb("awkv", [P, DB, 2 * W])
        wo = sb("awo", [P, WB, D])
        bo = sb("abo", [P, D])
        stats = sb("a_stats", [P, QT, 6])
        mv = sb("a_mv", [P, QT, 2])
        veps = sb("a_veps", [P, QT])
        std = sb("a_std", [P, QT])
        rstd = sb("a_rstd", [P, QT])
        xn = sb("a_xn", [P, QT, D])
        xnT = sb("a_xnT", [P, DB, NQ])
        q_pad = sb("a_q", [P, H, NQ])
        kT = sb("a_kT", [P, WB, NQ])
        v = sb("a_v", [P, QT, W])
        causal = sb("causal", [P, QT, NQ])
        mx = sb("a_max", [P, H, QT])
        mneg = sb("a_mneg", [P, H, QT])
        e = sb("a_e", [P, 2, QT, NQ])
        p = sb("a_p", [P, 2, QT, NQ])
        den = sb("a_den", [P, H, QT])
        den_eps = sb("a_den_eps", [P, H, QT])
        rden = sb("a_rden", [P, H, QT])
        pT = sb("a_pT", [P, 2, 3 * P])
        a = sb("a_a", [P, QT, W])
        aT = sb("a_aT", [P, WB, NQ])

        order = [("xnT", i) for i in range(2)]
        order += [(k, i) for i in range(4) for k in ("q", "k")] + [("v", i) for i in range(4)]
        order += [("s", 0), ("s", 1)]
        for h in range(H):
            order += [("pT", h)] + ([("s", h + 2)] if h + 2 < H else []) + ([("o", h - 1)] if h else [])
        order += [("o", H - 1)] + [("aT", i) for i in range(4)] + [("y", t) for t in range(QT)]
        ps = Banks(nc, ctx, "a_ps", 8, order)

        w_ld, b_ld = [sem(f"aw_ld{i}") for i in range(3)], sem("abo_ld")
        chain = sem("a_chain")
        causal_set, q_zero = sem("causal_set"), sem("q_zero")
        var_ready, std_ready, xn_ready = sem("a_var_ready"), sem("a_std_ready"), sem("a_xn_ready")
        m_ready, p_ready = sem("a_m_ready"), sem("a_p_ready")
        block = ctx.enter_context(nc.Block())

        @block.sync
        def _(sp):
            sp.dma_start(wq[:], A["aWq"].rearrange("(j p) n -> p j n", p=P)).then_inc(w_ld[0], 16)
            sp.dma_start(wkv[:], A["aWkv"].rearrange("(j p) n -> p j n", p=P)).then_inc(w_ld[1], 16)
            sp.dma_start(wo[:], A["aWo"].rearrange("(j p) n -> p j n", p=P)).then_inc(w_ld[2], 16)
            sp.dma_start(bo[:], A["abo"].rearrange("(a d) -> a d", a=1).to_broadcast([P, D])).then_inc(b_ld, 16)

        @block.gpsimd
        def _(pool):
            pool.memset(q_pad[:], 0.0).then_inc(q_zero, 1)
            pool.memset(causal[:], 1.0).then_inc(causal_set, 1)
            pool.wait_ge(causal_set, 1)
            for t in range(QT):
                pool.affine_select(out=causal[:, t, :], in_=causal[:, t, :], compare_op=ALU.is_ge, fill=0.0,
                                   base=t * P, pattern=[[-1, NQ]], channel_multiplier=1).then_inc(causal_set, 1)

        def copy_pT(act, h):
            ps.wait_full(act, ("pT", h))
            if h >= 2:
                ps.wait_full(act, ("o", h - 2))
            ins = nc.scalar.activation(pT[:, h % 2, :], ps["pT", h][:, 0:3 * P], ACT.Copy)
            ps.is_free(ins, ("pT", h))

        @block.scalar
        def _(act):
            act.wait_ge(var_ready, 1)
            nc.scalar.activation(std[:], veps[:], ACT.Sqrt).then_inc(std_ready, 1)
            act.wait_ge(q_zero, 1)
            for i in range(4):
                ps.wait_full(act, ("q", i))
                src = ps["q", i][:].rearrange("p (b q) -> p b q", b=2)
                for r in range(2):
                    rows = slice(DH * r, DH * (r + 1))
                    ins = nc.scalar.activation(q_pad[rows, 4 * i + r:4 * i + r + 3:2, :], src[rows], ACT.Copy,
                                               scale=DH ** -0.5)
                ps.is_free(ins, ("q", i))
            for h in range(H):
                act.wait_ge(m_ready, h + 1)
                if h >= 2:
                    act.wait_ge(p_ready, QT * (h - 1))
                for t in range(QT):
                    ins = nc.scalar.activation(e[:, h % 2, t, :], ps["s", h][:, t * NQ:(t + 1) * NQ], ACT.Exp,
                                               bias=mneg[:, h, t:t + 1])
                ps.is_free(ins, ("s", h))
                if h:
                    copy_pT(act, h - 1)
            copy_pT(act, H - 1)

        @block.vector
        def _(dve):
            n = [0]

            def link(ins):
                n[0] += 1
                ins.then_inc(chain, 1)
                dve.wait_ge(chain, n[0])

            for t in range(QT):
                link(dve.bn_stats(stats[:, t, :], S["x"][:, t, :]))
                link(dve.bn_aggr(mv[:, t, :], stats[:, t, :]))
            dve.tensor_scalar(veps[:], mv[:, :, 1], LN_EPS, None, ALU.add).then_inc(var_ready, 1)
            dve.wait_ge(std_ready, 1)
            link(dve.reciprocal(rstd[:], std[:]))
            for t in range(QT):
                dve.tensor_scalar(xn[:, t, :], S["x"][:, t, :], mv[:, t, 0:1], rstd[:, t:t + 1],
                                  ALU.subtract, ALU.mult).then_inc(xn_ready, 1)
            dve.wait_ge(b_ld, 16)
            for t in range(QT):
                link(dve.tensor_tensor(S["x"][:, t, :], S["x"][:, t, :], bo[:], ALU.add))

            def take(key, dst, src):
                ps.wait_full(dve, key)
                ps.is_free(dve.tensor_copy(dst, src), key)

            for i in range(2):
                take(("xnT", i), xnT[:, 2 * i:2 * i + 2, :],
                     ps["xnT", i][:].rearrange("p (j q) -> p j q", j=2))
            for i in range(4):
                take(("k", i), kT[:, 2 * i:2 * i + 2, :], ps["k", i][:].rearrange("p (j q) -> p j q", j=2))
            for i in range(4):
                take(("v", i), v[:, i // 2, bass.ts(i % 2, D)], ps["v", i][:])

            def maximum(h):
                ps.wait_full(dve, ("s", h))
                link(dve.tensor_reduce(mx[:, h, :], ps["s", h][:].rearrange("p (t k) -> p t k", t=QT), AX_X, ALU.max))
                dve.tensor_scalar(mneg[:, h, :], mx[:, h, :], -1.0, None, ALU.mult).then_inc(m_ready, 1)

            def mask(h):
                ps.wait_read(dve, ("s", h))
                if h >= 2:
                    ps.wait_full(dve, ("pT", h - 2))
                for t in range(QT):
                    dve.tensor_tensor_reduce(p[:, h % 2, t, :], e[:, h % 2, t, :], causal[:, t, :], 1.0, 0.0,
                                             ALU.mult, ALU.add, den[:, h, t:t + 1]).then_inc(p_ready, 1)
                dve.wait_ge(p_ready, QT * (h + 1))
                link(dve.tensor_scalar(den_eps[:, h, :], den[:, h, :], EPS, None, ALU.add))
                link(dve.reciprocal(rden[:, h, :], den_eps[:, h, :]))

            def normalise(h):
                ps.wait_full(dve, ("o", h))
                for t in range(QT):
                    ins = dve.tensor_scalar(a[:, t, bass.ts(h, DH)], ps["o", h][:, bass.ts(t, DH)],
                                            rden[:, h, t:t + 1], None, ALU.mult)
                ps.is_free(ins, ("o", h))

            dve.wait_ge(causal_set, 1 + QT)
            maximum(0)
            for h in range(H):
                if h + 1 < H:
                    maximum(h + 1)
                mask(h)
                if h:
                    normalise(h - 1)
            normalise(H - 1)
            for i in range(4):
                take(("aT", i), aT[:, 2 * i:2 * i + 2, :], ps["aT", i][:].rearrange("p (j q) -> p j q", j=2))
            for t in range(QT):
                ps.wait_full(dve, ("y", t))
                link(dve.tensor_tensor(S["x"][:, t, :], S["x"][:, t, :], ps["y", t][:], ALU.add))

        @block.tensor
        def _(pe):
            def turn(key, src):
                ps.wait_free(pe, key)
                for j in range(2):
                    for t in range(QT):
                        at = j * NQ + t * P
                        last = pe.transpose(ps[key][:, at:at + P], src[:, t, bass.ts(2 * key[1] + j, P)],
                                            S["ident"][:])
                ps.is_full(last, key)

            pe.wait_ge(xn_ready, QT)
            for i in range(2):
                turn(("xnT", i), xn)
            ps.wait_read(pe, ("xnT", 0))
            ps.wait_read(pe, ("xnT", 1))
            pe.wait_ge(w_ld[0], 16)
            pe.wait_ge(w_ld[1], 16)
            for i in range(4):
                for k, w in (("q", wq), ("k", wkv)):
                    ps.wait_free(pe, (k, i))
                    for b in range(2):
                        for j in range(DB):
                            last = pe.matmul(ps[k, i][:, bass.ts(b, NQ)], w[:, j, bass.ts(2 * i + b, P)],
                                             xnT[:, j, :], start=(j == 0), stop=(j == DB - 1))
                    ps.is_full(last, (k, i))
            for i in range(4):
                ps.wait_free(pe, ("v", i))
                for j in range(DB):
                    last = pe.matmul(ps["v", i][:], xnT[:, j, bass.ts(i // 2, P)],
                                     wkv[:, j, W + (i % 2) * D:W + (i % 2 + 1) * D],
                                     start=(j == 0), stop=(j == DB - 1))
                ps.is_full(last, ("v", i))

            def scores(h):
                ps.wait_free(pe, ("s", h))
                if h % 4 == 0:
                    ps.wait_read(pe, ("q", h // 4))
                    ps.wait_read(pe, ("k", h // 4))
                for t in range(QT):
                    last = pe.matmul(ps["s", h][:, bass.ts(t, NQ)], q_pad[:, h, bass.ts(t, P)], kT[:, h // 2, :],
                                     start=True, stop=True)
                ps.is_full(last, ("s", h))

            def turn_probabilities(h):
                ps.wait_free(pe, ("pT", h))
                pe.wait_ge(p_ready, QT * (h + 1))
                for i, (t, b) in enumerate(((0, 0), (1, 0), (1, 1))):
                    last = pe.transpose(ps["pT", h][:, bass.ts(i, P)], p[:, h % 2, t, bass.ts(b, P)], S["ident"][:])
                ps.is_full(last, ("pT", h))

            def values(h):
                ps.wait_free(pe, ("o", h))
                ps.wait_read(pe, ("pT", h))
                if h == 0:
                    ps.wait_read(pe, ("v", 3))
                for t in range(QT):
                    for b in range(t + 1):
                        last = pe.matmul(ps["o", h][:, bass.ts(t, DH)], pT[:, h % 2, bass.ts(t + b, P)],
                                         v[:, b, bass.ts(h, DH)], start=(b == 0), stop=(b == t))
                ps.is_full(last, ("o", h))

            scores(0)
            scores(1)
            for h in range(H):
                turn_probabilities(h)
                if h + 2 < H:
                    scores(h + 2)
                if h:
                    values(h - 1)
            values(H - 1)
            ps.wait_read(pe, ("o", H - 1))
            for i in range(4):
                turn(("aT", i), a)
            pe.wait_ge(w_ld[2], 16)
            ps.wait_read(pe, ("aT", 3))
            for t in range(QT):
                ps.wait_free(pe, ("y", t))
                for j in range(WB):
                    last = pe.matmul(ps["y", t][:], aT[:, j, bass.ts(t, P)], wo[:, j, :],
                                     start=(j == 0), stop=(j == WB - 1))
                ps.is_full(last, ("y", t))


def moe(nc, A, S):
    LAYERS, E, _ = A["rb"].shape[0], A["rb"].shape[1], None
    RMS_EPS = 1e-6
    FAR = 1e30
    U = E + 2
    WR = 4
    WS = 3
    NB = 6
    BUP, BG, SBUP, SBG = 0, E * DB, 2 * E * DB, 2 * E * DB + 2 * DB
    NBIAS = SBG + DB
    assert D // P == DB and NBIAS <= P

    ops = []
    for i in range(U + 2):
        ops += [("up", i)] if i < U else []
        ops += [("down", i - 2)] if 0 <= i - 2 and i - 2 != U - 2 else []
        ops += [("g", i - 1)] if 0 <= i - 1 < U else []
    MIX_AT = 3
    order = [("xT", i) for i in range(2)] + [("gate", t) for t in range(QT)]
    for i, (kind, u) in enumerate(ops):
        if i == MIX_AT:
            order += [("wT", t) for t in range(QT)] + [("bd", t) for t in range(QT)]
        order += [(kind, u, t) for t in range(2)]
    def matrix(kind, u):
        if kind == "up":
            return ("up", u)
        return (kind, min(u, E))
    matrices, last_use = [], {}
    for kind, u in ops:
        m = matrix(kind, u)
        if m not in matrices:
            matrices.append(m)
        last_use[m] = (kind, u, 1)
    NM = len(matrices)

    def matrix_no(i):
        return matrices.index(matrix(*ops[i]))

    def new_matrix(i):
        return i < len(ops) and matrix_no(i) not in [matrix_no(k) for k in range(i)]

    assert len(order) % NB == 0

    def source(m):
        kind, u = m
        if kind == "up":
            w = A["eWup"][u] if u < E else A["sWup"][:, (u - E) * D:(u - E + 1) * D]
        elif kind == "g":
            w = A["eWg"][u] if u < E else A["sWg"]
        else:
            w = A["eWdown"][u] if u < E else A["sWdown"]
        return w.rearrange("(j p) n -> p j n", p=P)

    with ExitStack() as ctx:
        def sb(name, shape, dt=F32):
            return ctx.enter_context(nc.sbuf_tensor(name, shape, dt))

        def sem(name):
            return ctx.enter_context(nc.semaphore(name))

        w_sb = sb("m_w", [P, WR, DB, D])
        w_hi = sb("m_w_hi", [P, WS, DB, D], F32R)
        w_lo = sb("m_w_lo", [P, WS, DB, D], F32R)
        bias_rows = sb("bias_rows", [NBIAS, P])
        bias = sb("bias_cols", [P, NBIAS])
        bdown = sb("bdown", [E + 1, D])
        rw = sb("router_w", [P, LAYERS, DB, E])
        rb = sb("router_b", [P, LAYERS, E])
        gb = sb("gate_bias", [P, LAYERS, E])
        nw = sb("norm_w", [P, LAYERS, D])
        earlier = sb("earlier", [P, E, E])
        stats = sb("m_stats", [P, QT, 6])
        mv = sb("m_mv", [P, QT, 2])
        veps = sb("m_veps", [P, QT])
        std = sb("m_std", [P, QT])
        rstd = sb("m_rstd", [P, QT])
        xf = sb("xf", [P, QT, D])
        xfT = sb("xfT", [P, DB, NQ])
        acc = sb("acc", [P, QT, D])
        square = sb("square", [P, QT, D])
        sq_sum = sb("sq_sum", [P, QT])
        x_hi = sb("x_hi", [P, DB, NQ], F32R)
        x_lo = sb("x_lo", [P, DB, NQ], F32R)
        hT = sb("hT", [P, 2, DB, NQ])
        h_hi = sb("h_hi", [P, 2, DB, NQ], F32R)
        h_lo = sb("h_lo", [P, 2, DB, NQ], F32R)
        sT = sb("sT", [P, DB, NQ])
        aT = sb("m_aT", [P, 2, DB, NQ])
        a_hi = sb("a_hi", [P, DB, NQ], F32R)
        a_lo = sb("a_lo", [P, DB, NQ], F32R)
        gate = sb("gate", [P, QT, E])
        biased = sb("biased", [P, QT, E])
        above = sb("above", [P, QT, E, E])
        ties = sb("ties", [P, QT, E, E])
        rank = sb("rank", [P, QT, E])
        sel = sb("sel", [P, QT, E])
        far = sb("far", [P, QT, E])
        gate_max = sb("gate_max", [P, QT])
        e_sum = sb("e_sum", [P, QT])
        e_gate = sb("e_gate", [P, QT, E])
        wt = sb("wt", [P, QT, E + 1])
        wT = sb("wT", [E + 1, QT, P])

        ps = Banks(nc, ctx, "m_ps", NB, order, looped=True)
        bias_ps = ctx.enter_context(nc.psum_tensor("bias_ps", [P, 512], F32))
        w_ld = [sem(f"m_w_ld{i}") for i in range(WR)]
        bias_ld, small_ld = sem("bias_ld_m"), sem("small_ld")
        consts, bias_full, bias_ready = sem("m_consts"), sem("bias_full"), sem("bias_ready")
        chain = sem("m_chain")
        var_ready, std_ready = sem("m_var_ready"), sem("m_std_ready")
        xf_ready = sem("xf_ready")
        far_ready, gate_e = sem("far_ready"), sem("gate_e")
        wt_ready = sem("wt_ready")
        x_hi_done = sem("x_hi_done")
        w_hi_done, w_lo_done = sem("w_hi_done"), sem("w_lo_done")
        h_hi_done, h_lo_done = sem("h_hi_done"), sem("h_lo_done")
        a_done, a_split = sem("m_a_done"), sem("a_split")
        block = ctx.enter_context(nc.Block())

        @block.sync
        def _(sp):
            def load(layer, i):
                before = [q for q in range(layer * NM + i) if q % NM % WR == i % WR]
                if before:
                    sp.wait_ge(w_lo_done, before[-1] + 1)
                sp.dma_start(w_sb[:, i % WR, :, :], source(matrices[i])).then_inc(w_ld[i % WR], 16)

            ps.give_credit(sp)
            sp.sem_inc(a_done, 1)
            load(0, 0)
            row = 0
            for name, pat, count in (("ebup", "e (i p) -> (e i) p", E * DB), ("ebg", "e (i p) -> (e i) p", E * DB),
                                     ("sbup", "(i p) -> i p", 2 * DB), ("sbg", "(i p) -> i p", DB)):
                sp.dma_start(bias_rows[row:row + count, :], A[name].rearrange(pat, p=P)).then_inc(bias_ld, 16)
                row += count
            for layer in range(LAYERS):
                sp.dma_start(rw[:, layer, :, :], A["rW"][layer].rearrange("(j p) e -> p j e", p=P)
                             ).then_inc(small_ld, 16)
            for dst, src, width in ((rb, "rb", E), (gb, "gb", E), (nw, "nw", D)):
                flat = A[src].rearrange("(a l) e -> a l e", a=1)
                sp.dma_start(dst[:], flat.to_broadcast([P, LAYERS, width])).then_inc(small_ld, 16)
            sp.dma_start(bdown[0:E, :], A["ebdown"]).then_inc(small_ld, 16)
            sp.dma_start(bdown[E:E + 1, :], A["sbdown"].rearrange("(a d) -> a d", a=1)).then_inc(small_ld, 16)
            for layer in range(LAYERS):
                for i in range(NM):
                    if layer or i:
                        load(layer, i)

        SMALL = 16 * (LAYERS + 5)

        @block.gpsimd
        def _(pool):
            pool.memset(wt[:], 2.0).then_inc(consts, 1)
            pool.memset(earlier[:], 1.0).then_inc(consts, 1)
            pool.wait_ge(consts, 2)
            pool.affine_select(out=earlier[:], in_=earlier[:], compare_op=ALU.is_gt, fill=0.0, base=0,
                               pattern=[[1, E], [-1, E]], channel_multiplier=0).then_inc(consts, 1)

        def bias_column(kind, u, b):
            if kind == "up":
                at = BUP + u * DB + b if u < E else SBUP + (u - E) * DB + b
            else:
                at = BG + u * DB + b if u < E else SBG + b
            return bias[:, at:at + 1]

        @block.scalar
        def _(act):
            act.wait_ge(var_ready, 1)
            nc.scalar.activation(std[:], veps[:], ACT.Sqrt).then_inc(std_ready, 1)
            act.wait_ge(bias_ready, 1)

            def split_weights(j, m):
                act.wait_ge(w_ld[m % WR], 16 * (len(range(m % WR, NM, WR)) * j + m // WR + 1))
                if m >= WS:
                    ps.wait_full(act, last_use[matrices[m - WS]], j)
                else:
                    ps.wait_full_before(act, last_use[matrices[max(range(m, NM, WS))]], j)
                nc.scalar.activation(w_hi[:, m % WS, :, :], w_sb[:, m % WR, :, :], ACT.Copy).then_inc(w_hi_done, 1)

            with act.Fori(0, LAYERS) as j:
                split_weights(j, 0)
                for i in range(2):
                    ps.wait_full(act, ("xT", i), j)
                    src = ps["xT", i][:].rearrange("p (j q) -> p j q", j=2)
                    nc.scalar.activation(xfT[:, 2 * i:2 * i + 2, :], src, ACT.Copy)
                    nc.scalar.activation(x_hi[:, 2 * i:2 * i + 2, :], src, ACT.Copy).then_inc(x_hi_done, 1)
                split_weights(j, 1)
                for i, (kind, u) in enumerate(ops):
                    if i == 2:
                        act.wait_ge(far_ready, j + 1)
                        for t in range(QT):
                            nc.scalar.activation(e_gate[:, t, :], far[:, t, :], ACT.Exp, bias=gate_max[:, t:t + 1],
                                                 accum_out=e_sum[:, t:t + 1]).then_inc(gate_e, 1)
                    if new_matrix(i + 2):
                        split_weights(j, matrix_no(i + 2))
                    if kind == "up":
                        act.wait_ge(a_done, U * j + max(0, u - 1) + 1)
                    elif kind == "g":
                        act.wait_ge(a_done, U * j + u + 1)
                    else:
                        continue
                    for tile in range(2):
                        ps.wait_full(act, (kind, u, tile), j)
                        for r in range(2):
                            b = 2 * tile + r
                            dst = hT[:, u % 2, b, :] if kind == "up" else sT[:, b, :]
                            ins = nc.scalar.activation(dst, ps[kind, u, tile][:, bass.ts(r, NQ)],
                                                       ACT.Identity if kind == "up" else ACT.Silu,
                                                       bias=bias_column(kind, u, b))
                        ps.is_free(ins, (kind, u, tile))
                    if kind == "up":
                        ps.wait_read(act, ("up", u, 1), j)
                        if u >= 2:
                            ps.wait_full(act, ("g", u - 2, 1), j)
                        nc.scalar.activation(h_hi[:, u % 2, :, :], hT[:, u % 2, :, :], ACT.Copy
                                             ).then_inc(h_hi_done, 1)
                act.wait_ge(var_ready, j + 2)
                nc.scalar.activation(std[:], veps[:], ACT.Sqrt).then_inc(std_ready, 1)

        @block.vector
        def _(dve):
            n = [0]
            base = [0]

            def link(ins):
                n[0] += 1
                ins.then_inc(chain, 1)
                dve.wait_ge(chain, base[0] + n[0])

            for t in range(QT):
                link(dve.bn_stats(stats[:, t, :], S["x"][:, t, :]))
                link(dve.bn_aggr(mv[:, t, :], stats[:, t, :]))
            dve.tensor_scalar(veps[:], mv[:, :, 1], LN_EPS, None, ALU.add).then_inc(var_ready, 1)
            dve.wait_ge(std_ready, 1)
            link(dve.reciprocal(rstd[:], std[:]))
            for t in range(QT):
                dve.tensor_scalar(xf[:, t, :], S["x"][:, t, :], mv[:, t, 0:1], rstd[:, t:t + 1],
                                  ALU.subtract, ALU.mult).then_inc(xf_ready, 1)
            dve.wait_ge(bias_full, 1)
            dve.tensor_copy(bias[:], bias_ps[:, 0:NBIAS]).then_inc(bias_ready, 1)
            dve.wait_ge(small_ld, SMALL)
            dve.wait_ge(consts, 3)
            before = n[0]
            n[0] = 0

            def router(j):
                one = bass.ds(j, 1)
                for t in range(QT):
                    ps.wait_full(dve, ("gate", t), j)
                    ps.is_free(dve.tensor_tensor(gate[:, t:t + 1, :], ps["gate", t][:, 0:E].rearrange(
                        "p (a e) -> p a e", a=1), rb[:, one, :], ALU.add), ("gate", t))
                ps.wait_read(dve, ("gate", QT - 1), j)
                for t in range(QT):
                    link(dve.tensor_tensor(biased[:, t:t + 1, :], gate[:, t:t + 1, :], gb[:, one, :], ALU.add))
                for t in range(QT):
                    other = biased[:, t:t + 1, :].to_broadcast([P, E, E])
                    own = biased[:, t, :].rearrange("p (e a) -> p e a", a=1).to_broadcast([P, E, E])
                    link(dve.tensor_tensor(above[:, t, :, :], other, own, ALU.is_gt))
                    link(dve.tensor_tensor(ties[:, t, :, :], other, own, ALU.is_equal))
                    link(dve.tensor_tensor(ties[:, t, :, :], ties[:, t, :, :], earlier[:], ALU.mult))
                link(dve.tensor_tensor(above[:], above[:], ties[:], ALU.add))
                link(dve.tensor_reduce(rank[:], above[:], AX_X, ALU.add))
                link(dve.tensor_scalar(sel[:], rank[:], 1.5, None, ALU.is_lt))
                link(dve.tensor_scalar(far[:], sel[:], 1.0, FAR, ALU.subtract, ALU.mult))
                link(dve.tensor_tensor(sel[:], sel[:], gate[:], ALU.mult))
                link(dve.tensor_tensor(far[:], far[:], sel[:], ALU.add))
                link(dve.tensor_reduce(gate_max[:], far[:], AX_X, ALU.max))
                dve.tensor_scalar(gate_max[:], gate_max[:], -1.0, None, ALU.mult).then_inc(far_ready, 1)

            def weights(j):
                dve.wait_ge(gate_e, QT * j + QT)
                link(dve.reciprocal(e_sum[:], e_sum[:]))
                for t in range(QT):
                    dve.tensor_scalar(wt[:, t, 0:E], e_gate[:, t, :], e_sum[:, t:t + 1], None, ALU.mult
                                      ).then_inc(wt_ready, 1)
                for t in range(QT):
                    ps.wait_full(dve, ("wT", t), j)
                    ps.is_free(dve.tensor_copy(wT[:, t, :], ps["wT", t][0:E + 1, 0:P]), ("wT", t))
                for t in range(QT):
                    ps.wait_full(dve, ("bd", t), j)
                    ps.is_free(dve.tensor_tensor(acc[:, t, :], xf[:, t, :], ps["bd", t][:], ALU.add), ("bd", t))

            def split_weights(j, m):
                dve.wait_ge(w_hi_done, NM * j + m + 1)
                dve.tensor_tensor(w_lo[:, m % WS, :, :], w_sb[:, m % WR, :, :], w_hi[:, m % WS, :, :].bitcast(F32),
                                  ALU.subtract).then_inc(w_lo_done, 1)

            def split_h(j, u):
                dve.wait_ge(h_hi_done, U * j + u + 1)
                dve.tensor_tensor(h_lo[:, u % 2, :, :], hT[:, u % 2, :, :], h_hi[:, u % 2, :, :].bitcast(F32),
                                  ALU.subtract).then_inc(h_lo_done, 1)

            def gated(j, u):
                ps.wait_read(dve, ("g", u, 0), j)
                ps.wait_read(dve, ("g", u, 1), j)
                dve.tensor_tensor(aT[:, u % 2, :, :], sT[:], hT[:, u % 2, :, :], ALU.mult).then_inc(a_done, 1)
                dve.wait_ge(a_done, U * j + u + 2)
                if u == U - 2:
                    return
                if u == U - 1:
                    link(dve.tensor_tensor(aT[:, 1, :, :], aT[:, 1, :, :], aT[:, 0, :, :], ALU.add))
                if u:
                    ps.wait_full(dve, ("down", u - 1 if u < E else E - 1, 1), j)
                link(dve.tensor_copy(a_hi[:], aT[:, u % 2, :, :]))
                dve.tensor_tensor(a_lo[:], aT[:, u % 2, :, :], a_hi[:].bitcast(F32), ALU.subtract
                                  ).then_inc(a_split, 1)

            def accumulate(j, u):
                for t in range(QT):
                    key = ("down", u, t)
                    ps.wait_full(dve, key, j)
                    if u == 0:
                        ps.wait_read(dve, ("bd", t), j)
                    else:
                        ps.wait_read(dve, ("down", u - 1 if u < E else E - 1, t), j)
                    if u < E:
                        ins = dve.scalar_tensor_tensor(out=acc[:, t, :], in0=ps[key][:], scalar=wt[:, t, u:u + 1],
                                                       in1=acc[:, t, :], op0=ALU.mult, op1=ALU.add)
                    else:
                        ins = dve.tensor_tensor(acc[:, t, :], acc[:, t, :], ps[key][:], ALU.add)
                    ps.is_free(ins, key)

            LINKS = 19 + U
            with dve.Fori(0, LAYERS) as j:
                base[0] = LINKS * j + before
                split_weights(j, 0)
                for i in range(2):
                    two = slice(2 * i, 2 * i + 2)
                    dve.wait_ge(x_hi_done, 2 * j + i + 1)
                    ps.is_free(dve.tensor_tensor(x_lo[:, two, :], ps["xT", i][:].rearrange("p (j q) -> p j q", j=2),
                                                 x_hi[:, two, :].bitcast(F32), ALU.subtract), ("xT", i))
                split_weights(j, 1)
                router(j)
                for i, (kind, u) in enumerate(ops):
                    if i == MIX_AT:
                        weights(j)
                    if new_matrix(i + 2):
                        split_weights(j, matrix_no(i + 2))
                    if kind == "up":
                        split_h(j, u)
                    elif kind == "g":
                        gated(j, u)
                    elif kind == "down":
                        accumulate(j, u)
                ps.wait_read(dve, ("down", U - 1, QT - 1), j)
                for t in range(QT):
                    link(dve.tensor_tensor_reduce(square[:, t, :], acc[:, t, :], acc[:, t, :], 1.0, 0.0, ALU.mult,
                                                  ALU.add, sq_sum[:, t:t + 1]))
                dve.tensor_scalar(veps[:], sq_sum[:], 1.0 / D, RMS_EPS, ALU.mult, ALU.add).then_inc(var_ready, 1)
                dve.wait_ge(std_ready, j + 2)
                link(dve.reciprocal(rstd[:], std[:]))
                for t in range(QT):
                    dve.scalar_tensor_tensor(out=xf[:, t:t + 1, :], in0=acc[:, t:t + 1, :], scalar=rstd[:, t:t + 1],
                                             in1=nw[:, bass.ds(j, 1), :], op0=ALU.mult, op1=ALU.mult
                                             ).then_inc(xf_ready, 1)
                assert n[0] == LINKS, n[0]
            dve.wait_ge(xf_ready, QT * (LAYERS + 1))
            for t in range(QT):
                n[0] += 1
                dve.tensor_tensor(S["x"][:, t, :], S["x"][:, t, :], xf[:, t, :], ALU.add)

        @block.tensor
        def _(pe):
            pe.wait_ge(bias_ld, 64)
            pe.transpose(bias_ps[:, 0:NBIAS], bias_rows[:], S["ident"][0:NBIAS, 0:NBIAS]).then_inc(bias_full, 1)
            pe.wait_ge(small_ld, SMALL)
            with pe.Fori(0, LAYERS) as j:
                pe.wait_ge(xf_ready, QT * j + QT)
                for i in range(2):
                    ps.wait_free(pe, ("xT", i), j)
                    for b in range(2):
                        for t in range(QT):
                            at = b * NQ + t * P
                            last = pe.transpose(ps["xT", i][:, at:at + P], xf[:, t, bass.ts(2 * i + b, P)],
                                                S["ident"][:])
                    ps.is_full(last, ("xT", i))
                ps.wait_read(pe, ("xT", 0), j)
                ps.wait_read(pe, ("xT", 1), j)
                for t in range(QT):
                    ps.wait_free(pe, ("gate", t), j)
                    for b in range(DB):
                        last = pe.matmul(ps["gate", t][:, 0:E], xfT[:, b, bass.ts(t, P)],
                                         rw[:, bass.ds(j, 1), b, :].rearrange("p a e -> p (a e)"),
                                         start=(b == 0), stop=(b == DB - 1))
                    ps.is_full(last, ("gate", t))

                def mix():
                    pe.wait_ge(wt_ready, QT * j + QT)
                    for t in range(QT):
                        ps.wait_free(pe, ("wT", t), j)
                        ps.is_full(pe.transpose(ps["wT", t][0:E + 1, 0:P], wt[:, t, :], S["ident"][:]), ("wT", t))
                    for t in range(QT):
                        ps.wait_free(pe, ("bd", t), j)
                        ps.wait_read(pe, ("wT", t), j)
                        ps.is_full(pe.matmul(ps["bd", t][:], wT[:, t, :], bdown[:], start=True, stop=True), ("bd", t))

                for i, (kind, u) in enumerate(ops):
                    if i == MIX_AT:
                        mix()
                    m = matrix_no(i)
                    pe.wait_ge(w_lo_done, NM * j + m + 1)
                    whi, wlo = w_hi[:, m % WS, :, :], w_lo[:, m % WS, :, :]
                    if kind == "g":
                        pe.wait_ge(h_lo_done, U * j + u + 1)
                    if kind == "down":
                        pe.wait_ge(a_split, (U - 1) * j + (u + 1 if u < E else U - 1))
                    for tile in range(2):
                        ps.wait_free(pe, (kind, u, tile), j)
                        out = ps[kind, u, tile]
                        if kind == "down":
                            rows = bass.ts(tile, P)
                            for b in range(DB):
                                for s, (x, w) in enumerate(((a_hi, whi), (a_hi, wlo), (a_lo, whi))):
                                    last = pe.matmul(out[:], x[:, b, rows], w[:, b, :],
                                                     start=(b == 0 and s == 0), stop=(b == DB - 1 and s == 2))
                        else:
                            xh, xl = (x_hi, x_lo) if kind == "up" else (h_hi[:, u % 2, :, :], h_lo[:, u % 2, :, :])
                            for r in range(2):
                                cols = bass.ts(2 * tile + r, P)
                                for b in range(DB):
                                    for s, (w, x) in enumerate(((whi, xh), (whi, xl), (wlo, xh))):
                                        last = pe.matmul(out[:, bass.ts(r, NQ)], w[:, b, cols], x[:, b, :],
                                                         start=(b == 0 and s == 0), stop=(b == DB - 1 and s == 2))
                        ps.is_full(last, (kind, u, tile))


def store(nc, A, S):
    with ExitStack() as ctx:
        stored = ctx.enter_context(nc.semaphore("stored"))
        block = ctx.enter_context(nc.Block())

        @block.sync
        def _(sp):
            sp.dma_start(A["out"].rearrange("(t p) d -> p t d", p=P), S["x"][:]).then_inc(stored, 16)
            sp.wait_ge(stored, 16)


def program(nc, A, stages):
    with ExitStack() as ctx:
        S = {
            "x": ctx.enter_context(nc.sbuf_tensor("x_sb", [P, QT, D], F32)),
            "ident": ctx.enter_context(nc.sbuf_tensor("ident", [P, P], F32)),
            "mask_row": nc.dram_tensor("mask_row", [A["ctx"].shape[0]], F32, kind="Internal").ap(),
        }
        for stage in stages:
            stage(nc, A, S)


def context_attention(nc, A, S):
    with ExitStack() as ctx:
        def sb(name, shape, dt=F32):
            return ctx.enter_context(nc.sbuf_tensor(name, shape, dt))

        S = S | {
            "bk": sb("bk_sb", [P, NG]),
            "q_stack": sb("q_stack", [P, H, NQ], F32R),
            "m_old": sb("m_old", [P, H, QT]),
            "l": sb("l_run", [P, H, QT]),
            "o": sb("o_run", [P, QT, H, HD]),
        }
        for w in ("wk_hi", "wk_lo", "wv_hi", "wv_lo"):
            S[w] = sb(w, [P, DB, D], F32R)
        for stage in (load_and_project_queries, cross_attention, attention_output):
            stage(nc, A, S)


_NAMES = {
    "x": "x", "ctx_1024": "ctx", "fside_Bx16xSxS2_0": "bias", "mask_BxS2_bk0": "mask",
    "L0_xattn_Wq": "xWq", "L0_xattn_bq": "xbq", "L0_xattn_Wk": "xWk", "L0_xattn_bk": "xbk",
    "L0_xattn_Wv": "xWv", "L0_xattn_bv": "xbv", "L0_xattn_Wo": "xWo", "L0_xattn_bo": "xbo",
    "L0_attn_Wq": "aWq", "L0_attn_Wkv": "aWkv", "L0_attn_Wo": "aWo", "L0_attn_bo": "abo",
    "L0_ffn_router_W": "rW", "L0_ffn_router_b": "rb", "L0_ffn_gate_bias": "gb",
    "L0_ffn_exp_Wup": "eWup", "L0_ffn_exp_bup": "ebup", "L0_ffn_exp_Wg": "eWg", "L0_ffn_exp_bg": "ebg",
    "L0_ffn_exp_Wdown": "eWdown", "L0_ffn_exp_bdown": "ebdown",
    "L0_ffn_share_Wup": "sWup", "L0_ffn_share_bup": "sbup", "L0_ffn_share_Wg": "sWg",
    "L0_ffn_share_bg": "sbg", "L0_ffn_share_Wdown": "sWdown", "L0_ffn_share_bdown": "sbdown",
    "L0_ffn_norm_w": "nw",
}
_BATCHED = ("x", "ctx", "bias", "mask")


def kernel(**inputs):
    import numpy as _np
    import concourse.bacc as _bacc
    from concourse import mybir as _mybir
    from concourse.bass_utils import run_bass_kernel_spmd as _run

    nc = _bacc.Bacc("TRN2", target_bir_lowering=False, num_devices=1)
    arrays, A = {}, {}
    for name, short in _NAMES.items():
        a = _np.ascontiguousarray(inputs[name])
        if short in _BATCHED:
            a = a.reshape(a.shape[1:])
        arrays[f"in_{short}_dram"] = a
        A[short] = nc.dram_tensor(f"in_{short}_dram", a.shape, _mybir.dt.from_np(a.dtype),
                                  kind="ExternalInput").ap()
    A["out"] = nc.dram_tensor("out_0_dram", A["x"].shape, _mybir.dt.float32, kind="ExternalOutput").ap()
    program(nc, A, (context_attention, self_attention, moe, store))
    r = _run(nc, [arrays], core_ids=[0])
    got = r.results[0]["out_0_dram"]
    return got.reshape((1,) + got.shape)
```

```python
from contextlib import ExitStack

import concourse.bass as bass
from concourse import mybir

F32 = mybir.dt.float32
F32R = mybir.dt.float32r
U8 = mybir.dt.uint8
ALU = mybir.AluOpType
ACT = mybir.ActivationFunctionType
AX_X = mybir.AxisListType.X

P = 128
D = 512
DB = D // P
NQ = 256
QT = NQ // P
H = 16
HD = D // H
KC = 512
KB = KC // P
HG = P // HD
NG = H // HG
SCALE = HD ** -0.5
ADH = 64
AW = H * ADH
MASKED = -(2.0 ** 100)
NO_MAX = -3.0e38
LN_EPS = 1e-5

RING = 8
AHEAD = RING - 1
KDMA = 3 * HG + 1
TILES = 12
V1, CT, K01, V0, K23 = 0, 2, 6, 8, 10
K_TILE = {0: K01, 1: K01 + 1, 2: K23, 3: K23 + 1}
SHARE = [[(V1, 0)], [(V1, 1)], [(V1 + 1, 0)], [(V1 + 1, 1)],
         [(CT, 1), (CT + 1, 1)], [(CT + 2, 1), (CT + 3, 1)],
         [(K01, 0), (K01, 1)], [(K01 + 1, 0), (K01 + 1, 1)],
         [(V0, 0)], [(V0, 1)], [(V0 + 1, 0)], [(V0 + 1, 1)],
         [(K23, 0)], [(K23, 1)], [(K23 + 1, 0)], [(K23 + 1, 1)]]
PROJECT_LATE = [h for h in range(H) if SHARE[h][0][0] in (K01, K01 + 1)]


def hold_clock(pe, S, bank, times):
    for _ in range(times):
        pe.transpose(bank[:, 0:P], S["ident"][:], S["ident"][:])


def cross_attention(nc, A, S):
    n_keys = A["ctx"].shape[0]
    NC = n_keys // KC
    assert n_keys % KC == 0 and NC >= 4
    with ExitStack() as ctx:
        def sb(name, shape, dt=F32):
            return ctx.enter_context(nc.sbuf_tensor(name, shape, dt))

        def bank(name):
            return ctx.enter_context(nc.psum_tensor(name, [P, 512], F32))

        def sem(name):
            return ctx.enter_context(nc.semaphore(name))

        k_stack = sb("k_stack", [P, H, KC], F32R)
        v = sb("v", [P, KB, H, 2, HD], F32R)
        ctx_sb = sb("ctx_sb", [P, KB, D])
        ctxT_hi = sb("ctxT_hi", [P, DB, KC], F32R)
        ctxT_lo = sb("ctxT_lo", [P, DB, KC], F32R)
        k_hi = sb("k_hi", [P, 2, KC], F32R)
        k_lo = sb("k_lo", [P, 2, KC], F32R)
        logits = sb("logits", [P, RING, QT, KC])
        pT_hi = sb("pT_hi", [P, 2, 2, 2 * NQ], F32R)
        pT_lo = sb("pT_lo", [P, 2, 2, 2 * NQ], F32R)
        oT = sb("oT", [P, 2, NQ])
        o_new = sb("o_new", [P, 2, QT * 2, HD])
        m_new = sb("m_new", [P, H, QT])
        m_neg = sb("m_neg", [P, H, QT])
        m_diff = sb("m_diff", [P, H, QT])
        alpha = sb("alpha", [P, H, QT])
        row_sum = sb("row_sum", [P, H, QT])
        one = sb("one", [P, QT])
        m_old, l, o = S["m_old"], S["l"], S["o"]

        wq, wk, wv = (logits[:, 2 * i + 1:2 * i + 3, :, :].rearrange("p a b n -> p (a b) n") for i in range(3))
        q_hi, q_lo = (pT_hi[:, i, :, :].rearrange("p a (g q) -> p (a g) q", q=NQ) for i in range(2))
        xn = S["wo"][:, 0:2, :]
        xnT = S["wo"][:, 2:4, :].rearrange("p a (j q) -> p (a j) q", q=NQ)
        q_f = logits[:, RING - 1, :, :].rearrange("p t (g q) -> p (t g) q", q=NQ)
        stats = sb("ln_stats", [P, QT, 6])
        mv = sb("ln_mv", [P, QT, 2])
        veps = sb("ln_veps", [P, QT])
        std = sb("ln_std", [P, QT])
        rstd = sb("ln_rstd", [P, QT])
        bq = sb("bq", [P, NG])
        n_cols = n_keys // P
        mask_u8 = sb("mask_u8", [P, n_cols], U8)
        mask_f = sb("mask_f", [P, n_cols])
        mask_r = sb("mask_r", [P, n_cols], F32R)
        mask_min = sb("mask_min", [P, 1])
        all_masked = sb("all_masked", [P, 1])
        ones = sb("ones", [P, P])

        s_ps = [bank(f"s_ps{t}") for t in range(QT)]
        pT_ps = [bank(f"pT_ps{b}") for b in range(2)]
        proj_ps = [bank(f"proj_ps{b}") for b in range(2)]
        oT_ps = bank("oT_ps")
        o_ps = bank("o_ps")

        bias_ld = [sem(f"bias_ld{r}") for r in range(RING)]
        ctx_ld = sem("ctx_ld")
        k_ld = [sem(f"k_ld{half}") for half in range(2)]
        s_full = sem("s_full")
        t_done = sem("t_done")
        m_ready = sem("m_ready")
        one_set = sem("one_set")
        m_saved = sem("m_saved")
        p_done = sem("p_done")
        a_done = sem("a_done")
        l_scaled = sem("l_scaled")
        o_scaled = sem("o_scaled")
        l_done = sem("l_done")
        tr_done = sem("tr_done")
        hi_done = sem("hi_done")
        lo_done = sem("lo_done")
        pv_done = sem("pv_done")
        oT_done = sem("oT_done")
        ox_done = sem("ox_done")
        fold_done = sem("fold_done")
        o_done = sem("o_done")
        proj_full = sem("proj_full")
        proj_hi = sem("proj_hi")
        proj_lo = sem("proj_lo")
        x_ld, wq_ld, wk_ld, wv_ld = sem("x_ld"), sem("wq_ld"), sem("wk_ld"), sem("wv_ld")
        mask_ld, const_ld, q_ld = sem("mask_ld"), sem("const_ld"), sem("q_ld")
        mask_stored = sem("mask_stored")
        zeroed, consts, first_values = sem("zeroed"), sem("consts"), sem("first_values")
        chain = sem("prep_chain")
        var_ready, std_ready = sem("var_ready"), sem("std_ready")
        xn_ready, xnT_full, xnT_ready = sem("xn_ready"), sem("xnT_full"), sem("xnT_ready")
        q_full, q_free, q_split = sem("q_full"), sem("q_free"), sem("q_split")
        w_hi, w_lo = sem("w_hi"), sem("w_lo")
        min_ready, count_ready, mask_ready = sem("min_ready"), sem("count_ready"), sem("mask_ready")

        block = ctx.enter_context(nc.Block())

        def group_of(i):
            return {tile: g for g, tile in K_TILE.items()}[i]

        def tiles(c, i):
            return TILES * (c + 1) + i - 1

        def wait(eng, s, value):
            if not isinstance(value, int) or value > 0:
                eng.wait_ge(s, value)

        def over_chunks(eng, steps):
            steps(0, False)
            with eng.Fori(1, NC - 1) as c:
                steps(c, False)
            steps(NC - 1, True)

        @block.sync
        def _(sp):
            def load_bias(c, h):
                n = H * c + h
                wait(sp, tr_done, 2 * (n - RING + 1))
                src = A["bias"][h, :, bass.ds(c * KC, KC)].rearrange("(t p) k -> p t k", p=P)
                sp.dma_start(logits[:, h % RING, :, :], src).then_inc(bias_ld[h % RING], 16)

            def load_ctx(c):
                sp.dma_start(ctx_sb[:], A["ctx"][bass.ds(c * KC, KC), :].rearrange("(b p) d -> p b d", p=P)
                             ).then_inc(ctx_ld, 16)

            def stack_keys(c, half):
                heads = slice(H // 2 * half, H // 2 * (half + 1))
                wait(sp, s_full, QT * (H * c + H // 2 * (half + 1)))
                row = S["mask_row"][bass.ds((c + 1) * KC, KC)].rearrange("(a b k) -> a b k", a=1, b=1)
                sp.dma_start(k_stack[3 * HD:3 * HD + 1, heads, :].bitcast(F32),
                             row.to_broadcast([1, H // 2, KC])).then_inc(k_ld[half], 16)
                sp.wait_ge(proj_lo, tiles(c, K_TILE[2 * half + 1]))
                for i in range(HG):
                    rows = slice(HD * i, HD * (i + 1))
                    for r, part in enumerate((k_hi, k_lo, k_hi)):
                        sp.dma_start(k_stack[HD * r:HD * (r + 1), heads, :][:, i::HG, :].bitcast(F32),
                                     part[rows, :, :].bitcast(F32)).then_inc(k_ld[half], 16)

            sp.dma_start(S["x"][:], A["x"].rearrange("(t p) d -> p t d", p=P)).then_inc(x_ld, 16)
            sp.dma_start(wq, A["xWq"].rearrange("(j p) n -> p j n", p=P)).then_inc(wq_ld, 16)
            sp.dma_start(mask_u8[:], A["mask"].rearrange("(p t) -> p t", p=P)).then_inc(mask_ld, 16)
            sp.dma_start(bq[:], A["xbq"].rearrange("(g p) -> p g", p=P),
                         allow_slow_non_contiguous=True).then_inc(const_ld, 16)
            sp.dma_start(S["bk"][:], A["xbk"].rearrange("(g p) -> p g", p=P),
                         allow_slow_non_contiguous=True).then_inc(const_ld, 16)
            sp.dma_start(wk, A["xWk"].rearrange("(j p) n -> p j n", p=P)).then_inc(wk_ld, 16)
            load_ctx(0)
            sp.dma_start(wv, A["xWv"].rearrange("(j p) n -> p j n", p=P)).then_inc(wv_ld, 16)
            load_bias(0, 0)
            sp.wait_ge(mask_ready, 1)
            sp.dma_start(S["mask_row"].rearrange("(p t) -> p t", p=P), mask_r[:].bitcast(F32)
                         ).then_inc(mask_stored, 16)
            sp.wait_ge(q_split, NG)
            for i in range(HG):
                rows = slice(HD * i, HD * (i + 1))
                for r, part in enumerate((q_hi, q_hi, q_lo)):
                    sp.dma_start(S["q_stack"][HD * r:HD * (r + 1), i::HG, :].bitcast(F32),
                                 part[rows].bitcast(F32)).then_inc(q_ld, 16)
            sp.wait_ge(mask_stored, 16)
            stack_keys(-1, 0)
            load_bias(0, 1)
            load_bias(0, 2)
            sp.wait_ge(w_lo, 2)
            for n in range(3, AHEAD):
                load_bias(0, n)
            stack_keys(-1, 1)
            load_ctx(1)
            sp.dma_start(S["wo"][:], A["xWo"].rearrange("(j p) n -> p j n", p=P)).then_inc(S["out_ld"], 16)
            for name in ("bv", "bo"):
                sp.dma_start(S[name][:], A["x" + name].rearrange("(a d) -> a d", a=1).to_broadcast([P, D])
                             ).then_inc(S["out_ld"], 16)

            def steps(c, last):
                for h in range(H):
                    if h + AHEAD < H:
                        load_bias(c, h + AHEAD)
                    elif not last:
                        load_bias(c + 1, h + AHEAD - H)
                    if last:
                        continue
                    if h == 6 and not (isinstance(c, int) and c == NC - 2):
                        sp.wait_ge(proj_full, tiles(c, CT + DB - 1))
                        load_ctx(c + 2)
                    if h == 8:
                        stack_keys(c, 0)
                    if h == 15:
                        stack_keys(c, 1)

            steps(0, False)
            with sp.Fori(1, NC - 2) as c:
                steps(c, False)
            steps(NC - 2, False)
            steps(NC - 1, True)

        @block.tensor
        def _(pe):
            def transpose(c, h, b):
                n = H * c + h
                if b == 0:
                    pe.wait_ge(p_done, QT * (n + 1))
                wait(pe, lo_done, 2 * (n - 1) + b + 1)
                for k in range(2):
                    for t in range(QT):
                        at = k * NQ + t * P
                        last = pe.transpose(pT_ps[b][:, at:at + P],
                                            logits[:, h % RING, t, bass.ts(2 * b + k, P)], S["ident"][:])
                last.then_inc(tr_done, 1)

            def scores(c, h):
                n = H * c + h
                if h % (H // 2) == 0:
                    pe.wait_ge(k_ld[h // (H // 2)], 16 * KDMA * (c + 1))
                for t in range(QT):
                    wait(pe, t_done, QT * (n - 1) + t + 1)
                    pe.matmul(s_ps[t][:], S["q_stack"][0:3 * HD + 1, h, bass.ts(t, P)],
                              k_stack[0:3 * HD + 1, h, :], start=True, stop=True).then_inc(s_full, 1)

            def weighted_values(c, h):
                n = H * c + h
                pe.wait_ge(lo_done, 2 * (n + 1))
                wait(pe, oT_done, n)
                if h == 0:
                    pe.wait_ge(proj_lo, tiles(c - 1, V0 + 1))
                if h == H // 2:
                    pe.wait_ge(proj_lo, tiles(c, V1 + 1))
                for kb in range(KB):
                    for i, part in enumerate((pT_hi, pT_lo)):
                        last = pe.matmul(oT_ps[0:2 * HD, 0:NQ],
                                         v[:, kb, h, :, :].rearrange("p a d -> p (a d)"),
                                         part[:, h % 2, kb // 2, (kb % 2) * NQ:(kb % 2 + 1) * NQ],
                                         start=(kb == 0 and i == 0), stop=(kb == KB - 1 and i == 1))
                last.then_inc(pv_done, 1)

            def turn_output(c, h):
                pair = H // 2 * c + h // 2
                pe.wait_ge(oT_done, H * c + h + 1)
                wait(pe, fold_done, pair)
                for t in range(QT):
                    last = pe.transpose(o_ps[:, bass.ts(t, P)], oT[:, h // 2 % 2, bass.ts(t, P)], S["ident"][:])
                last.then_inc(ox_done, 1)

            def free_bank(c, i):
                wait(pe, proj_lo, tiles(c, i) - 2)

            def context_tile(c, j):
                i = CT + j
                free_bank(c, i)
                if j == 0:
                    pe.wait_ge(ctx_ld, 16 * (c + 2))
                for b in range(KB):
                    last = pe.transpose(proj_ps[i % 2][:, bass.ts(b, P)], ctx_sb[:, b, bass.ts(j, P)],
                                        S["ident"][:])
                last.then_inc(proj_full, 1)

            def key_tile(c, g, part):
                i = K_TILE[g]
                if part == 0:
                    free_bank(c, i)
                    if g == 0:
                        pe.wait_ge(proj_lo, tiles(c, CT + DB - 1))
                for j in (0, 1) if part == 0 else (2, 3):
                    for s, (w, x) in enumerate((("wk_hi", ctxT_hi), ("wk_hi", ctxT_lo), ("wk_lo", ctxT_hi))):
                        last = pe.matmul(proj_ps[i % 2][:], S[w][:, j, bass.ts(g, P)], x[:, j, :],
                                         start=(j == 0 and s == 0), stop=(j == DB - 1 and s == 2))
                if part == 1:
                    last.then_inc(proj_full, 1)

            def value_tile(c, i, half, part):
                if part == 0:
                    free_bank(c, i)
                b = 2 * (i % 2) + part
                cols = slice(half * D // 2, (half + 1) * D // 2)
                for j in range(DB):
                    for s, (x, w) in enumerate(((ctxT_hi, "wv_hi"), (ctxT_hi, "wv_lo"), (ctxT_lo, "wv_hi"))):
                        last = pe.matmul(proj_ps[i % 2][:, part * 256:(part + 1) * 256], x[:, j, bass.ts(b, P)],
                                         S[w][:, j, cols], start=(j == 0 and s == 0),
                                         stop=(j == DB - 1 and s == 2))
                if part == 1:
                    last.then_inc(proj_full, 1)

            pe.wait_ge(consts, 2)
            hold_clock(pe, S, oT_ps, 30)
            pe.wait_ge(xn_ready, QT)
            for h in range(2):
                for j in (2 * h, 2 * h + 1):
                    for t in range(QT):
                        at = (j % 2) * NQ + t * P
                        last = pe.transpose(pT_ps[h][:, at:at + P], xn[:, t, j * P:(j + 1) * P], S["ident"][:])
                last.then_inc(xnT_full, 1)
            pe.wait_ge(min_ready, 1)
            pe.matmul(o_ps[:, 0:1], ones[:], mask_min[:], start=True, stop=True).then_inc(count_ready, 1)
            pe.wait_ge(xnT_ready, 2)
            pe.wait_ge(wq_ld, 16)
            for g in range(NG):
                if g >= 2:
                    pe.wait_ge(q_free, g - 1)
                for j in range(DB):
                    last = pe.matmul(s_ps[g % 2][:, 0:NQ], wq[:, j, g * P:(g + 1) * P], xnT[:, j, :],
                                     start=(j == 0), stop=(j == DB - 1))
                last.then_inc(q_full, 1)
                if g == 2:
                    context_tile(-1, 0), context_tile(-1, 1)
            for j in (2, 3):
                context_tile(-1, j)
            pe.wait_ge(w_lo, 1)
            for g in (0, 1):
                key_tile(-1, g, 0), key_tile(-1, g, 1)
            pe.wait_ge(w_lo, 2)
            for i in (0, 1):
                value_tile(-1, V0 + i, 0, 0), value_tile(-1, V0 + i, 0, 1)
            for g in (2, 3):
                key_tile(-1, g, 0), key_tile(-1, g, 1)
            pe.wait_ge(q_ld, 16 * 3 * HG)
            pe.wait_ge(first_values, 4)
            scores(0, 0)
            scores(0, 1)

            def project(c, h, last):
                for i, half in SHARE[h]:
                    if last and i >= CT:
                        continue
                    if CT <= i < CT + DB:
                        context_tile(c, i - CT)
                    elif i in K_TILE.values():
                        key_tile(c, group_of(i), half)
                    else:
                        value_tile(c, i, 1 if i < CT else 0, half)

            def steps(c, last):
                for h in range(H):
                    transpose(c, h, 0)
                    transpose(c, h, 1)
                    if h + 2 < H:
                        scores(c, h + 2)
                    elif not last:
                        scores(c + 1, h + 2 - H)
                    if h not in PROJECT_LATE:
                        project(c, h, last)
                    if h >= 1:
                        weighted_values(c, h - 1)
                    elif not (isinstance(c, int) and c == 0):
                        weighted_values(c - 1, H - 1)
                    if h in PROJECT_LATE:
                        project(c, h, last)
                    if h >= 3 and h % 2:
                        turn_output(c, h - 2)
                    elif h == 1 and not (isinstance(c, int) and c == 0):
                        turn_output(c - 1, H - 1)

            over_chunks(pe, steps)
            weighted_values(NC - 1, H - 1)
            turn_output(NC - 1, H - 1)

        def finished_tiles(h):
            return [i for i, half in SHARE[h] if half == 1]

        def value_out(i, half, part):
            b = 2 * (i % 2)
            return v[:, b:b + 2, half * H // 2:(half + 1) * H // 2, part, :]

        @block.scalar
        def _(act):
            def split_hi(c, h, b):
                n = H * c + h
                act.wait_ge(tr_done, 2 * n + b + 1)
                wait(act, pv_done, n - 1)
                nc.scalar.activation(pT_hi[:, h % 2, b, :], pT_ps[b][:], ACT.Copy).then_inc(hi_done, 1)

            def exponentials(c, h, t):
                n = H * c + h
                if t == 0:
                    act.wait_ge(m_ready, 2 * (n + 1))
                    wait(act, l_done, n - H + 1)
                at = logits[:, h % RING, t, :]
                nc.scalar.activation(at, at, ACT.Exp, bias=m_neg[:, h, t:t + 1],
                                     accum_out=row_sum[:, h, t:t + 1]).then_inc(p_done, 1)

            def rescaling(c, h):
                wait(act, o_done, H // 2 * (c - 1) + h // 2 + 1)
                nc.scalar.activation(alpha[:, h, :], m_diff[:, h, :], ACT.Exp).then_inc(a_done, 1)

            def copy_output(c, h):
                n = H * c + h
                act.wait_ge(pv_done, n + 1)
                wait(act, ox_done, H // 2 * c + h // 2 - 1)
                rows = slice(2 * HD * (h % 2), 2 * HD * (h % 2 + 1))
                nc.scalar.activation(oT[rows, h // 2 % 2, :], oT_ps[0:2 * HD, 0:NQ], ACT.Copy).then_inc(oT_done, 1)

            def tile_hi(c, i):
                act.wait_ge(proj_full, tiles(c, i))
                src = proj_ps[i % 2]
                if CT <= i < CT + DB:
                    ins = nc.scalar.activation(ctxT_hi[:, i - CT, :], src[:], ACT.Copy)
                elif i in (V1, V1 + 1, V0, V0 + 1):
                    half = 1 if i < CT else 0
                    wait(act, pv_done, H * c if half else H * c + H // 2)
                    ins = nc.scalar.activation(value_out(i, half, 0),
                                               src[:].rearrange("p (b h d) -> p b h d", b=2, d=HD), ACT.Copy)
                else:
                    g = group_of(i)
                    if g >= 2:
                        act.wait_ge(k_ld[0], 16 * KDMA * (c + 2))
                    else:
                        wait(act, k_ld[1], 16 * KDMA * (c + 1))
                    ins = nc.scalar.activation(k_hi[:, g % 2, :], src[:], ACT.Identity, bias=S["bk"][:, g:g + 1])
                ins.then_inc(proj_hi, 1)

            act.wait_ge(var_ready, 1)
            nc.scalar.activation(std[:], veps[:], ACT.Sqrt).then_inc(std_ready, 1)
            act.wait_ge(wk_ld, 16)
            nc.scalar.activation(S["wk_hi"][:], wk, ACT.Copy).then_inc(w_hi, 1)
            for i in range(CT, CT + DB):
                tile_hi(-1, i)
            act.wait_ge(wv_ld, 16)
            nc.scalar.activation(S["wv_hi"][:], wv, ACT.Copy).then_inc(w_hi, 1)
            act.wait_ge(const_ld, 32)
            for i in range(K01, K23):
                tile_hi(-1, i)
            for t in range(QT):
                exponentials(0, 0, t)
            rescaling(0, 0)
            for i in range(K23, TILES):
                tile_hi(-1, i)

            def steps(c, last):
                for h in range(H):
                    ahead = (c, h + 1) if h + 1 < H else (c + 1, 0)
                    more = h + 1 < H or not last
                    split_hi(c, h, 0)
                    if more:
                        exponentials(*ahead, 0)
                    split_hi(c, h, 1)
                    if more:
                        exponentials(*ahead, 1)
                        rescaling(*ahead)
                    for i in finished_tiles(h):
                        if not last or i < CT:
                            tile_hi(c, i)
                    if h >= 1:
                        copy_output(c, h - 1)
                    elif not (isinstance(c, int) and c == 0):
                        copy_output(c - 1, H - 1)

            over_chunks(act, steps)
            copy_output(NC - 1, H - 1)

        @block.vector
        def _(dve):
            def split_lo(c, h, b):
                dve.wait_ge(hi_done, 2 * (H * c + h) + b + 1)
                dve.tensor_tensor(pT_lo[:, h % 2, b, :], pT_ps[b][:],
                                  pT_hi[:, h % 2, b, :].bitcast(F32), ALU.subtract).then_inc(lo_done, 1)

            def await_logits(c, h, t):
                n = H * c + h
                if t == 0:
                    use = (H // RING) * c + h // RING + 1
                    dve.wait_ge(bias_ld[h % RING], 16 * use)
                    wait(dve, m_saved, n - H + 1)
                dve.wait_ge(s_full, QT * n + t + 1)

            def logits_and_max(c, h, t):
                at = logits[:, h % RING, t, :]
                dve.tensor_tensor_reduce(at, s_ps[t][:], at, 1.0, m_old[:, h, t:t + 1], ALU.add, ALU.max,
                                         m_new[:, h, t:t + 1]).then_inc(t_done, 1)

            def fold_output(c, h):
                pair = H // 2 * c + h // 2
                dve.wait_ge(ox_done, pair + 1)
                wait(dve, o_done, pair - 1)
                dve.tensor_reduce(o_new[:, h // 2 % 2, :, :],
                                  o_ps[:, 0:QT * P].rearrange("p (b a d) -> p b d a", a=2, d=HD),
                                  AX_X, ALU.add).then_inc(fold_done, 1)

            def tile_lo(c, i):
                dve.wait_ge(proj_hi, tiles(c, i))
                src = proj_ps[i % 2]
                if CT <= i < CT + DB:
                    ins = dve.tensor_tensor(ctxT_lo[:, i - CT, :], src[:],
                                            ctxT_hi[:, i - CT, :].bitcast(F32), ALU.subtract)
                elif i in (V1, V1 + 1, V0, V0 + 1):
                    half = 1 if i < CT else 0
                    ins = dve.tensor_tensor(value_out(i, half, 1),
                                            src[:].rearrange("p (b h d) -> p b h d", b=2, d=HD),
                                            value_out(i, half, 0).bitcast(F32), ALU.subtract)
                else:
                    g = group_of(i)
                    ins = dve.scalar_tensor_tensor(out=k_lo[:, g % 2, :], in0=src[:], scalar=S["bk"][:, g:g + 1],
                                                   in1=k_hi[:, g % 2, :].bitcast(F32), op0=ALU.add,
                                                   op1=ALU.subtract)
                ins.then_inc(proj_lo, 1)

            n_links = [0]

            def link(ins):
                n_links[0] += 1
                ins.then_inc(chain, 1)
                dve.wait_ge(chain, n_links[0])

            dve.wait_ge(x_ld, 16)
            for t in range(QT):
                link(dve.bn_stats(stats[:, t, :], S["x"][:, t, :]))
                link(dve.bn_aggr(mv[:, t, :], stats[:, t, :]))
            dve.tensor_scalar(veps[:], mv[:, :, 1], LN_EPS, None, ALU.add).then_inc(var_ready, 1)
            dve.wait_ge(std_ready, 1)
            link(dve.reciprocal(rstd[:], std[:]))
            for t in range(QT):
                dve.tensor_scalar(xn[:, t, :], S["x"][:, t, :], mv[:, t, 0:1], rstd[:, t:t + 1],
                                  ALU.subtract, ALU.mult).then_inc(xn_ready, 1)
            dve.wait_ge(mask_ld, 16)
            link(dve.tensor_copy(mask_f[:], mask_u8[:]))
            dve.tensor_reduce(mask_min[:], mask_f[:], AX_X, ALU.min).then_inc(min_ready, 1)
            for h in range(2):
                dve.wait_ge(xnT_full, h + 1)
                dve.tensor_copy(xnT[:, 2 * h:2 * h + 2, :], pT_ps[h][:].rearrange("p (j q) -> p j q", j=2)
                                ).then_inc(xnT_ready, 1)
            dve.wait_ge(count_ready, 1)
            link(dve.tensor_scalar(all_masked[:], o_ps[:, 0:1], P - 0.5, None, ALU.is_ge))
            link(dve.tensor_tensor(mask_f[0:1, 0:1], mask_f[0:1, 0:1], all_masked[0:1, :], ALU.subtract))
            dve.tensor_scalar(mask_r[:], mask_f[:], MASKED, None, ALU.mult).then_inc(mask_ready, 1)
            dve.wait_ge(w_hi, 1)
            dve.tensor_tensor(S["wk_lo"][:], wk, S["wk_hi"][:].bitcast(F32), ALU.subtract).then_inc(w_lo, 1)
            dve.wait_ge(const_ld, 32)
            for g in range(NG):
                dve.wait_ge(q_full, g + 1)
                dve.tensor_scalar(q_f[:, g, :], s_ps[g % 2][:, 0:NQ], bq[:, g:g + 1], SCALE, ALU.add, ALU.mult
                                  ).then_inc(q_free, 1)
                dve.wait_ge(q_free, g + 1)
                link(dve.tensor_copy(q_hi[:, g, :], q_f[:, g, :]))
                dve.tensor_tensor(q_lo[:, g, :], q_f[:, g, :], q_hi[:, g, :].bitcast(F32),
                                  ALU.subtract).then_inc(q_split, 1)
            for i in range(CT, CT + DB):
                tile_lo(-1, i)
            dve.wait_ge(w_hi, 2)
            dve.tensor_tensor(S["wv_lo"][:], wv, S["wv_hi"][:].bitcast(F32), ALU.subtract).then_inc(w_lo, 1)
            for i in range(K01, K23):
                tile_lo(-1, i)
            dve.wait_ge(first_values, 4)
            for h in range(2):
                for t in range(QT):
                    await_logits(0, h, t)
                    logits_and_max(0, h, t)
            for i in range(K23, TILES):
                tile_lo(-1, i)

            def steps(c, last):
                for h in range(H):
                    ahead = (c, h + 2) if h + 2 < H else (c + 1, h + 2 - H)
                    more = h + 2 < H or not last
                    for t in range(QT):
                        if more:
                            await_logits(*ahead, t)
                        split_lo(c, h, t)
                        if more:
                            logits_and_max(*ahead, t)
                    for i in finished_tiles(h):
                        if not last or i < CT:
                            tile_lo(c, i)
                    if h >= 3 and h % 2:
                        fold_output(c, h - 2)
                    elif h == 1 and not (isinstance(c, int) and c == 0):
                        fold_output(c - 1, H - 1)

            over_chunks(dve, steps)
            fold_output(NC - 1, H - 1)

        @block.gpsimd
        def _(pool):
            def maxima(c, h):
                n = H * c + h
                pool.wait_ge(t_done, QT * (n + 1))
                wait(pool, p_done, QT * (n - H + 1))
                wait(pool, a_done, n - H + 1)
                pool.tensor_tensor(m_diff[:, h, :], m_old[:, h, :], m_new[:, h, :],
                                   ALU.subtract).then_inc(m_ready, 1)
                pool.tensor_scalar(m_neg[:, h, :], m_new[:, h, :], -1.0, None, ALU.mult).then_inc(m_ready, 1)
                pool.wait_ge(m_ready, 2 * (n + 1))
                pool.tensor_tensor(m_old[:, h, :], m_new[:, h, :], one[:], ALU.mult).then_inc(m_saved, 1)

            def rescale(c, h):
                n = H * c + h
                pool.wait_ge(a_done, n + 1)
                wait(pool, l_done, n - H + 1)
                pool.tensor_tensor(l[:, h, :], l[:, h, :], alpha[:, h, :], ALU.mult).then_inc(l_scaled, 1)
                pool.wait_ge(p_done, QT * (n + 1))
                pool.wait_ge(l_scaled, n + 1)
                pool.tensor_tensor(l[:, h, :], l[:, h, :], row_sum[:, h, :], ALU.add).then_inc(l_done, 1)

            def update_output(c, h):
                pair = H // 2 * c + h // 2
                heads = slice(h - 1, h + 1)
                factors = alpha[:, heads, :].rearrange("p h (t a) -> p t h a", a=1).to_broadcast([P, QT, 2, HD])
                wait(pool, o_done, H // 2 * (c - 1) + h // 2 + 1)
                pool.tensor_tensor(o[:, :, heads, :], o[:, :, heads, :], factors, ALU.mult).then_inc(o_scaled, 1)
                pool.wait_ge(fold_done, pair + 1)
                pool.wait_ge(o_scaled, pair + 1)
                pool.tensor_tensor(o[:, :, heads, :], o[:, :, heads, :],
                                   o_new[:, h // 2 % 2, :, :].rearrange("p (t h) d -> p t h d", t=QT),
                                   ALU.add).then_inc(o_done, 1)

            pool.memset(S["ident"][:], 0.0).then_inc(zeroed, 1)
            pool.wait_ge(zeroed, 1)
            pool.affine_select(out=S["ident"][:], in_=S["ident"][:], compare_op=ALU.not_equal, fill=1.0,
                               base=0, pattern=[[-1, P]], channel_multiplier=1).then_inc(consts, 1)
            pool.memset(ones[:], 1.0).then_inc(consts, 1)
            pool.memset(one[:], 1.0).then_inc(one_set, 1)
            pool.memset(m_old[:], NO_MAX).then_inc(first_values, 1)
            pool.memset(l[:], 0.0).then_inc(first_values, 1)
            pool.memset(o[:], 0.0).then_inc(first_values, 1)
            pool.wait_ge(consts, 2)
            pool.wait_ge(one_set, 1)
            pool.wait_ge(first_values, 3)
            pool.memset(S["q_stack"][3 * HD:3 * HD + 1, :, :].bitcast(F32), 1.0).then_inc(first_values, 1)
            pool.wait_ge(first_values, 4)
            maxima(0, 0)
            rescale(0, 0)
            maxima(0, 1)

            def steps(c, last):
                for h in range(H):
                    if h + 1 < H:
                        rescale(c, h + 1)
                    elif not last:
                        rescale(c + 1, 0)
                    if h + 2 < H:
                        maxima(c, h + 2)
                    elif not last:
                        maxima(c + 1, h + 2 - H)
                    if h >= 3 and h % 2:
                        update_output(c, h - 2)
                    elif h == 1 and not (isinstance(c, int) and c == 0):
                        update_output(c - 1, H - 1)

            over_chunks(pool, steps)
            update_output(NC - 1, H - 1)


def attention_output(nc, A, S):
    with ExitStack() as ctx:
        def sb(name, shape, dt=F32):
            return ctx.enter_context(nc.sbuf_tensor(name, shape, dt))

        def sem(name):
            return ctx.enter_context(nc.semaphore(name))

        wo, bv, bo = S["wo"], S["bv"], S["bo"]
        l_inv = sb("l_inv", [P, H, QT])
        a = sb("a", [P, QT, D])
        aT = sb("aT", [P, DB, NQ])
        aT_ps = [ctx.enter_context(nc.psum_tensor(f"aT_ps{i}", [P, 512], F32)) for i in range(2)]
        y_ps = [ctx.enter_context(nc.psum_tensor(f"y_ps{i}", [P, 512], F32)) for i in range(QT)]
        chain = sem("out_chain")
        a_ready, aT_full, aT_ready, y_full = sem("a_ready"), sem("aT_full"), sem("aT_ready"), sem("y_full")
        block = ctx.enter_context(nc.Block())

        @block.sync
        def _(sp):
            for i, (dst, src) in enumerate((("awq", "aWq"), ("awkv", "aWkv"), ("awo", "aWo"))):
                sp.dma_start(S[dst][:], A[src].rearrange("(j p) n -> p j n", p=P)).then_inc(S["aw_ld"][i], 16)
            sp.dma_start(S["abo"][:], A["abo"].rearrange("(a d) -> a d", a=1).to_broadcast([P, D])
                         ).then_inc(S["abo_ld"], 16)

        @block.vector
        def _(dve):
            n = [0]

            def link(ins):
                n[0] += 1
                ins.then_inc(chain, 1)
                dve.wait_ge(chain, n[0])

            link(dve.reciprocal(l_inv[:], S["l"][:]))
            dve.wait_ge(S["out_ld"], 48)
            for t in range(QT):
                link(dve.tensor_tensor(a[:, t, :].rearrange("p (h d) -> p h d", h=H), S["o"][:, t, :, :],
                                       l_inv[:, :, t:t + 1].to_broadcast([P, H, HD]), ALU.mult))
                dve.tensor_tensor(a[:, t, :], a[:, t, :], bv[:], ALU.add).then_inc(a_ready, 1)
            for t in range(QT):
                link(dve.tensor_tensor(S["x"][:, t, :], S["x"][:, t, :], bo[:], ALU.add))
            for i in range(2):
                dve.wait_ge(aT_full, i + 1)
                dve.tensor_copy(aT[:, 2 * i:2 * i + 2, :], aT_ps[i][:].rearrange("p (j q) -> p j q", j=2)
                                ).then_inc(aT_ready, 1)
            for t in range(QT):
                dve.wait_ge(y_full, t + 1)
                link(dve.tensor_tensor(S["x"][:, t, :], S["x"][:, t, :], y_ps[t][:], ALU.add))

        @block.tensor
        def _(pe):
            hold_clock(pe, S, y_ps[0], 32)
            pe.wait_ge(a_ready, QT)
            for i in range(2):
                for j in (2 * i, 2 * i + 1):
                    for t in range(QT):
                        at = (j % 2) * NQ + t * P
                        last = pe.transpose(aT_ps[i][:, at:at + P], a[:, t, bass.ts(j, P)], S["ident"][:])
                last.then_inc(aT_full, 1)
            pe.wait_ge(S["out_ld"], 48)
            pe.wait_ge(aT_ready, 2)
            for t in range(QT):
                for j in range(DB):
                    last = pe.matmul(y_ps[t][:], aT[:, j, bass.ts(t, P)], wo[:, j, :],
                                     start=(j == 0), stop=(j == DB - 1))
                last.then_inc(y_full, 1)


class Banks:

    def __init__(self, nc, ctx, name, count, order, looped=False):
        self.bank = [ctx.enter_context(nc.psum_tensor(f"{name}{b}", [P, 512], F32)) for b in range(count)]
        self.full = [ctx.enter_context(nc.semaphore(f"{name}_full{b}")) for b in range(count)]
        self.free = [ctx.enter_context(nc.semaphore(f"{name}_free{b}")) for b in range(count)]
        self.at = {key: (i % count, i // count) for i, key in enumerate(order)}
        assert len(self.at) == len(order)
        self.rounds = len(order) // count
        self.credit = self.rounds if looped else 0

    def __getitem__(self, key):
        return self.bank[self.at[key][0]]

    def give_credit(self, eng):
        for s in self.full + self.free:
            eng.sem_inc(s, self.credit)

    def wait_free(self, pe, key, j=0):
        b, use = self.at[key]
        value = use + self.rounds * j + self.credit
        if not isinstance(value, int) or value > 0:
            pe.wait_ge(self.free[b], value)

    def wait_full(self, eng, key, j=0):
        b, use = self.at[key]
        eng.wait_ge(self.full[b], use + 1 + self.rounds * j + self.credit)

    def wait_full_before(self, eng, key, j):
        b, use = self.at[key]
        eng.wait_ge(self.full[b], use + 1 + self.rounds * j)

    def wait_read(self, eng, key, j=0):
        b, use = self.at[key]
        eng.wait_ge(self.free[b], use + 1 + self.rounds * j + self.credit)

    def is_full(self, ins, key):
        ins.then_inc(self.full[self.at[key][0]], 1)

    def is_free(self, ins, key):
        ins.then_inc(self.free[self.at[key][0]], 1)


def self_attention(nc, A, S):
    WB = AW // P
    EPS = 1e-8
    AHEAD_S = 2
    first = [("q", 0), ("k", 0)]
    second = [("v", 0), ("v", 2), ("q", 1)]
    beside = {0: [("k", 1)], 2: [("q", 2)], 4: [("k", 2)], 6: [("v", 1)], 7: [("v", 3)], 8: [("q", 3)],
              10: [("k", 3)], 11: [("aT", 0)], 12: [("y", 0)], 13: [("aT", 1)], 14: [("y", 1)]}
    with ExitStack() as ctx:
        def sb(name, shape, dt=F32):
            return ctx.enter_context(nc.sbuf_tensor(name, shape, dt))

        def sem(name):
            return ctx.enter_context(nc.semaphore(name))

        wq, wkv, wo, bo = S["awq"], S["awkv"], S["awo"], S["abo"]
        stats = sb("a_stats", [P, QT, 6])
        mv = sb("a_mv", [P, QT, 2])
        veps = sb("a_veps", [P, QT])
        std = sb("a_std", [P, QT])
        rstd = sb("a_rstd", [P, QT])
        xn = sb("a_xn", [P, QT, D])
        xnT = sb("a_xnT", [P, DB, NQ])
        q_pad = sb("a_q", [P, H, NQ])
        kT = sb("a_kT", [P, WB, NQ])
        v = sb("a_v", [P, QT, AW])
        causal = sb("causal", [P, QT, NQ])
        mx = sb("a_max", [P, H, QT])
        mneg = sb("a_mneg", [P, H, QT])
        e = sb("a_e", [P, 2, QT, NQ])
        p = sb("a_p", [P, 2, QT, NQ])
        den = sb("a_den", [P, H, QT])
        den_eps = sb("a_den_eps", [P, H, QT])
        rden = sb("a_rden", [P, H, QT])
        pT = sb("a_pT", [P, 2, 3 * P])
        a = sb("a_a", [P, QT, AW])
        aT = sb("a_aT", [P, WB, NQ])

        order = [("xnT", i) for i in range(2)] + first + [("s", h) for h in range(AHEAD_S)] + second
        for h in range(H):
            order += [item for item in beside.get(h, []) if item[0] != "y"]
            order += ([("s", h + AHEAD_S)] if h + AHEAD_S < H else []) + [("pT", h)] + ([("o", h - 1)] if h else [])
        order += [("o", H - 1), ("aT", 2), ("aT", 3)]
        ps = Banks(nc, ctx, "a_ps", 6, order)
        y_ps = [ctx.enter_context(nc.psum_tensor(f"a_y_ps{t}", [P, D], F32)) for t in range(QT)]

        chain = sem("a_chain")
        causal_set, q_zero = sem("causal_set"), sem("q_zero")
        var_ready, std_ready, xn_ready = sem("a_var_ready"), sem("a_std_ready"), sem("a_xn_ready")
        m_ready, p_ready = sem("a_m_ready"), sem("a_p_ready")
        y_full = sem("a_y_full")
        block = ctx.enter_context(nc.Block())

        @block.sync
        def _(sp):
            preload_moe(A, S, sp)

        @block.gpsimd
        def _(pool):
            pool.memset(q_pad[:], 0.0).then_inc(q_zero, 1)
            pool.memset(causal[:], 1.0).then_inc(causal_set, 1)
            pool.wait_ge(causal_set, 1)
            for t in range(QT):
                pool.affine_select(out=causal[:, t, :], in_=causal[:, t, :], compare_op=ALU.is_ge, fill=0.0,
                                   base=t * P, pattern=[[-1, NQ]], channel_multiplier=1).then_inc(causal_set, 1)

        @block.scalar
        def _(act):
            act.wait_ge(var_ready, 1)
            nc.scalar.activation(std[:], veps[:], ACT.Sqrt).then_inc(std_ready, 1)

            def take(items):
                for kind, i in items:
                    if kind not in ("q", "v", "aT"):
                        continue
                    ps.wait_full(act, (kind, i))
                    bank = ps[kind, i]
                    if kind == "q":
                        for r in range(2):
                            rows = slice(ADH * r, ADH * (r + 1))
                            ins = nc.scalar.activation(q_pad[rows, 4 * i + r:4 * i + r + 3:2, :],
                                                       bank[rows].rearrange("p (b q) -> p b q", b=2), ACT.Copy,
                                                       scale=ADH ** -0.5)
                    elif kind == "v":
                        ins = nc.scalar.activation(v[:, i // 2, bass.ts(i % 2, D)], bank[:], ACT.Copy)
                    else:
                        ins = nc.scalar.activation(aT[:, 2 * i:2 * i + 2, :],
                                                   bank[:].rearrange("p (j q) -> p j q", j=2), ACT.Copy)
                    ps.is_free(ins, (kind, i))

            def exponentials(h):
                act.wait_ge(m_ready, h + 1)
                if h >= 2:
                    act.wait_ge(p_ready, QT * (h - 1))
                for t in range(QT):
                    ins = nc.scalar.activation(e[:, h % 2, t, :], ps["s", h][:, t * NQ:(t + 1) * NQ], ACT.Exp,
                                               bias=mneg[:, h, t:t + 1])
                ps.is_free(ins, ("s", h))

            def copy_pT(h):
                ps.wait_full(act, ("pT", h))
                if h >= 2:
                    ps.wait_full(act, ("o", h - 2))
                ins = nc.scalar.activation(pT[:, h % 2, :], ps["pT", h][:, 0:3 * P], ACT.Copy)
                ps.is_free(ins, ("pT", h))

            act.wait_ge(q_zero, 1)
            take(first)
            exponentials(0)
            take(second)
            for h in range(H):
                if h + 1 < H:
                    exponentials(h + 1)
                take(beside.get(h, []))
                if h:
                    copy_pT(h - 1)
            copy_pT(H - 1)
            take([("aT", 2), ("aT", 3)])

        @block.vector
        def _(dve):
            n = [0]

            def link(ins):
                n[0] += 1
                ins.then_inc(chain, 1)
                dve.wait_ge(chain, n[0])

            for t in range(QT):
                link(dve.bn_stats(stats[:, t, :], S["x"][:, t, :]))
                link(dve.bn_aggr(mv[:, t, :], stats[:, t, :]))
            dve.tensor_scalar(veps[:], mv[:, :, 1], LN_EPS, None, ALU.add).then_inc(var_ready, 1)
            dve.wait_ge(std_ready, 1)
            link(dve.reciprocal(rstd[:], std[:]))
            for t in range(QT):
                dve.tensor_scalar(xn[:, t, :], S["x"][:, t, :], mv[:, t, 0:1], rstd[:, t:t + 1],
                                  ALU.subtract, ALU.mult).then_inc(xn_ready, 1)

            def take(key, dst):
                ps.wait_full(dve, key)
                ps.is_free(dve.tensor_copy(dst, ps[key][:].rearrange("p (j q) -> p j q", j=2)), key)

            def take_keys(items):
                for kind, i in items:
                    if kind == "k":
                        take((kind, i), kT[:, 2 * i:2 * i + 2, :])

            def maximum(h):
                ps.wait_full(dve, ("s", h))
                link(dve.tensor_reduce(mx[:, h, :], ps["s", h][:].rearrange("p (t k) -> p t k", t=QT), AX_X, ALU.max))
                dve.tensor_scalar(mneg[:, h, :], mx[:, h, :], -1.0, None, ALU.mult).then_inc(m_ready, 1)

            def mask(h):
                ps.wait_read(dve, ("s", h))
                if h >= 2:
                    ps.wait_full(dve, ("pT", h - 2))
                for t in range(QT):
                    dve.tensor_tensor_reduce(p[:, h % 2, t, :], e[:, h % 2, t, :], causal[:, t, :], 1.0, 0.0,
                                             ALU.mult, ALU.add, den[:, h, t:t + 1]).then_inc(p_ready, 1)

            def normalise(h):
                link(dve.tensor_scalar(den_eps[:, h, :], den[:, h, :], EPS, None, ALU.add))
                link(dve.reciprocal(rden[:, h, :], den_eps[:, h, :]))
                ps.wait_full(dve, ("o", h))
                for t in range(QT):
                    ins = dve.tensor_scalar(a[:, t, bass.ts(h, ADH)], ps["o", h][:, bass.ts(t, ADH)],
                                            rden[:, h, t:t + 1], None, ALU.mult)
                ps.is_free(ins, ("o", h))

            for i in range(2):
                take(("xnT", i), xnT[:, 2 * i:2 * i + 2, :])
            dve.wait_ge(S["abo_ld"], 16)
            for t in range(QT):
                link(dve.tensor_tensor(S["x"][:, t, :], S["x"][:, t, :], bo[:], ALU.add))
            take_keys(first)
            dve.wait_ge(causal_set, 1 + QT)
            for h in range(AHEAD_S):
                maximum(h)
            take_keys(second)
            for h in range(H):
                mask(h)
                take_keys(beside.get(h, []))
                if h + AHEAD_S < H:
                    maximum(h + AHEAD_S)
                if h >= 2:
                    dve.wait_ge(p_ready, QT * (h - 1))
                    normalise(h - 2)
            dve.wait_ge(p_ready, QT * H)
            normalise(H - 2)
            normalise(H - 1)
            for t in range(QT):
                dve.wait_ge(y_full, t + 1)
                link(dve.tensor_tensor(S["x"][:, t, :], S["x"][:, t, :], y_ps[t][:], ALU.add))

        @block.tensor
        def _(pe):
            def turn(key, src):
                ps.wait_free(pe, key)
                for j in range(2):
                    for t in range(QT):
                        at = j * NQ + t * P
                        last = pe.transpose(ps[key][:, at:at + P], src[:, t, bass.ts(2 * key[1] + j, P)],
                                            S["ident"][:])
                ps.is_full(last, key)

            def project(kind, i):
                ps.wait_free(pe, (kind, i))
                if kind == "v":
                    for j in range(DB):
                        last = pe.matmul(ps["v", i][:], xnT[:, j, bass.ts(i // 2, P)],
                                         wkv[:, j, AW + (i % 2) * D:AW + (i % 2 + 1) * D],
                                         start=(j == 0), stop=(j == DB - 1))
                else:
                    w = wq if kind == "q" else wkv
                    for b in range(2):
                        for j in range(DB):
                            last = pe.matmul(ps[kind, i][:, bass.ts(b, NQ)], w[:, j, bass.ts(2 * i + b, P)],
                                             xnT[:, j, :], start=(j == 0), stop=(j == DB - 1))
                ps.is_full(last, (kind, i))

            def output(i):
                ps.wait_read(pe, ("aT", i))
                for t in range(QT):
                    for j in (2 * i, 2 * i + 1):
                        last = pe.matmul(y_ps[t][:], aT[:, j, bass.ts(t, P)], wo[:, j, :],
                                         start=(j == 0), stop=(j == WB - 1))
                    if j == WB - 1:
                        last.then_inc(y_full, 1)

            def work(items):
                for kind, i in items:
                    if kind == "aT":
                        ps.wait_read(pe, ("o", 4 * i + 3))
                        turn((kind, i), a)
                    elif kind == "y":
                        output(i)
                    else:
                        project(kind, i)

            def scores(h):
                ps.wait_free(pe, ("s", h))
                if h % 4 == 0:
                    ps.wait_read(pe, ("q", h // 4))
                    ps.wait_read(pe, ("k", h // 4))
                for t in range(QT):
                    last = pe.matmul(ps["s", h][:, bass.ts(t, NQ)], q_pad[:, h, bass.ts(t, P)], kT[:, h // 2, :],
                                     start=True, stop=True)
                ps.is_full(last, ("s", h))

            def turn_probabilities(h):
                ps.wait_free(pe, ("pT", h))
                pe.wait_ge(p_ready, QT * (h + 1))
                for i, (t, b) in enumerate(((0, 0), (1, 0), (1, 1))):
                    last = pe.transpose(ps["pT", h][:, bass.ts(i, P)], p[:, h % 2, t, bass.ts(b, P)], S["ident"][:])
                ps.is_full(last, ("pT", h))

            def values(h):
                ps.wait_free(pe, ("o", h))
                ps.wait_read(pe, ("pT", h))
                if h % 8 == 0:
                    ps.wait_read(pe, ("v", h // 8))
                    ps.wait_read(pe, ("v", 2 + h // 8))
                for t in range(QT):
                    for b in range(t + 1):
                        last = pe.matmul(ps["o", h][:, bass.ts(t, ADH)], pT[:, h % 2, bass.ts(t + b, P)],
                                         v[:, b, bass.ts(h, ADH)], start=(b == 0), stop=(b == t))
                ps.is_full(last, ("o", h))

            hold_clock(pe, S, y_ps[0], 32)
            pe.wait_ge(xn_ready, QT)
            for i in range(2):
                turn(("xnT", i), xn)
            ps.wait_read(pe, ("xnT", 0))
            ps.wait_read(pe, ("xnT", 1))
            pe.wait_ge(S["aw_ld"][0], 16)
            pe.wait_ge(S["aw_ld"][1], 16)
            work(first)
            for h in range(AHEAD_S):
                scores(h)
            work(second)
            pe.wait_ge(S["aw_ld"][2], 16)
            for h in range(H):
                work(beside.get(h, []))
                if h + AHEAD_S < H:
                    scores(h + AHEAD_S)
                turn_probabilities(h)
                if h:
                    values(h - 1)
            values(H - 1)
            work([("aT", 2), ("y", 2), ("aT", 3), ("y", 3)])


MOE_BUFFERS = 4


def moe_matrix(E, kind, u):
    return (kind, u if kind == "up" else min(u, E))


def moe_order(E):
    U = E + 2
    ops = []
    for i in range(U + 2):
        ops += [("up", i)] if i < U else []
        ops += [("down", i - 2)] if 0 <= i - 2 and i - 2 != U - 2 else []
        ops += [("g", i - 1)] if 0 <= i - 1 < U else []
    matrices, last_use = [], {}
    for kind, u in ops:
        m = moe_matrix(E, kind, u)
        if m not in matrices:
            matrices.append(m)
        last_use[m] = (kind, u, 1)
    return ops, matrices, last_use


def moe_weights(A, m):
    kind, u = m
    E = A["rb"].shape[1]
    if kind == "up":
        w = A["eWup"][u] if u < E else A["sWup"][:, (u - E) * D:(u - E + 1) * D]
    elif kind == "g":
        w = A["eWg"][u] if u < E else A["sWg"]
    else:
        w = A["eWdown"][u] if u < E else A["sWdown"]
    return w.rearrange("(j p) n -> p j n", p=P)


def moe_bias_rows(E):
    return 2 * E * DB + 3 * DB


def preload_moe(A, S, sp):
    layers, E = A["rb"].shape

    def load(i):
        sp.dma_start(S["m_w"][:, i, :, :], moe_weights(A, moe_order(E)[1][i])).then_inc(S["m_w_ld"][i], 16)

    load(0)
    row = 0
    for name, pat, count in (("ebup", "e (i p) -> (e i) p", E * DB), ("ebg", "e (i p) -> (e i) p", E * DB),
                             ("sbup", "(i p) -> i p", 2 * DB), ("sbg", "(i p) -> i p", DB)):
        sp.dma_start(S["bias_rows"][row:row + count, :], A[name].rearrange(pat, p=P)).then_inc(S["m_bias_ld"], 16)
        row += count
    for layer in range(layers):
        sp.dma_start(S["rw"][:, layer, :, :], A["rW"][layer].rearrange("(j p) e -> p j e", p=P)
                     ).then_inc(S["m_small_ld"], 16)
    for name, width in (("rb", E), ("gb", E), ("nw", D)):
        flat = A[name].rearrange("(a l) e -> a l e", a=1)
        sp.dma_start(S[name][:], flat.to_broadcast([P, layers, width])).then_inc(S["m_small_ld"], 16)
    sp.dma_start(S["bdown"][0:E, :], A["ebdown"]).then_inc(S["m_small_ld"], 16)
    sp.dma_start(S["bdown"][E:E + 1, :], A["sbdown"].rearrange("(a d) -> a d", a=1)).then_inc(S["m_small_ld"], 16)
    for i in range(1, MOE_BUFFERS):
        load(i)


def moe(nc, A, S):
    LAYERS, E = A["rb"].shape
    RMS_EPS = 1e-6
    FAR = 1e30
    U = E + 2
    WR = MOE_BUFFERS
    WS = 4
    POOL = 2
    NB = 6
    BUP, BG, SBUP, SBG = 0, E * DB, 2 * E * DB, 2 * E * DB + 2 * DB
    NBIAS = moe_bias_rows(E)
    assert NBIAS <= P

    ops, matrices, last_use = moe_order(E)
    GATE_AT, TURN_AT, MIX_AT = 1, 2, 3
    order = [("xT", i) for i in range(2)]
    for i, (kind, u) in enumerate(ops):
        if i == GATE_AT:
            order += [("gate", t) for t in range(QT)]
        if i == TURN_AT:
            order += [("wT", t) for t in range(QT)]
        if i == MIX_AT:
            order += [("bd", t) for t in range(QT)]
        order += [(kind, u, t) for t in range(2)]
    NM = len(matrices)

    def matrix_no(i):
        return matrices.index(moe_matrix(E, *ops[i]))

    def new_matrix(i):
        return i < len(ops) and matrix_no(i) not in [matrix_no(k) for k in range(i)]

    assert len(order) % NB == 0

    with ExitStack() as ctx:
        def sb(name, shape, dt=F32):
            return ctx.enter_context(nc.sbuf_tensor(name, shape, dt))

        def sem(name):
            return ctx.enter_context(nc.semaphore(name))

        w_sb, bias_rows, bdown = S["m_w"], S["bias_rows"], S["bdown"]
        rw, rb, gb, nw = S["rw"], S["rb"], S["gb"], S["nw"]
        w_hi = sb("m_w_hi", [P, WS, DB, D], F32R)
        w_lo = sb("m_w_lo", [P, WS, DB, D], F32R)
        bias = sb("bias_cols", [P, NBIAS])
        earlier = sb("earlier", [P, E, E])
        stats = sb("m_stats", [P, QT, 6])
        mv = sb("m_mv", [P, QT, 2])
        veps = sb("m_veps", [P, QT])
        std = sb("m_std", [P, QT])
        rstd = sb("m_rstd", [P, QT])
        xf = sb("xf", [P, QT, D])
        xfT = sb("xfT", [P, DB, NQ])
        acc = sb("acc", [P, QT, D])
        square = sb("square", [P, QT, D])
        sq_sum = sb("sq_sum", [P, QT])
        x_hi = sb("x_hi", [P, DB, NQ], F32R)
        x_lo = sb("x_lo", [P, DB, NQ], F32R)
        hT = sb("hT", [P, 2, DB, NQ])
        h_hi = sb("h_hi", [P, 2, DB, NQ], F32R)
        h_lo = sb("h_lo", [P, 2, DB, NQ], F32R)
        sT = sb("sT", [P, DB, NQ])
        aT = sb("m_aT", [P, 2, DB, NQ])
        a_hi = sb("a_hi", [P, DB, NQ], F32R)
        a_lo = sb("a_lo", [P, DB, NQ], F32R)
        gate = sb("gate", [P, QT, E])
        biased = sb("biased", [P, QT, E])
        above = sb("above", [P, QT, E, E])
        ties = sb("ties", [P, QT, E, E])
        rank = sb("rank", [P, QT, E])
        sel = sb("sel", [P, QT, E])
        far = sb("far", [P, QT, E])
        gate_max = sb("gate_max", [P, QT])
        e_sum = sb("e_sum", [P, QT])
        e_gate = sb("e_gate", [P, QT, E])
        wt = sb("wt", [P, QT, E + 1])
        wT = sb("wT", [E + 1, QT, P])

        ps = Banks(nc, ctx, "m_ps", NB, order, looped=True)
        bias_ps = ctx.enter_context(nc.psum_tensor("bias_ps", [P, 512], F32))
        scratch = ctx.enter_context(nc.psum_tensor("m_scratch", [P, 512], F32))
        w_ld, bias_ld, small_ld = S["m_w_ld"], S["m_bias_ld"], S["m_small_ld"]
        consts, bias_full, bias_ready = sem("m_consts"), sem("bias_full"), sem("bias_ready")
        chain = sem("m_chain")
        var_ready, std_ready = sem("m_var_ready"), sem("m_std_ready")
        xf_ready = sem("xf_ready")
        far_ready, gate_e = sem("far_ready"), sem("gate_e")
        wt_ready = sem("wt_ready")
        x_hi_done = sem("x_hi_done")
        x_lo_done = sem("x_lo_done")
        w_hi_done = sem("w_hi_done")
        w_lo_done, w_lo_pool = sem("w_lo_done"), sem("w_lo_pool")
        h_hi_done, h_lo_done = sem("h_hi_done"), sem("h_lo_done")
        a_done, a_split = sem("m_a_done"), sem("a_split")
        block = ctx.enter_context(nc.Block())

        def wait_lo(eng, layer, m):
            if m < POOL:
                eng.wait_ge(w_lo_pool, POOL * layer + m + 1)
            else:
                eng.wait_ge(w_lo_done, (NM - POOL) * layer + m - POOL + 1)

        @block.sync
        def _(sp):
            def load(layer, i):
                before = [q for q in range(layer * NM + i) if q % NM % WR == i % WR]
                if before:
                    wait_lo(sp, before[-1] // NM, before[-1] % NM)
                sp.dma_start(w_sb[:, i % WR, :, :], moe_weights(A, matrices[i])).then_inc(w_ld[i % WR], 16)

            ps.give_credit(sp)
            sp.sem_inc(a_done, 1)
            for layer in range(LAYERS):
                for i in range(NM):
                    if layer or i >= WR:
                        load(layer, i)

        SMALL = 16 * (LAYERS + 5)

        @block.gpsimd
        def _(pool):
            pool.memset(wt[:], 2.0).then_inc(consts, 1)
            pool.memset(earlier[:], 1.0).then_inc(consts, 1)
            pool.wait_ge(consts, 2)
            pool.affine_select(out=earlier[:], in_=earlier[:], compare_op=ALU.is_gt, fill=0.0, base=0,
                               pattern=[[1, E], [-1, E]], channel_multiplier=0).then_inc(consts, 1)
            with pool.Fori(0, LAYERS) as j:
                for m in range(POOL):
                    pool.wait_ge(w_hi_done, NM * j + m + 1)
                    pool.tensor_tensor(w_lo[:, m % WS, :, :], w_sb[:, m % WR, :, :],
                                       w_hi[:, m % WS, :, :].bitcast(F32), ALU.subtract).then_inc(w_lo_pool, 1)

        def bias_column(kind, u, b):
            if kind == "up":
                at = BUP + u * DB + b if u < E else SBUP + (u - E) * DB + b
            else:
                at = BG + u * DB + b if u < E else SBG + b
            return bias[:, at:at + 1]

        @block.scalar
        def _(act):
            def root(value):
                act.wait_ge(var_ready, value)
                nc.scalar.activation(std[:], veps[:], ACT.Sqrt).then_inc(std_ready, 1)

            def split_weights(j, m):
                act.wait_ge(w_ld[m % WR], 16 * (len(range(m % WR, NM, WR)) * j + m // WR + 1))
                if m >= WS:
                    ps.wait_full(act, last_use[matrices[m - WS]], j)
                else:
                    ps.wait_full_before(act, last_use[matrices[max(range(m, NM, WS))]], j)
                nc.scalar.activation(w_hi[:, m % WS, :, :], w_sb[:, m % WR, :, :], ACT.Copy).then_inc(w_hi_done, 1)

            with act.Fori(0, LAYERS) as j:
                split_weights(j, 0)
                root(j + 1)
                for i in range(2):
                    ps.wait_full(act, ("xT", i), j)
                    src = ps["xT", i][:].rearrange("p (j q) -> p j q", j=2)
                    nc.scalar.activation(x_hi[:, 2 * i:2 * i + 2, :], src, ACT.Copy).then_inc(x_hi_done, 1)
                split_weights(j, 1)
                act.wait_ge(bias_ready, 1)
                for i, (kind, u) in enumerate(ops):
                    if i == GATE_AT:
                        act.wait_ge(far_ready, j + 1)
                        for t in range(QT):
                            nc.scalar.activation(e_gate[:, t, :], far[:, t, :], ACT.Exp, bias=gate_max[:, t:t + 1],
                                                 accum_out=e_sum[:, t:t + 1]).then_inc(gate_e, 1)
                    if new_matrix(i + 2):
                        split_weights(j, matrix_no(i + 2))
                    if kind == "up":
                        act.wait_ge(a_done, U * j + max(0, u - 1) + 1)
                    elif kind == "g":
                        act.wait_ge(a_done, U * j + u + 1)
                    else:
                        continue
                    for tile in range(2):
                        ps.wait_full(act, (kind, u, tile), j)
                        for r in range(2):
                            b = 2 * tile + r
                            dst = hT[:, u % 2, b, :] if kind == "up" else sT[:, b, :]
                            ins = nc.scalar.activation(dst, ps[kind, u, tile][:, bass.ts(r, NQ)],
                                                       ACT.Identity if kind == "up" else ACT.Silu,
                                                       bias=bias_column(kind, u, b))
                        ps.is_free(ins, (kind, u, tile))
                    if kind == "up":
                        ps.wait_read(act, ("up", u, 1), j)
                        if u >= 2:
                            ps.wait_full(act, ("g", u - 2, 1), j)
                        nc.scalar.activation(h_hi[:, u % 2, :, :], hT[:, u % 2, :, :], ACT.Copy
                                             ).then_inc(h_hi_done, 1)
            root(LAYERS + 1)

        @block.vector
        def _(dve):
            n = [0]
            base = [0]

            def link(ins):
                n[0] += 1
                ins.then_inc(chain, 1)
                dve.wait_ge(chain, base[0] + n[0])

            for t in range(QT):
                link(dve.bn_stats(stats[:, t, :], S["x"][:, t, :]))
                link(dve.bn_aggr(mv[:, t, :], stats[:, t, :]))
            dve.tensor_scalar(veps[:], mv[:, :, 1], LN_EPS, None, ALU.add).then_inc(var_ready, 1)
            dve.wait_ge(std_ready, 1)
            link(dve.reciprocal(rstd[:], std[:]))
            for t in range(QT):
                dve.tensor_scalar(xf[:, t, :], S["x"][:, t, :], mv[:, t, 0:1], rstd[:, t:t + 1],
                                  ALU.subtract, ALU.mult).then_inc(xf_ready, 1)
            dve.wait_ge(bias_full, 1)
            dve.tensor_copy(bias[:], bias_ps[:, 0:NBIAS]).then_inc(bias_ready, 1)
            dve.wait_ge(small_ld, SMALL)
            dve.wait_ge(consts, 3)
            before = n[0]
            n[0] = 0

            def router(j):
                one = bass.ds(j, 1)
                for t in range(QT):
                    ps.wait_full(dve, ("gate", t), j)
                    ps.is_free(dve.tensor_tensor(gate[:, t:t + 1, :], ps["gate", t][:, 0:E].rearrange(
                        "p (a e) -> p a e", a=1), rb[:, one, :], ALU.add), ("gate", t))
                ps.wait_read(dve, ("gate", QT - 1), j)
                for t in range(QT):
                    link(dve.tensor_tensor(biased[:, t:t + 1, :], gate[:, t:t + 1, :], gb[:, one, :], ALU.add))
                for t in range(QT):
                    other = biased[:, t:t + 1, :].to_broadcast([P, E, E])
                    own = biased[:, t, :].rearrange("p (e a) -> p e a", a=1).to_broadcast([P, E, E])
                    link(dve.tensor_tensor(above[:, t, :, :], other, own, ALU.is_gt))
                    link(dve.tensor_tensor(ties[:, t, :, :], other, own, ALU.is_equal))
                    link(dve.tensor_tensor(ties[:, t, :, :], ties[:, t, :, :], earlier[:], ALU.mult))
                link(dve.tensor_tensor(above[:], above[:], ties[:], ALU.add))
                link(dve.tensor_reduce(rank[:], above[:], AX_X, ALU.add))
                link(dve.tensor_scalar(sel[:], rank[:], 1.5, None, ALU.is_lt))
                link(dve.tensor_scalar(far[:], sel[:], 1.0, FAR, ALU.subtract, ALU.mult))
                link(dve.tensor_tensor(sel[:], sel[:], gate[:], ALU.mult))
                link(dve.tensor_tensor(far[:], far[:], sel[:], ALU.add))
                link(dve.tensor_reduce(gate_max[:], far[:], AX_X, ALU.max))
                dve.tensor_scalar(gate_max[:], gate_max[:], -1.0, None, ALU.mult).then_inc(far_ready, 1)

            def weights(j):
                dve.wait_ge(gate_e, QT * j + QT)
                link(dve.reciprocal(e_sum[:], e_sum[:]))
                for t in range(QT):
                    dve.tensor_scalar(wt[:, t, 0:E], e_gate[:, t, :], e_sum[:, t:t + 1], None, ALU.mult
                                      ).then_inc(wt_ready, 1)

            def copy_weights(j):
                for t in range(QT):
                    ps.wait_full(dve, ("wT", t), j)
                    ps.is_free(dve.tensor_copy(wT[:, t, :], ps["wT", t][0:E + 1, 0:P]), ("wT", t))

            def first_sum(j):
                for t in range(QT):
                    ps.wait_full(dve, ("bd", t), j)
                    ps.is_free(dve.tensor_tensor(acc[:, t, :], xf[:, t, :], ps["bd", t][:], ALU.add), ("bd", t))

            def split_weights(j, m):
                dve.wait_ge(w_hi_done, NM * j + m + 1)
                dve.tensor_tensor(w_lo[:, m % WS, :, :], w_sb[:, m % WR, :, :], w_hi[:, m % WS, :, :].bitcast(F32),
                                  ALU.subtract).then_inc(w_lo_done, 1)

            def split_h(j, u):
                dve.wait_ge(h_hi_done, U * j + u + 1)
                dve.tensor_tensor(h_lo[:, u % 2, :, :], hT[:, u % 2, :, :], h_hi[:, u % 2, :, :].bitcast(F32),
                                  ALU.subtract).then_inc(h_lo_done, 1)

            def gated(j, u):
                if u == U - 1:
                    for tile in range(2):
                        two = slice(2 * tile, 2 * tile + 2)
                        ps.wait_read(dve, ("g", u, tile), j)
                        ins = dve.tensor_tensor(aT[:, 1, two, :], sT[:, two, :], hT[:, 1, two, :], ALU.mult)
                        if tile == 0:
                            link(ins)
                            ps.wait_full(dve, ("down", E - 1, 1), j)
                        else:
                            ins.then_inc(a_done, 1)
                            dve.wait_ge(a_done, U * j + u + 2)
                        link(dve.tensor_tensor(aT[:, 1, two, :], aT[:, 1, two, :], aT[:, 0, two, :], ALU.add))
                        link(dve.tensor_copy(a_hi[:, two, :], aT[:, 1, two, :]))
                        ins = dve.tensor_tensor(a_lo[:, two, :], aT[:, 1, two, :], a_hi[:, two, :].bitcast(F32),
                                                ALU.subtract)
                        if tile == 0:
                            link(ins)
                        else:
                            ins.then_inc(a_split, 1)
                    return
                ps.wait_read(dve, ("g", u, 0), j)
                ps.wait_read(dve, ("g", u, 1), j)
                dve.tensor_tensor(aT[:, u % 2, :, :], sT[:], hT[:, u % 2, :, :], ALU.mult).then_inc(a_done, 1)
                dve.wait_ge(a_done, U * j + u + 2)
                if u == U - 2:
                    return
                if u:
                    ps.wait_full(dve, ("down", u - 1 if u < E else E - 1, 1), j)
                link(dve.tensor_copy(a_hi[:], aT[:, u % 2, :, :]))
                dve.tensor_tensor(a_lo[:], aT[:, u % 2, :, :], a_hi[:].bitcast(F32), ALU.subtract
                                  ).then_inc(a_split, 1)

            def accumulate(j, u, tiles=range(QT)):
                for t in tiles:
                    key = ("down", u, t)
                    ps.wait_full(dve, key, j)
                    if u == 0:
                        ps.wait_read(dve, ("bd", t), j)
                    else:
                        ps.wait_read(dve, ("down", u - 1 if u < E else E - 1, t), j)
                    if u < E:
                        ins = dve.scalar_tensor_tensor(out=acc[:, t, :], in0=ps[key][:], scalar=wt[:, t, u:u + 1],
                                                       in1=acc[:, t, :], op0=ALU.mult, op1=ALU.add)
                    else:
                        ins = dve.tensor_tensor(acc[:, t, :], acc[:, t, :], ps[key][:], ALU.add)
                    ps.is_free(ins, key)

            LINKS = 23 + U
            with dve.Fori(0, LAYERS) as j:
                base[0] = LINKS * j + before
                for i in range(2):
                    two = slice(2 * i, 2 * i + 2)
                    dve.wait_ge(x_hi_done, 2 * j + i + 1)
                    dve.tensor_tensor(x_lo[:, two, :], ps["xT", i][:].rearrange("p (j q) -> p j q", j=2),
                                      x_hi[:, two, :].bitcast(F32), ALU.subtract).then_inc(x_lo_done, 1)
                for i in range(2):
                    ps.is_free(dve.tensor_copy(xfT[:, 2 * i:2 * i + 2, :],
                                               ps["xT", i][:].rearrange("p (j q) -> p j q", j=2)), ("xT", i))
                for i, (kind, u) in enumerate(ops):
                    if i == GATE_AT:
                        router(j)
                        weights(j)
                    if i == TURN_AT:
                        copy_weights(j)
                    if i == MIX_AT:
                        first_sum(j)
                    if new_matrix(i + 2):
                        split_weights(j, matrix_no(i + 2))
                    if kind == "up":
                        split_h(j, u)
                    elif kind == "g":
                        gated(j, u)
                    elif kind == "down" and u < U - 1:
                        accumulate(j, u)
                for t in range(QT):
                    accumulate(j, U - 1, [t])
                    ps.wait_read(dve, ("down", U - 1, t), j)
                    link(dve.tensor_tensor_reduce(square[:, t, :], acc[:, t, :], acc[:, t, :], 1.0, 0.0, ALU.mult,
                                                  ALU.add, sq_sum[:, t:t + 1]))
                dve.tensor_scalar(veps[:], sq_sum[:], 1.0 / D, RMS_EPS, ALU.mult, ALU.add).then_inc(var_ready, 1)
                dve.wait_ge(std_ready, j + 2)
                link(dve.reciprocal(rstd[:], std[:]))
                for t in range(QT):
                    dve.scalar_tensor_tensor(out=xf[:, t:t + 1, :], in0=acc[:, t:t + 1, :], scalar=rstd[:, t:t + 1],
                                             in1=nw[:, bass.ds(j, 1), :], op0=ALU.mult, op1=ALU.mult
                                             ).then_inc(xf_ready, 1)
                assert n[0] == LINKS, n[0]
            dve.wait_ge(xf_ready, QT * (LAYERS + 1))
            for t in range(QT):
                n[0] += 1
                dve.tensor_tensor(S["x"][:, t, :], S["x"][:, t, :], xf[:, t, :], ALU.add)

        @block.tensor
        def _(pe):
            pe.wait_ge(bias_ld, 64)
            pe.transpose(bias_ps[:, 0:NBIAS], bias_rows[:], S["ident"][0:NBIAS, 0:NBIAS]).then_inc(bias_full, 1)
            pe.wait_ge(small_ld, SMALL)
            hold_clock(pe, S, scratch, 12)
            with pe.Fori(0, LAYERS) as j:
                hold_clock(pe, S, scratch, 30)
                pe.wait_ge(xf_ready, QT * j + QT)
                for i in range(2):
                    ps.wait_free(pe, ("xT", i), j)
                    for b in range(2):
                        for t in range(QT):
                            at = b * NQ + t * P
                            last = pe.transpose(ps["xT", i][:, at:at + P], xf[:, t, bass.ts(2 * i + b, P)],
                                                S["ident"][:])
                    ps.is_full(last, ("xT", i))

                def gates():
                    ps.wait_read(pe, ("xT", 0), j)
                    ps.wait_read(pe, ("xT", 1), j)
                    for t in range(QT):
                        ps.wait_free(pe, ("gate", t), j)
                        for b in range(DB):
                            last = pe.matmul(ps["gate", t][:, 0:E], xfT[:, b, bass.ts(t, P)],
                                             rw[:, bass.ds(j, 1), b, :].rearrange("p a e -> p (a e)"),
                                             start=(b == 0), stop=(b == DB - 1))
                        ps.is_full(last, ("gate", t))

                def turn_weights():
                    pe.wait_ge(wt_ready, QT * j + QT)
                    for t in range(QT):
                        ps.wait_free(pe, ("wT", t), j)
                        ps.is_full(pe.transpose(ps["wT", t][0:E + 1, 0:P], wt[:, t, :], S["ident"][:]), ("wT", t))

                def mix():
                    for t in range(QT):
                        ps.wait_free(pe, ("bd", t), j)
                        ps.wait_read(pe, ("wT", t), j)
                        ps.is_full(pe.matmul(ps["bd", t][:], wT[:, t, :], bdown[:], start=True, stop=True), ("bd", t))

                pe.wait_ge(x_lo_done, 2 * j + 2)
                for i, (kind, u) in enumerate(ops):
                    if i == GATE_AT:
                        gates()
                    if i == TURN_AT:
                        turn_weights()
                    if i == MIX_AT:
                        mix()
                    m = matrix_no(i)
                    wait_lo(pe, j, m)
                    whi, wlo = w_hi[:, m % WS, :, :], w_lo[:, m % WS, :, :]
                    if kind == "g":
                        pe.wait_ge(h_lo_done, U * j + u + 1)
                    if kind == "down":
                        if u == U - 1:
                            hold_clock(pe, S, scratch, 30)
                        pe.wait_ge(a_split, (U - 1) * j + (u + 1 if u < E else U - 1))
                    for tile in range(2):
                        ps.wait_free(pe, (kind, u, tile), j)
                        out = ps[kind, u, tile]
                        if kind == "down":
                            rows = bass.ts(tile, P)
                            for b in range(DB):
                                for s, (x, w) in enumerate(((a_hi, whi), (a_hi, wlo), (a_lo, whi))):
                                    last = pe.matmul(out[:], x[:, b, rows], w[:, b, :],
                                                     start=(b == 0 and s == 0), stop=(b == DB - 1 and s == 2))
                        else:
                            xh, xl = (x_hi, x_lo) if kind == "up" else (h_hi[:, u % 2, :, :], h_lo[:, u % 2, :, :])
                            for r in range(2):
                                cols = bass.ts(2 * tile + r, P)
                                for b in range(DB):
                                    for s, (w, x) in enumerate(((whi, xh), (whi, xl), (wlo, xh))):
                                        last = pe.matmul(out[:, bass.ts(r, NQ)], w[:, b, cols], x[:, b, :],
                                                         start=(b == 0 and s == 0), stop=(b == DB - 1 and s == 2))
                        ps.is_full(last, (kind, u, tile))


def store(nc, A, S):
    with ExitStack() as ctx:
        stored = ctx.enter_context(nc.semaphore("stored"))
        block = ctx.enter_context(nc.Block())

        @block.sync
        def _(sp):
            sp.dma_start(A["out"].rearrange("(t p) d -> p t d", p=P), S["x"][:]).then_inc(stored, 16)
            sp.wait_ge(stored, 16)


def program(nc, A, stages):
    with ExitStack() as ctx:
        S = {
            "x": ctx.enter_context(nc.sbuf_tensor("x_sb", [P, QT, D], F32)),
            "ident": ctx.enter_context(nc.sbuf_tensor("ident", [P, P], F32)),
            "mask_row": nc.dram_tensor("mask_row", [A["ctx"].shape[0]], F32, kind="Internal").ap(),
            "l": ctx.enter_context(nc.sbuf_tensor("l_run", [P, H, QT], F32)),
            "o": ctx.enter_context(nc.sbuf_tensor("o_run", [P, QT, H, HD], F32)),
            "wo": ctx.enter_context(nc.sbuf_tensor("wo", [P, DB, D], F32)),
            "bv": ctx.enter_context(nc.sbuf_tensor("bv", [P, D], F32)),
            "bo": ctx.enter_context(nc.sbuf_tensor("bo", [P, D], F32)),
            "out_ld": ctx.enter_context(nc.semaphore("out_ld")),
        }
        for stage in stages:
            stage(nc, A, S)


def context_attention(nc, A, S):
    with ExitStack() as ctx:
        def sb(name, shape, dt=F32):
            return ctx.enter_context(nc.sbuf_tensor(name, shape, dt))

        S = S | {
            "bk": sb("bk_sb", [P, NG]),
            "q_stack": sb("q_stack", [P, H, NQ], F32R),
            "m_old": sb("m_old", [P, H, QT]),
        }
        for w in ("wk_hi", "wk_lo", "wv_hi", "wv_lo"):
            S[w] = sb(w, [P, DB, D], F32R)
        cross_attention(nc, A, S)


def latent_attention(nc, A, S):
    with ExitStack() as ctx:
        def sb(name, shape):
            return ctx.enter_context(nc.sbuf_tensor(name, shape, F32))

        S = S | {
            "awq": sb("awq", [P, DB, AW]),
            "awkv": sb("awkv", [P, DB, 2 * AW]),
            "awo": sb("awo", [P, AW // P, D]),
            "abo": sb("abo", [P, D]),
            "aw_ld": [ctx.enter_context(nc.semaphore(f"aw_ld{i}")) for i in range(3)],
            "abo_ld": ctx.enter_context(nc.semaphore("abo_ld")),
        }
        for stage in (attention_output, self_attention):
            stage(nc, A, S)


def latents(nc, A, S):
    layers, E = A["rb"].shape
    with ExitStack() as ctx:
        def sb(name, shape):
            return ctx.enter_context(nc.sbuf_tensor(name, shape, F32))

        S = S | {
            "m_w": sb("m_w", [P, MOE_BUFFERS, DB, D]),
            "bias_rows": sb("bias_rows", [moe_bias_rows(E), P]),
            "bdown": sb("bdown", [E + 1, D]),
            "rw": sb("router_w", [P, layers, DB, E]),
            "rb": sb("router_b", [P, layers, E]),
            "gb": sb("gate_bias", [P, layers, E]),
            "nw": sb("norm_w", [P, layers, D]),
            "m_w_ld": [ctx.enter_context(nc.semaphore(f"m_w_ld{i}")) for i in range(MOE_BUFFERS)],
            "m_bias_ld": ctx.enter_context(nc.semaphore("m_bias_ld")),
            "m_small_ld": ctx.enter_context(nc.semaphore("m_small_ld")),
        }
        for stage in (latent_attention, moe):
            stage(nc, A, S)


_NAMES = {
    "x": "x", "ctx_1024": "ctx", "fside_Bx16xSxS2_0": "bias", "mask_BxS2_bk0": "mask",
    "L0_xattn_Wq": "xWq", "L0_xattn_bq": "xbq", "L0_xattn_Wk": "xWk", "L0_xattn_bk": "xbk",
    "L0_xattn_Wv": "xWv", "L0_xattn_bv": "xbv", "L0_xattn_Wo": "xWo", "L0_xattn_bo": "xbo",
    "L0_attn_Wq": "aWq", "L0_attn_Wkv": "aWkv", "L0_attn_Wo": "aWo", "L0_attn_bo": "abo",
    "L0_ffn_router_W": "rW", "L0_ffn_router_b": "rb", "L0_ffn_gate_bias": "gb",
    "L0_ffn_exp_Wup": "eWup", "L0_ffn_exp_bup": "ebup", "L0_ffn_exp_Wg": "eWg", "L0_ffn_exp_bg": "ebg",
    "L0_ffn_exp_Wdown": "eWdown", "L0_ffn_exp_bdown": "ebdown",
    "L0_ffn_share_Wup": "sWup", "L0_ffn_share_bup": "sbup", "L0_ffn_share_Wg": "sWg",
    "L0_ffn_share_bg": "sbg", "L0_ffn_share_Wdown": "sWdown", "L0_ffn_share_bdown": "sbdown",
    "L0_ffn_norm_w": "nw",
}
_BATCHED = ("x", "ctx", "bias", "mask")


def kernel(**inputs):
    import numpy as _np
    import concourse.bacc as _bacc
    from concourse import mybir as _mybir
    from concourse.bass_utils import run_bass_kernel_spmd as _run

    nc = _bacc.Bacc("TRN2", target_bir_lowering=False, num_devices=1)
    arrays, A = {}, {}
    for name, short in _NAMES.items():
        a = _np.ascontiguousarray(inputs[name])
        if short in _BATCHED:
            a = a.reshape(a.shape[1:])
        arrays[f"in_{short}_dram"] = a
        A[short] = nc.dram_tensor(f"in_{short}_dram", a.shape, _mybir.dt.from_np(a.dtype),
                                  kind="ExternalInput").ap()
    A["out"] = nc.dram_tensor("out_0_dram", A["x"].shape, _mybir.dt.float32, kind="ExternalOutput").ap()
    program(nc, A, (context_attention, latents, store))
    r = _run(nc, [arrays], core_ids=[0])
    got = r.results[0]["out_0_dram"]
    return got.reshape((1,) + got.shape)
```
